# Optimizing a Trainium2 kernel written in Bass

```python
import numpy as np
import jax
import jax.numpy as jnp

def _softmax(x, axis=-1):
    return jax.nn.softmax(x, axis=axis)

def _gelu(x):
    return jax.nn.gelu(x, approximate=True)

def _silu(x):
    return jax.nn.silu(x)

def _sigmoid(x):
    return jax.nn.sigmoid(x)

def _layernorm(x, axis=-1, eps=1e-05):
    m = jnp.mean(x, axis=axis, keepdims=True)
    v = jnp.var(x, axis=axis, keepdims=True)
    return (x - m) / jnp.sqrt(v + eps)

def _scatter_add(tgt, idx, src, axis=0):
    return tgt.at[idx].add(src)

def _segment_sum(src, seg, n):
    return jax.ops.segment_sum(src, seg, n)
kernel_name = 'mk_adj_seq_d4_adj_r2_650bc8'

def setup_inputs(seed: int=0):
    np.random.seed(seed)
    _w = jnp.asarray

    def _rec_inputs():
        import jax
        import jax.numpy as jnp
        _gk = jax.random.key(seed)
        x = 0.0003765 + 1 * jax.random.normal(jax.random.fold_in(_gk, 1), (16, 512, 256), jnp.float32)
        _w = (1.0 + jnp.arange(512, dtype=jnp.float32)) ** (-0.5)
        _w = _w / _w.mean()
        _pij = jnp.clip(0.03125 * _w[:, None] * _w[None, :], 0.0, 1.0)
        _a = jax.random.uniform(jax.random.fold_in(_gk, 2), (16, 512, 512)) < _pij
        adj = _a.astype(jnp.int32)
        return (x, adj)
    x, adj = _rec_inputs()

    def _L0_gnn_setup():
        import jax, jax.numpy as jnp
        import numpy as np
        B, N, H, D = (8, 512, 256, 4)
        EPS = 1e-08
        LN_EPS = 1e-05

        def _linear(x, W, b):
            return x @ W.T + b
        key = jax.random.key(seed)
        ks = jax.random.split(key, 20)
        inp = {'adj': jax.random.randint(ks[0], (B, N, N), 0, D + 1, dtype=jnp.int32), 'relative_pos': jax.random.randint(ks[1], (B, N, N), 0, 16, dtype=jnp.int32), 'hid': jax.random.normal(ks[2], (B, N, H), dtype=jnp.float32), 'Wd': jax.random.normal(ks[3], (H, D * H), dtype=jnp.float32) * (1.0 / np.sqrt(D * H)), 'bd': jnp.zeros((H,), jnp.float32)}
        s = 1.0 / np.sqrt(H)
        for i, nm in enumerate(['ri', 'rh', 'zi', 'zh', 'ni', 'nh']):
            inp['W' + nm] = jax.random.normal(ks[4 + i], (H, H), dtype=jnp.float32) * s
            inp['b' + nm] = jnp.zeros((H,), jnp.float32)
        inp['gamma'] = jnp.ones((H,), jnp.float32)
        inp['beta'] = jnp.zeros((H,), jnp.float32)
        return inp
    _L0_gnn_all = _L0_gnn_setup()
    _L0_gnn_in = {k: v for k, v in _L0_gnn_all.items() if k in ('Wd', 'bd', 'Wri', 'bri', 'Wrh', 'brh', 'Wzi', 'bzi', 'Wzh', 'bzh', 'Wni', 'bni', 'Wnh', 'bnh', 'gamma', 'beta')}
    del _L0_gnn_all

    def _L1_gnn_setup():
        import jax, jax.numpy as jnp
        import numpy as np
        B, N, E, FF, L = (8, 1024, 256, 128, 2)
        LN_EPS = 1e-05
        SCALE = float(np.sqrt(FF))

        def layer_norm(x, g, b):
            m = jnp.mean(x, axis=-1, keepdims=True)
            v = jnp.mean(jnp.square(x - m), axis=-1, keepdims=True)
            return (x - m) * jax.lax.rsqrt(v + LN_EPS) * g + b
        key = jax.random.key(seed)
        ks = jax.random.split(key, 9)
        s = 0.02
        node_fts = jax.random.normal(ks[0], (B, N, E), jnp.float32)
        rel_edges = jax.random.randint(ks[1], (B, N, N), 0, 2, jnp.int32)
        Wq = jax.random.normal(ks[2], (L, FF, E), jnp.float32) * s
        bq = jnp.zeros((L, FF), jnp.float32)
        Wk = jax.random.normal(ks[3], (L, FF, E), jnp.float32) * s
        bk = jnp.zeros((L, FF), jnp.float32)
        Wc = jax.random.normal(ks[4], (L, E, E), jnp.float32) * s
        ln_g = jnp.ones((L, E), jnp.float32)
        ln_b = jnp.zeros((L, E), jnp.float32)
        return {'node_fts': node_fts, 'rel_edges': rel_edges, 'Wq': Wq, 'bq': bq, 'Wk': Wk, 'bk': bk, 'Wc': Wc, 'ln_g': ln_g, 'ln_b': ln_b}
    _L1_gnn_all = _L1_gnn_setup()
    _L1_gnn_in = {k: v for k, v in _L1_gnn_all.items() if k in ('Wq', 'bq', 'Wk', 'bk', 'Wc', 'ln_g', 'ln_b')}
    del _L1_gnn_all

    def _L2_gnn_setup():
        import jax, jax.numpy as jnp
        import numpy as np
        import math
        D = 256
        B, L = (8, 1024)
        EPS = 1e-05

        def layer_norm(y, gamma, beta):
            mu = jnp.mean(y, axis=-1, keepdims=True)
            var = jnp.mean(jnp.square(y - mu), axis=-1, keepdims=True)
            return (y - mu) * jax.lax.rsqrt(var + EPS) * gamma + beta
        key = jax.random.key(seed)
        ks = jax.random.split(key, 8)
        s = 1.0 / math.sqrt(D)
        x = jax.random.normal(ks[0], (B, L, D), dtype=jnp.float32)
        adj = jax.random.randint(ks[1], (B, L, L), 0, 2, dtype=jnp.int32)
        Wq = jax.random.normal(ks[2], (D, D), dtype=jnp.float32) * s
        Wk = jax.random.normal(ks[3], (D, D), dtype=jnp.float32) * s
        Wv = jax.random.normal(ks[4], (D, D), dtype=jnp.float32) * s
        Wo = jax.random.normal(ks[5], (D, D), dtype=jnp.float32) * s
        bo = jnp.zeros((D,), dtype=jnp.float32)
        gamma = jnp.ones((D,), dtype=jnp.float32)
        beta = jnp.zeros((D,), dtype=jnp.float32)
        return {'x': x, 'adj': adj, 'Wq': Wq, 'Wk': Wk, 'Wv': Wv, 'Wo': Wo, 'bo': bo, 'gamma': gamma, 'beta': beta}
    _L2_gnn_all = _L2_gnn_setup()
    _L2_gnn_in = {k: v for k, v in _L2_gnn_all.items() if k in ('Wq', 'Wk', 'Wv', 'Wo', 'bo', 'gamma', 'beta')}
    del _L2_gnn_all

    def _L3_gnn_setup():
        import jax, jax.numpy as jnp
        import numpy as np
        B, N, D, H = (4, 1024, 256, 8)
        HD = D // H
        EPS = 1e-05
        key = jax.random.key(seed)
        ks = jax.random.split(key, 12)
        x = jax.random.normal(ks[0], (B, N, D), dtype=jnp.float32)
        adj = jax.random.randint(ks[1], (B, N, N), 0, 2, dtype=jnp.int32)
        adj = jnp.maximum(adj, jnp.eye(N, dtype=jnp.int32)[None, :, :])
        s = 1.0 / np.sqrt(D)
        Wq = jax.random.uniform(ks[2], (D, D), jnp.float32, -s, s)
        bq = jnp.zeros((D,), jnp.float32)
        Wk = jax.random.uniform(ks[3], (D, D), jnp.float32, -s, s)
        bk = jnp.zeros((D,), jnp.float32)
        Wv = jax.random.uniform(ks[4], (D, D), jnp.float32, -s, s)
        bv = jnp.zeros((D,), jnp.float32)
        Wo = jax.random.uniform(ks[5], (D, D), jnp.float32, -s, s)
        bo = jnp.zeros((D,), jnp.float32)
        gamma = jnp.ones((D,), jnp.float32)
        beta = jnp.zeros((D,), jnp.float32)
        return {'x': x, 'adj': adj, 'Wq': Wq, 'bq': bq, 'Wk': Wk, 'bk': bk, 'Wv': Wv, 'bv': bv, 'Wo': Wo, 'bo': bo, 'gamma': gamma, 'beta': beta}
    _L3_gnn_all = _L3_gnn_setup()
    _L3_gnn_in = {k: v for k, v in _L3_gnn_all.items() if k in ('Wq', 'bq', 'Wk', 'bk', 'Wv', 'bv', 'Wo', 'bo', 'gamma', 'beta')}
    del _L3_gnn_all
    return {'x': x, 'adj': adj, 'L0_gnn_Wd': _L0_gnn_in['Wd'], 'L0_gnn_bd': _L0_gnn_in['bd'], 'L0_gnn_Wri': _L0_gnn_in['Wri'], 'L0_gnn_bri': _L0_gnn_in['bri'], 'L0_gnn_Wrh': _L0_gnn_in['Wrh'], 'L0_gnn_brh': _L0_gnn_in['brh'], 'L0_gnn_Wzi': _L0_gnn_in['Wzi'], 'L0_gnn_bzi': _L0_gnn_in['bzi'], 'L0_gnn_Wzh': _L0_gnn_in['Wzh'], 'L0_gnn_bzh': _L0_gnn_in['bzh'], 'L0_gnn_Wni': _L0_gnn_in['Wni'], 'L0_gnn_bni': _L0_gnn_in['bni'], 'L0_gnn_Wnh': _L0_gnn_in['Wnh'], 'L0_gnn_bnh': _L0_gnn_in['bnh'], 'L0_gnn_gamma': _L0_gnn_in['gamma'], 'L0_gnn_beta': _L0_gnn_in['beta'], 'L1_gnn_Wq': _L1_gnn_in['Wq'], 'L1_gnn_bq': _L1_gnn_in['bq'], 'L1_gnn_Wk': _L1_gnn_in['Wk'], 'L1_gnn_bk': _L1_gnn_in['bk'], 'L1_gnn_Wc': _L1_gnn_in['Wc'], 'L1_gnn_ln_g': _L1_gnn_in['ln_g'], 'L1_gnn_ln_b': _L1_gnn_in['ln_b'], 'L2_gnn_Wq': _L2_gnn_in['Wq'], 'L2_gnn_Wk': _L2_gnn_in['Wk'], 'L2_gnn_Wv': _L2_gnn_in['Wv'], 'L2_gnn_Wo': _L2_gnn_in['Wo'], 'L2_gnn_bo': _L2_gnn_in['bo'], 'L2_gnn_gamma': _L2_gnn_in['gamma'], 'L2_gnn_beta': _L2_gnn_in['beta'], 'L3_gnn_Wq': _L3_gnn_in['Wq'], 'L3_gnn_bq': _L3_gnn_in['bq'], 'L3_gnn_Wk': _L3_gnn_in['Wk'], 'L3_gnn_bk': _L3_gnn_in['bk'], 'L3_gnn_Wv': _L3_gnn_in['Wv'], 'L3_gnn_bv': _L3_gnn_in['bv'], 'L3_gnn_Wo': _L3_gnn_in['Wo'], 'L3_gnn_bo': _L3_gnn_in['bo'], 'L3_gnn_gamma': _L3_gnn_in['gamma'], 'L3_gnn_beta': _L3_gnn_in['beta']}

def reference(x, adj, L0_gnn_Wd, L0_gnn_bd, L0_gnn_Wri, L0_gnn_bri, L0_gnn_Wrh, L0_gnn_brh, L0_gnn_Wzi, L0_gnn_bzi, L0_gnn_Wzh, L0_gnn_bzh, L0_gnn_Wni, L0_gnn_bni, L0_gnn_Wnh, L0_gnn_bnh, L0_gnn_gamma, L0_gnn_beta, L1_gnn_Wq, L1_gnn_bq, L1_gnn_Wk, L1_gnn_bk, L1_gnn_Wc, L1_gnn_ln_g, L1_gnn_ln_b, L2_gnn_Wq, L2_gnn_Wk, L2_gnn_Wv, L2_gnn_Wo, L2_gnn_bo, L2_gnn_gamma, L2_gnn_beta, L3_gnn_Wq, L3_gnn_bq, L3_gnn_Wk, L3_gnn_bk, L3_gnn_Wv, L3_gnn_bv, L3_gnn_Wo, L3_gnn_bo, L3_gnn_gamma, L3_gnn_beta):
    import jax
    import jax.numpy as jnp

    def _L0_gnn_ref(adj, relative_pos, hid, Wd, bd, Wri, bri, Wrh, brh, Wzi, bzi, Wzh, bzh, Wni, bni, Wnh, bnh, gamma, beta):
        import jax, jax.numpy as jnp
        import numpy as np
        B, N, H, D = (8, 512, 256, 4)
        EPS = 1e-08
        LN_EPS = 1e-05

        def _linear(x, W, b):
            return x @ W.T + b
        dt = hid.dtype
        labels = jnp.arange(1, D + 1, dtype=adj.dtype)
        mask = (adj[None] == labels[:, None, None, None]).astype(dt)
        weight = mask / (jnp.sum(mask, axis=-1, keepdims=True) + EPS)
        agg = jnp.einsum('dbmn,bnh->bmdh', weight, hid).reshape(hid.shape[0], hid.shape[1], D * H)
        out = jax.nn.relu(_linear(agg, Wd, bd))
        r = jax.nn.sigmoid(_linear(out, Wri, bri) + _linear(hid, Wrh, brh))
        z = jax.nn.sigmoid(_linear(out, Wzi, bzi) + _linear(hid, Wzh, bzh))
        n = jnp.tanh(_linear(out, Wni, bni) + r * _linear(hid, Wnh, bnh))
        out = (1.0 - z) * n + z * hid
        mu = jnp.mean(out, axis=-1, keepdims=True)
        var = jnp.var(out, axis=-1, keepdims=True)
        return (out - mu) / jnp.sqrt(var + LN_EPS) * gamma + beta

    def _L1_gnn_ref(node_fts, rel_edges, Wq, bq, Wk, bk, Wc, ln_g, ln_b):
        import jax, jax.numpy as jnp
        import numpy as np
        B, N, E, FF, L = (8, 1024, 256, 128, 2)
        LN_EPS = 1e-05
        SCALE = float(np.sqrt(FF))

        def layer_norm(x, g, b):
            m = jnp.mean(x, axis=-1, keepdims=True)
            v = jnp.mean(jnp.square(x - m), axis=-1, keepdims=True)
            return (x - m) * jax.lax.rsqrt(v + LN_EPS) * g + b
        x = node_fts
        mask = rel_edges == 0
        for k in range(L):
            q = jnp.einsum('bnd,fd->bnf', x, Wq[k]) + bq[k]
            kk = jnp.einsum('bnd,fd->bnf', x, Wk[k]) + bk[k]
            scores = jnp.einsum('bof,bif->boi', q, kk) / SCALE
            scores = jnp.where(mask, -10000000000.0, scores)
            attn = jax.nn.softmax(scores, axis=2)
            attn = jnp.where(mask, 0.0, attn)
            ctx = jnp.einsum('boi,bid->bod', attn, x)
            ctx = jnp.einsum('bnd,ed->bne', ctx, Wc[k])
            x = layer_norm(x + ctx, ln_g[k], ln_b[k])
        return x

    def _L2_gnn_ref(x, adj, Wq, Wk, Wv, Wo, bo, gamma, beta):
        import jax, jax.numpy as jnp
        import numpy as np
        import math
        D = 256
        B, L = (8, 1024)
        EPS = 1e-05

        def layer_norm(y, gamma, beta):
            mu = jnp.mean(y, axis=-1, keepdims=True)
            var = jnp.mean(jnp.square(y - mu), axis=-1, keepdims=True)
            return (y - mu) * jax.lax.rsqrt(var + EPS) * gamma + beta
        d_out = Wq.shape[1]
        scale = 1.0 / math.sqrt(d_out)
        Q = x @ Wq
        K = x @ Wk
        V = x @ Wv
        sc = jnp.einsum('bld,bmd->blm', Q, K) * scale
        mask = adj == 0
        sc = jnp.where(mask, -jnp.inf, sc)
        all_inf = jnp.all(mask, axis=-1, keepdims=True)
        sc = jnp.where(all_inf, 0.0, sc)
        w = jax.nn.softmax(sc, axis=-1)
        out = jnp.einsum('blm,bmd->bld', w, V)
        y = x + out @ Wo + bo
        return layer_norm(y, gamma, beta)

    def _L3_gnn_ref(x, adj, Wq, bq, Wk, bk, Wv, bv, Wo, bo, gamma, beta):
        import jax, jax.numpy as jnp
        import numpy as np
        B, N, D, H = (4, 1024, 256, 8)
        HD = D // H
        EPS = 1e-05
        b, n, d = x.shape
        scale = 1.0 / np.sqrt(HD).astype(np.float32)
        q = (x @ Wq + bq).reshape(b, n, H, HD)
        k = (x @ Wk + bk).reshape(b, n, H, HD)
        v = (x @ Wv + bv).reshape(b, n, H, HD)
        scores = jnp.einsum('bnhd,bmhd->bhnm', q, k) * scale
        mask = (adj == 0)[:, None, :, :]
        scores = jnp.where(mask, jnp.float32(-jnp.inf), scores)
        attn = jax.nn.softmax(scores, axis=-1)
        h = jnp.einsum('bhnm,bmhd->bnhd', attn, v).reshape(b, n, d)
        h = h @ Wo + bo
        y = h + x
        mu = jnp.mean(y, axis=-1, keepdims=True)
        var = jnp.mean(jnp.square(y - mu), axis=-1, keepdims=True)
        return (y - mu) * jax.lax.rsqrt(var + EPS) * gamma + beta
    x = _L0_gnn_ref(adj, adj, x, L0_gnn_Wd, L0_gnn_bd, L0_gnn_Wri, L0_gnn_bri, L0_gnn_Wrh, L0_gnn_brh, L0_gnn_Wzi, L0_gnn_bzi, L0_gnn_Wzh, L0_gnn_bzh, L0_gnn_Wni, L0_gnn_bni, L0_gnn_Wnh, L0_gnn_bnh, L0_gnn_gamma, L0_gnn_beta)
    x = _L1_gnn_ref(x, adj, L1_gnn_Wq, L1_gnn_bq, L1_gnn_Wk, L1_gnn_bk, L1_gnn_Wc, L1_gnn_ln_g, L1_gnn_ln_b)
    x = _L2_gnn_ref(x, adj, L2_gnn_Wq, L2_gnn_Wk, L2_gnn_Wv, L2_gnn_Wo, L2_gnn_bo, L2_gnn_gamma, L2_gnn_beta)
    x = _L3_gnn_ref(x, adj, L3_gnn_Wq, L3_gnn_bq, L3_gnn_Wk, L3_gnn_bk, L3_gnn_Wv, L3_gnn_bv, L3_gnn_Wo, L3_gnn_bo, L3_gnn_gamma, L3_gnn_beta)
    return x

_drawn_inputs = setup_inputs


def setup_inputs(seed=0):
    import zlib

    import numpy as np

    out = dict(_drawn_inputs(seed))
    spreads = {'L0_gnn_bd': (0.0, 0.1),
     'L0_gnn_bri': (0.0, 0.603),
     'L0_gnn_brh': (0.0, 0.606),
     'L0_gnn_bzi': (0.0, 0.1),
     'L0_gnn_bzh': (0.0, 0.1),
     'L0_gnn_bni': (0.0, 0.1),
     'L0_gnn_bnh': (0.0, 0.1),
     'L0_gnn_gamma': (1.0, 0.2),
     'L0_gnn_beta': (0.0, 0.1),
     'L1_gnn_bq': (0.0, 0.8),
     'L1_gnn_bk': (0.0, 0.8),
     'L1_gnn_ln_g': (1.0, 0.2),
     'L1_gnn_ln_b': (0.0, 0.1),
     'L2_gnn_bo': (0.0, 0.1),
     'L2_gnn_gamma': (1.0, 0.2),
     'L2_gnn_beta': (0.0, 0.1),
     'L3_gnn_bq': (0.0, 0.8),
     'L3_gnn_bk': (0.0, 0.8),
     'L3_gnn_bv': (0.0, 0.1),
     'L3_gnn_bo': (0.0, 0.1),
     'L3_gnn_gamma': (1.0, 0.2),
     'L3_gnn_beta': (0.0, 0.1)}
    factors = {'L0_gnn_Wri': 3.413, 'L1_gnn_Wq': 3.947, 'L1_gnn_Wk': 3.711}
    for name, (base, spread) in spreads.items():
        noise = np.random.default_rng([zlib.crc32(name.encode()), seed]).standard_normal(out[name].shape)
        drawn = base * np.exp(spread * noise) if base else spread * noise
        out[name] = jnp.asarray(drawn.astype(out[name].dtype))
    for name, factor in factors.items():
        out[name] = (out[name] * factor).astype(out[name].dtype)
    return out
```

```python
from contextlib import ExitStack

import concourse.bass as bass
from concourse import mybir

F32 = mybir.dt.float32
F32R = mybir.dt.float32r
BF16 = mybir.dt.bfloat16
I32 = mybir.dt.int32
ALU = mybir.AluOpType
ACT = mybir.ActivationFunctionType
AX_X = mybir.AxisListType.X

P = 128
B, N, D = 16, 512, 256
F1 = 128
HEADS, HD = 8, 32
LABELS = 4
NT = N // P
DT = D // P
SLOTS = 2
MASKED = -1.0e30
LOWEST = -3.0e38
CNT_EPS = 1e-8
LN_EPS = 1e-5
SCALE = {"1a": F1 ** -0.5, "1b": F1 ** -0.5, "2": D ** -0.5, "3": HD ** -0.5}

WIDTH = [("wd1", D), ("ri", D), ("rh", D), ("zi", D), ("zh", D), ("ni", D), ("nh", D),
         ("q1a", F1), ("k1a", F1), ("c1a", D), ("q1b", F1), ("k1b", F1), ("c1b", D),
         ("q3", D), ("k3", D), ("v3", D), ("o3", D)]
COL = {}
RAW = 0
for _name, _width in WIDTH:
    COL[_name] = (RAW, _width)
    RAW += DT * _width
COL["a2"] = (RAW, D)
COL["c2"] = (RAW + DT * D, D)
WCOLS = RAW + 2 * DT * D
FOLD = ["qT2", "kT2", "vT2", "o2"]
GEN = DT * D * (LABELS - 1)

BIAS = ["bd", "bri", "brh", "bzi", "bzh", "bni", "bnh", "bq1a", "bk1a", "bq1b", "bk1b", "bq3", "bk3", "bv3",
        "r", "z", "h"]
BCOL, NB_IN = {}, 0
for _name in BIAS:
    if _name == "r":
        NB_IN_LAST = NB_IN
    BCOL[_name] = NB_IN
    NB_IN += 1 if _name[:3] in ("bq1", "bk1") else DT
NBIAS = NB_IN
NB_IN = NB_IN_LAST
REP = ["g0", "b0", "g1a", "b1a", "g1b", "b1b", "bo2", "g2", "b2", "bo3", "g3", "b3"]


def attention_order(units, hold):
    tiles = [(u, it) for u in units for it in range(NT)]
    lag, out, done = 3, [], []
    for n in range(len(tiles) + lag + hold):
        if lag <= n < len(tiles) + lag:
            out.append(("T",) + tiles[n - lag])
        if n < len(tiles):
            out.append(("S",) + tiles[n])
        m = n - lag - hold
        if m >= 0 and m % NT == NT - 1:
            u = units[m // NT]
            if u[0] == "3":
                out.append(("ov", u[1], u[2]))
            else:
                out += [("pv", u[0], u[1], ip) for ip in range(2)]
                out.append(("norm", u[0], u[1]))
    return out


def make_steps():
    st = []
    for s in range(SLOTS):
        st += [("cnt", s), ("agg", s, 0), ("agg", s, 1)]
    for s in range(SLOTS):
        st += [("more", s)] + [("wd", s, et) for et in range(DT)]
    for s in range(SLOTS):
        for et in range(DT):
            st += [("hn", s, et), ("r", s, et), ("in", s, et), ("z", s, et)]
    for s in range(SLOTS):
        st += [("lt", s, ip) for ip in range(2)] + [("norm", "0", s)]
    prev = "0"
    for layer in ("1a", "1b", "2"):
        for s in range(SLOTS):
            st += [("xt", prev, s, dt) for dt in range(DT)]
            st += [("q", layer, s, c) for c in range(DT if layer == "2" else 1)]
            st += [("k", layer, s, 0)] if layer != "2" else []
            st += [("v", layer, s, jp) for jp in range(2)]
        st += attention_order([(layer, s, 0) for s in range(SLOTS)], 1)
        prev = layer
    for s in range(SLOTS):
        st += [("xt", prev, s, dt) for dt in range(DT)]
    for s in range(SLOTS):
        for dt in range(DT):
            st += [("q", "3", s, dt), ("k", "3", s, dt)]
        st += [("v", "3", s, jp) for jp in range(2)]
        st += attention_order([("3", s, h) for h in range(HEADS)], 2)
        st += [("ht", s, it) for it in range(NT)]
        st += [("hx", s, dt) for dt in range(DT)]
        st += [("y", s, ip) for ip in range(2)] + [("norm", "3", s)]
    return st


STEPS = make_steps()
SPLIT = ("agg", "wd", "xt", "q", "k", "v", "hx")
GROUPS = [k for k in STEPS if k[0] not in ("S", "T", "norm", "more")]
GBANKS = 4


class Signal:

    def __init__(self, sem, keys):
        self.sem = sem
        self.where = {k: n + 1 for n, k in enumerate(keys)}
        assert len(self.where) == len(keys)

    def at(self, key):
        return self.where[key]


def terms3(lh, ll, rh, rl):
    return [(lh, rl), (ll, rh), (lh, rh)]


def build(nc, x, xT, adj, adjT, wraw, wfold, wgen, bcols, rep, out):
    ctx = ExitStack()
    with ctx:
        at = [nc.sbuf_base + 63 & ~63]

        def sb(name, shape, dt, where=None):
            size = mybir.dt.size(dt)
            for n in shape[1:]:
                size *= n
            if where is None:
                where = at[0]
                at[0] += (size + 63) & ~63
            return nc.alloc_sbuf_tensor_at(name, shape, dt, offset=where), where

        def new(name, shape, dt):
            return sb(name, shape, dt)[0]

        wh = new("weights_high", [P, WCOLS], F32R)
        wl = new("weights_low", [P, WCOLS], F32R)
        wg = new("weights_labels", [P, GEN], F32)
        rp = new("rows_replicated", [P, len(REP) * D], F32)
        bc = new("bias_columns", [P, NBIAS], F32)
        ident = new("identity", [P, P], F32)
        ones = new("ones", [P, P], F32R)
        ones_b = new("ones_bf16", [P, P], BF16)

        RING = 4
        probs, probs_at = sb("probs", [P, RING, N], F32)
        above = [sb(f"label_above_1_{s}", [P, NT, N], BF16, probs_at + s * 2 * 4 * N)[0] for s in range(SLOTS)]
        more = sb("more_messages", [P, DT, N], F32, probs_at)[0]

        mbias, labT, xi, vh, vl, xTh, xTl, qh, ql, pth, ptl = ([] for _ in range(11))
        xh, xl, outh, outl, xTf, tA, tB, tC, mask, rc, flt = ([] for _ in range(11))
        q3h, q3l, k3h, k3l, ovs, hn_i, hlo, hTh, hTl = ([] for _ in range(9))
        q_at = []
        for s in range(SLOTS):
            t, bias_at = sb(f"mask_bias{s}", [P, NT, N], BF16)
            mbias.append(t)
            t, lab_at = sb(f"labels_T{s}", [P, NT, N], BF16)
            labT.append(t)
            t, xi_at = sb(f"x_nodes{s}", [P, NT, D], F32)
            xi.append(t)
            t, v_at = sb(f"v_high{s}", [P, NT, D], F32R)
            vh.append(t)
            t, vl_at = sb(f"v_low{s}", [P, NT, D], F32R)
            vl.append(t)
            t, xt_at = sb(f"xT_high{s}", [P, DT, N], F32R)
            xTh.append(t)
            xTl.append(sb(f"xT_low{s}", [P, DT, N], F32R)[0])
            t, qa = sb(f"q_high{s}", [P, DT, N], F32R)
            qh.append(t)
            ql.append(sb(f"q_low{s}", [P, DT, N], F32R)[0])
            q_at.append(qa)
            t, pt_at = sb(f"probsT_high{s}", [P, NT, N], F32R)
            pth.append(t)
            ptl.append(sb(f"probsT_low{s}", [P, NT, N], F32R)[0])
            kb = 1024
            xh.append(sb(f"x_high{s}", [P, NT, D], F32R, v_at)[0])
            xl.append(sb(f"x_low{s}", [P, NT, D], F32R, vl_at)[0])
            outh.append(sb(f"msg_high{s}", [P, DT, N], F32R, qa)[0])
            outl.append(sb(f"msg_low{s}", [P, DT, N], F32R, qa + 4 * kb)[0])
            flt.append(sb(f"unsplit{s}", [P, DT, N], F32, xi_at)[0])
            xTf.append(sb(f"x_features{s}", [P, DT, N], F32, pt_at)[0])
            tA.append(sb(f"gate_r{s}", [P, DT, N], F32, pt_at + 4 * kb)[0])
            tB.append(sb(f"cand{s}", [P, DT, N], F32, pt_at + 8 * kb)[0])
            tC.append(sb(f"gate_z{s}", [P, DT, N], F32, pt_at + 12 * kb)[0])
            mask.append(sb(f"label_mask{s}", [P, NT, N], F32R, pt_at + 4 * kb)[0])
            rc.append(sb(f"one_over_count{s}", [P, N], F32, pt_at + 12 * kb)[0])
            ovs.append(sb(f"heads_T{s}", [P, HEADS // 2, N], F32, xt_at)[0])
            hn_i.append(sb(f"heads_nodes{s}", [P, NT, D], F32, lab_at)[0])
            hlo.append(sb(f"heads_low{s}", [P, NT, D], F32, bias_at)[0])
            hTh.append(sb(f"headsT_high{s}", [P, DT, N], F32R, v_at)[0])
            hTl.append(sb(f"headsT_low{s}", [P, DT, N], F32R, vl_at)[0])
        for s in range(SLOTS):
            q3h.append(sb(f"q3_high{s}", [P, DT, N], F32R, q_at[0])[0])
            q3l.append(sb(f"q3_low{s}", [P, DT, N], F32R, q_at[0] + 4 * kb)[0])
            k3h.append(sb(f"k3_high{s}", [P, DT, N], F32R, q_at[1])[0])
            k3l.append(sb(f"k3_low{s}", [P, DT, N], F32R, q_at[1] + 4 * kb)[0])

        rmax = new("row_max", [P, SLOTS * HEADS * NT], F32)
        nmax = new("row_shift", [P, SLOTS * HEADS * NT], F32)
        rsum = new("row_sum", [P, SLOTS, HEADS, NT], F32)
        rinv = new("row_inverse", [P, SLOTS, HEADS, NT], F32)
        flag = new("row_has_edge", [P, SLOTS, NT], F32)
        stats = new("ln_stats", [P, SLOTS, NT, 6], F32)
        mv = new("ln_mean_var", [P, SLOTS, NT, 2], F32)
        var = new("ln_var", [P, SLOTS, NT], F32)
        rstd = new("ln_rstd", [P, SLOTS, NT], F32)
        nt_ = new("ln_newton", [P, SLOTS, NT], F32)
        n_above = new("n_above", [1, SLOTS], F32)
        take_more = new("take_more", [1, SLOTS], I32)
        assert at[0] <= nc.sbuf_usable_end, at[0]
        raw = sb("weights_raw", [P, RAW], F32, (q_at[0] - 28 * kb))[0]
        fold_at = q_at[0] - 28 * kb + RAW * 4
        foldr = sb("fold_raw", [P, 4, DT, D], F32, fold_at)[0]
        foldh = sb("fold_high", [P, 4, DT, D], F32R, fold_at + 8 * kb)[0]
        foldl = sb("fold_low", [P, 4, DT, D], F32R, fold_at + 16 * kb)[0]

        psS = ctx.enter_context(nc.psum_tensor("scores_bank", [P, 2, 512], F32))
        psT = ctx.enter_context(nc.psum_tensor("transposed_bank", [P, 2, 512], F32))
        psG = ctx.enter_context(nc.psum_tensor("group_bank", [P, GBANKS, 512], F32))

        def W(name, kt, lo=0, hi=None):
            off, width = COL[name]
            hi = width if hi is None else hi
            a, b = off + kt * width + lo, off + kt * width + hi
            return wh[:, a:b], wl[:, a:b]

        def bias(name, c=0):
            return bc[:, BCOL[name] + c:BCOL[name] + c + 1]

        def row(name):
            n = REP.index(name)
            return rp[:, n * D:(n + 1) * D]

        def f32(ap):
            return ap.bitcast(F32)

        def sem(name):
            return ctx.enter_context(nc.semaphore(name))

        w_in, f_in, c_in, id0, id1 = sem("w_in"), sem("f_in"), sem("c_in"), sem("id0"), sem("id1")
        w_hi, w_lo, f_hi, f_lo, fold_mm, fold_hi, fold_lo, b_done = (sem(n) for n in (
            "w_hi", "w_lo", "f_hi", "f_lo", "fold_mm", "fold_hi", "fold_lo", "b_done"))
        CH = 1024
        chunks = [(a, min(a + CH, RAW)) for a in range(0, RAW, CH)]
        with nc.Block() as block:
            @block.sync
            def _(sp):
                sp.dma_start(foldr[:].rearrange("p a b c -> p (a b c)"), wfold).then_inc(f_in, 16)
                sp.dma_start(raw[:], wraw).then_inc(w_in, 16)
                sp.dma_start(wg[:], wgen).then_inc(c_in, 16)
                sp.dma_start(rp[:], rep).then_inc(c_in, 16)
                sp.dma_start(bc[:, 0:NB_IN], bcols).then_inc(c_in, 16)
                sp.wait_ge(c_in, 48)

            @block.gpsimd
            def _(pool):
                nc.gpsimd.memset(ident[:], 0.0).then_inc(id0, 1)
                pool.wait_ge(id0, 1)
                nc.gpsimd.affine_select(out=ident[:], in_=ident[:], compare_op=ALU.not_equal, fill=1.0, base=0,
                                        pattern=[[-1, P]], channel_multiplier=1).then_inc(id0, 1)
                nc.gpsimd.memset(f32(ones[:]), 1.0).then_inc(id1, 1)
                nc.gpsimd.memset(ones_b[:], 1.0).then_inc(id1, 1)

            @block.scalar
            def _(act):
                act.wait_ge(f_in, 16)
                nc.scalar.copy(foldh[:], foldr[:]).then_inc(f_hi, 1)
                act.wait_ge(w_in, 16)
                for a, b in chunks:
                    nc.scalar.copy(wh[:, a:b], raw[:, a:b]).then_inc(w_hi, 1)
                for g in range(4):
                    act.wait_ge(fold_mm, g + 1)
                    a = RAW + g * D
                    nc.scalar.copy(wh[:, a:a + D], psG[:, g, 0:D]).then_inc(fold_hi, 1)

            @block.vector
            def _(dve):
                dve.wait_ge(f_hi, 1)
                nc.vector.tensor_sub(foldl[:], foldr[:], f32(foldh[:])).then_inc(f_lo, 1)
                for n, (a, b) in enumerate(chunks):
                    dve.wait_ge(w_hi, n + 1)
                    nc.vector.tensor_sub(wl[:, a:b], raw[:, a:b], f32(wh[:, a:b])).then_inc(w_lo, 1)
                for g in range(4):
                    dve.wait_ge(fold_hi, g + 1)
                    a = RAW + g * D
                    nc.vector.tensor_sub(wl[:, a:a + D], psG[:, g, 0:D], f32(wh[:, a:a + D])).then_inc(fold_lo, 1)
                dve.wait_ge(c_in, 48)
                n = 0
                for to, parts in (("r", ("bri", "brh")), ("z", ("bzi", "bzh"))):
                    c, a, b = BCOL[to], BCOL[parts[0]], BCOL[parts[1]]
                    nc.vector.tensor_add(bc[:, c:c + DT], bc[:, a:a + DT], bc[:, b:b + DT]).then_inc(b_done, 1)
                    n += 1
                    dve.wait_ge(b_done, n)
                    nc.vector.tensor_scalar_mul(bc[:, c:c + DT], bc[:, c:c + DT], 0.5).then_inc(b_done, 1)
                    n += 1
                c, a = BCOL["h"], BCOL["bnh"]
                nc.vector.tensor_scalar_mul(bc[:, c:c + DT], bc[:, a:a + DT], 0.5).then_inc(b_done, 1)

            @block.tensor
            def _(pe):
                pe.wait_ge(f_lo, 1)
                for g in range(4):
                    left, right = (0, 1) if g < 2 else (2, 3)
                    c = slice((g % 2) * P, (g % 2) * P + P)
                    terms = []
                    for kt in range(DT):
                        terms += terms3(foldh[:, left, kt, c], foldl[:, left, kt, c],
                                        foldh[:, right, kt, :], foldl[:, right, kt, :])
                    for n, (a, b) in enumerate(terms):
                        mm = nc.tensor.matmul(psG[:, g, 0:D], a, b, start=(n == 0), stop=(n == len(terms) - 1))
                    mm.then_inc(fold_mm, 1)

        first = [0]

        def signal(name, keys):
            return Signal(sem(name), list(keys))

        slots = [(s,) for s in range(SLOTS)]
        split = [k for k in GROUPS if k[0] in SPLIT]
        adj_in = [sem(f"adj_in{s}") for s in range(SLOTS)]
        lab_in = [sem(f"lab_in{s}") for s in range(SLOTS)]
        x_in = [sem(f"x_in{s}") for s in range(SLOTS)]
        xT_in = [sem(f"xT_in{s}") for s in range(SLOTS)]
        g_ready = signal("g_ready", GROUPS)
        g_free = [sem(f"g_free{b}") for b in range(GBANKS)]
        hi = signal("hi", split)
        lo = signal("lo", [k for k in split if k[0] not in ("agg", "wd")])
        lo_pool = signal("lo_pool", [k for k in split if k[0] in ("agg", "wd")])
        full = signal("full", [k for k in split if k[0] == "agg"])
        relu = signal("relu", [k for k in split if k[0] == "wd"])
        x_hi = signal("x_hi", [(s, w) for s in range(SLOTS) for w in ("x", "xT")])
        x_lo = signal("x_lo", [(s, w) for s in range(SLOTS) for w in ("x", "xT")])
        labelled = signal("labelled", range(SLOTS))
        biased = signal("biased", range(SLOTS))
        rcs = signal("rcs", range(SLOTS))
        gru = [k for k in GROUPS if k[0] in ("hn", "r", "in", "z")]
        act_gru = signal("act_gru", [k + (w,) for k in gru for w in (("t",) if k[0] != "in" else ("n",))])
        dve_gru = signal("dve_gru", [k + (w,) for k in gru if k[0] in ("in", "z") for w in
                                     (("v", "w") if k[0] == "in" else ("e", "o"))])
        pool_d = signal("pool_d", [k for k in gru if k[0] == "z"])
        tiles_S = [k for k in STEPS if k[0] == "S"]
        tiles_T = [k for k in STEPS if k[0] == "T"]
        s_ready = signal("s_ready", tiles_S)
        s_taken = signal("s_taken", tiles_S)
        shifted = signal("shifted", tiles_S)
        p_ready = signal("p_ready", tiles_S)
        t_ready = signal("t_ready", tiles_T)
        pt_hi = signal("pt_hi", tiles_T)
        pt_lo = signal("pt_lo", tiles_T)
        normed = signal("normed", [k for k in STEPS if k[0] == "norm"])
        y_done = signal("y_done", [k for k in GROUPS if k[0] in ("pv", "y")])
        ov_out = signal("ov_out", [k for k in GROUPS if k[0] == "ov"])
        h_lo = signal("h_lo", [k for k in GROUPS if k[0] == "ht"])
        h_done = signal("h_done", [k for k in GROUPS if k[0] == "ht"])
        bo_in = signal("bo_in", [("2", s) for s in range(SLOTS)] + [("3", s) for s in range(SLOTS)])
        adj_here = sem("adj_here")
        compared = signal("compared", range(SLOTS))
        counted = signal("counted", range(SLOTS))
        told = signal("told", range(SLOTS))
        more_mask = [sem(f"more_mask{s}") for s in range(SLOTS)]
        more_sum = [sem(f"more_sum{s}") for s in range(SLOTS)]
        more_full = [sem(f"more_full{s}") for s in range(SLOTS)]
        more_used = [sem(f"more_used{s}") for s in range(SLOTS)]
        chain = sem("dve_chain")
        stored = sem("stored")
        sem_first, sem_last = x_in[0].num, stored.num

        def gbank(k):
            n = GROUPS.index(k)
            return psG[:, n % GBANKS, :]

        def free(ins, k):
            return ins.then_inc(g_free[GROUPS.index(k) % GBANKS], 1)

        def parts(k):
            kind = k[0]
            if kind == "agg":
                return qh[k[1]][:, k[2], :], ql[k[1]][:, k[2], :]
            if kind == "wd":
                return outh[k[1]][:, k[2], :], outl[k[1]][:, k[2], :]
            if kind == "xt":
                return xTh[k[2]][:, k[3], :], xTl[k[2]][:, k[3], :]
            if kind == "hx":
                return hTh[k[1]][:, k[2], :], hTl[k[1]][:, k[2], :]
            _, layer, s, c = k
            if kind == "q":
                return (q3h[s][:, c, :], q3l[s][:, c, :]) if layer == "3" else (qh[s][:, c, :], ql[s][:, c, :])
            if kind == "k":
                return (k3h[s][:, c, :], k3l[s][:, c, :]) if layer == "3" else (qh[s][:, 1, :], ql[s][:, 1, :])
            if layer == "3":
                return v3(s, c, 0), v3(s, c, 1)
            return vh[s][:, 2 * c:2 * c + 2, :], vl[s][:, 2 * c:2 * c + 2, :]

        v3t = [sb(f"v3_{s}", [P, NT, HEADS, 2, HD], F32R, w)[0] for s, w in
               ((0, q_at[0] - 16 * kb), (1, q_at[1] - 16 * kb))]

        def v3(s, jp, part):
            return v3t[s][:, 2 * jp:2 * jp + 2, :, part, :]

        def view(k, ap):
            if k[0] == "v":
                if k[1] == "3":
                    return ap.rearrange("p (j h d) -> p j h d", j=2, h=HEADS)
                return ap.rearrange("p (j d) -> p j d", j=2)
            return ap

        split_bias = {("q", "1a"): "bq1a", ("q", "1b"): "bq1b", ("k", "1a"): "bk1a", ("k", "1b"): "bk1b",
                      ("q", "3"): "bq3", ("k", "3"): "bk3"}

        def column(k):
            if k[0] == "hx":
                return bias("bv3", k[2])
            if k[0] in ("q", "k") and (k[0], k[1]) in split_bias:
                return bias(split_bias[k[0], k[1]], k[3])
            return None

        def hlo_view(s, it):
            return hlo[s][:, it, :].rearrange("p (h d) -> p h d", d=HD)

        def tile_at(k):
            return tiles_S.index(("S",) + k[1:])

        def shift_col(k):
            u, it = k[1], k[2]
            return (u[1] * HEADS + u[2]) * NT + it

        def pt_buf(u):
            return u[2] % 2 if u[0] == "3" else u[1]

        with nc.Fori(0, B // SLOTS) as i:
            with nc.Block() as block:
                @block.sync
                def _(sp):
                    for s in range(SLOTS):
                        b = i * SLOTS + s
                        sp.dma_start(xi[s][:], x[b].rearrange("(t p) d -> p t d", p=P)).then_inc(x_in[s], 16)
                        sp.dma_start(xTf[s][:], xT[b].rearrange("(t p) n -> p t n", p=P)).then_inc(xT_in[s], 16)
                    for s in range(SLOTS):
                        b = i * SLOTS + s
                        sp.wait_ge(normed.sem, normed.at(("norm", "3", s)))
                        sp.dma_start(out[b].rearrange("(t p) d -> p t d", p=P), xi[s][:]).then_inc(stored, 16)
                    sp.wait_ge(stored, 16 * SLOTS)

                @block.gpsimd
                def _(pool):
                    for s in range(SLOTS):
                        b = i * SLOTS + s
                        nc.gpsimd.dma_start(labT[s][:], adjT[b].rearrange("(t p) n -> p t n", p=P)).then_inc(lab_in[s], 16)
                    for s in range(SLOTS):
                        b = i * SLOTS + s
                        nc.gpsimd.dma_start(mbias[s][:], adj[b].rearrange("(t p) n -> p t n", p=P)).then_inc(adj_in[s], 16)
                    for s in range(SLOTS):
                        pool.wait_ge(x_hi.sem, x_hi.at((s, "x")))
                        nc.gpsimd.tensor_sub(xl[s][:], xi[s][:], f32(xh[s][:])).then_inc(x_lo.sem, 1)
                        pool.wait_ge(x_hi.sem, x_hi.at((s, "xT")))
                        nc.gpsimd.tensor_sub(xTl[s][:], xTf[s][:], f32(xTh[s][:])).then_inc(x_lo.sem, 1)
                    for s in range(SLOTS):
                        pool.wait_ge(adj_in[s], i * 16 + 16)
                        pool.sem_inc(adj_here, 1)
                        pool.wait_ge(adj_here, s + 1)
                        nc.gpsimd.tensor_scalar(mbias[s][:], mbias[s][:], 0.0, MASKED, ALU.is_equal, ALU.mult)\
                            .then_inc(biased.sem, 1)
                    for k in STEPS:
                        if k[0] in ("agg", "wd"):
                            src = flt[k[1]][:, k[2], :]
                            h, l = parts(k)
                            pool.wait_ge(hi.sem, hi.at(k))
                            nc.gpsimd.tensor_sub(l, src, f32(h)).then_inc(lo_pool.sem, 1)
                        elif k[0] == "z":
                            _, s, et = k
                            pool.wait_ge(act_gru.sem, act_gru.at(("in", s, et, "n")))
                            nc.gpsimd.tensor_sub(tA[s][:, et, :], xTf[s][:, et, :], tB[s][:, et, :]).then_inc(pool_d.sem, 1)
                        elif k[0] == "xt" and k[1] in ("1b", "2") and k[3] == DT - 1:
                            layer = "2" if k[1] == "1b" else "3"
                            s = k[2]
                            pool.wait_ge(g_ready.sem, g_ready.at(k))
                            r = row("bo" + layer)
                            for it in range(NT):
                                a = nc.gpsimd.tensor_add(xi[s][:, it, :], xi[s][:, it, :], r)
                            a.then_inc(bo_in.sem, 1)

                @block.scalar
                def _(act):
                    for s in range(SLOTS):
                        act.wait_ge(x_in[s], 16)
                        nc.scalar.copy(xh[s][:], xi[s][:]).then_inc(x_hi.sem, 1)
                        act.wait_ge(xT_in[s], 16)
                        nc.scalar.copy(xTh[s][:], xTf[s][:]).then_inc(x_hi.sem, 1)
                    for k in STEPS:
                        kind = k[0]
                        if kind == "agg":
                            act.wait_ge(full.sem, full.at(k))
                            nc.scalar.copy(parts(k)[0], flt[k[1]][:, k[2], :]).then_inc(hi.sem, 1)
                        elif kind == "wd":
                            _, s, et = k
                            act.wait_ge(g_ready.sem, g_ready.at(k))
                            if et == 0:
                                act.wait_ge(lo_pool.sem, lo_pool.at(("agg", s, DT - 1)))
                            f = nc.scalar.activation(flt[s][:, et, :], gbank(k), ACT.Relu, bias=bias("bd", et))
                            free(f, k)
                            act.wait_ge(g_free[GROUPS.index(k) % GBANKS], freed(k))
                            act.wait_ge(g_ready.sem, g_ready.at(("wd", s, DT - 1)))
                            nc.scalar.copy(parts(k)[0], flt[s][:, et, :]).then_inc(hi.sem, 1)
                        elif kind in ("hn", "r", "z"):
                            _, s, et = k
                            act.wait_ge(g_ready.sem, g_ready.at(k))
                            to, fn, b = {"hn": (tB, ACT.Identity, "h"), "r": (tA, ACT.Tanh, "r"), "z": (tC, ACT.Tanh, "z")}[kind]
                            a = nc.scalar.activation(to[s][:, et, :], gbank(k), fn, bias=bias(b, et), scale=0.5)
                            a.then_inc(act_gru.sem, 1)
                        elif kind == "in":
                            _, s, et = k
                            act.wait_ge(dve_gru.sem, dve_gru.at(k + ("w",)))
                            nc.scalar.activation(tB[s][:, et, :], tB[s][:, et, :], ACT.Tanh, bias=bias("bni", et))\
                                .then_inc(act_gru.sem, 1)
                        elif kind in ("xt", "q", "k", "v", "hx"):
                            act.wait_ge(g_ready.sem, g_ready.at(k))
                            h = parts(k)[0]
                            b = column(k)
                            if b is None:
                                a = nc.scalar.copy(h, view(k, gbank(k)))
                            else:
                                a = nc.scalar.activation(h, gbank(k), ACT.Identity, bias=b)
                            a.then_inc(hi.sem, 1)
                        elif kind == "S":
                            _, u, it = k
                            ring = probs[:, tile_at(k) % RING, :]
                            c = shift_col(k)
                            act.wait_ge(shifted.sem, shifted.at(k))
                            nc.scalar.activation(ring, ring, ACT.Exp, bias=nmax[:, c:c + 1], scale=SCALE[u[0]],
                                                 accum_out=rsum[:, u[1], u[2], it:it + 1]).then_inc(p_ready.sem, 1)
                        elif kind == "T":
                            _, u, it = k
                            act.wait_ge(t_ready.sem, t_ready.at(k))
                            n = tiles_T.index(k)
                            nc.scalar.copy(pth[pt_buf(u)][:, :, it * P:(it + 1) * P],
                                           psT[:, n % 2, :].rearrange("p (j i) -> p j i", j=NT)).then_inc(pt_hi.sem, 1)
                        elif kind == "ov":
                            _, s, h = k
                            a, b = (h % 2) * 64, (h % 2) * 64 + 64
                            act.wait_ge(g_ready.sem, g_ready.at(k))
                            free(nc.scalar.copy(ovs[s][a:b, h // 2, :], gbank(k)[a:b, :]), k)
                        elif kind == "ht":
                            _, s, it = k
                            act.wait_ge(g_ready.sem, g_ready.at(k))
                            lowp = gbank(k).rearrange("p (h w d) -> p h w d", w=2, d=HD)[:, :, 1, :]
                            nc.scalar.copy(hlo_view(s, it), lowp).then_inc(h_lo.sem, 1)

                @block.vector
                def _(dve):
                    links = [0]

                    def link(ins):
                        links[0] += 1
                        ins.then_inc(chain, 1)
                        dve.wait_ge(chain, links[0])

                    def layer_norm(layer, s, src):
                        for it in range(NT):
                            st = nc.vector.bn_stats(stats[:, s, it, :], src(it))
                        link(st)
                        for it in range(NT):
                            st = nc.vector.bn_aggr(mv[:, s, it, :], stats[:, s, it, :])
                        link(st)
                        v, y, t = var[:, s, :], rstd[:, s, :], nt_[:, s, :]
                        link(nc.vector.tensor_scalar_add(v, mv[:, s, :, 1], LN_EPS))
                        link(nc.vector.tensor_single_scalar(t.bitcast(I32), v.bitcast(I32), 1, ALU.logical_shift_right))
                        link(nc.vector.tensor_scalar(y.bitcast(I32), t.bitcast(I32), -1.0, float(0x5F3759DF), ALU.mult, ALU.add))
                        for _ in range(3):
                            link(nc.vector.tensor_mul(t, y, y))
                            link(nc.vector.scalar_tensor_tensor(out=t, in0=t, scalar=-0.5, in1=v, op0=ALU.mult, op1=ALU.mult))
                            link(nc.vector.scalar_tensor_tensor(out=y, in0=t, scalar=1.5, in1=y, op0=ALU.add, op1=ALU.mult))
                        for it in range(NT):
                            a = nc.vector.scalar_tensor_tensor(out=xi[s][:, it, :], in0=src(it), scalar=mv[:, s, it, 0:1],
                                                               in1=row("g" + layer), op0=ALU.subtract, op1=ALU.mult)
                            if layer == "0" and it % 2 == 1:
                                free(a, ("lt", s, it // 2))
                        links[0] += 1
                        if layer == "0":
                            nc.vector.tensor_copy(t, y).then_inc(chain, 1)
                            dve.wait_ge(chain, links[0])
                        else:
                            a.then_inc(chain, 1)
                            dve.wait_ge(chain, links[0])
                        for it in range(NT):
                            a = nc.vector.scalar_tensor_tensor(out=xi[s][:, it, :], in0=xi[s][:, it, :], scalar=y[:, it:it + 1],
                                                               in1=row("b" + layer), op0=ALU.mult, op1=ALU.add)
                        a.then_inc(normed.sem, 1)

                    for s in range(SLOTS):
                        dve.wait_ge(lab_in[s], i * 16 + 16)
                        nc.vector.tensor_scalar(mask[s][:], labT[s][:], 1.0, None, ALU.is_equal).then_inc(labelled.sem, 1)
                    for s in range(SLOTS):
                        nc.vector.tensor_scalar(above[s][:], labT[s][:], 2.0, None, ALU.is_ge).then_inc(compared.sem, 1)
                    for s in range(SLOTS):
                        dve.wait_ge(counted.sem, counted.at(s))
                        link(nc.vector.tensor_reduce(n_above[:, s:s + 1], psS[0:1, s, :], AX_X, ALU.max))
                        nc.vector.tensor_copy(take_more[:, s:s + 1], n_above[:, s:s + 1]).then_inc(told.sem, 1)

                    def more_labels(s):
                        for n in range(LABELS - 1):
                            m_mask, m_sum, m_full, m_used = more_mask[s], more_sum[s], more_full[s], more_used[s]
                            nc.vector.tensor_scalar(mask[s][:], labT[s][:], float(n + 2), None, ALU.is_equal)\
                                .then_inc(m_mask, 1)
                            dve.wait_ge(m_sum, 3 * n + 3)
                            nc.vector.tensor_scalar_add(rc[s][:], psS[:, 0, :], CNT_EPS).then_inc(m_full, 1)
                            dve.wait_ge(m_full, 4 * n + 1)
                            nc.vector.reciprocal(rc[s][:], rc[s][:]).then_inc(m_full, 1)
                            dve.wait_ge(m_full, 4 * n + 2)
                            for ht, bank in enumerate((psS[:, 1, :], psT[:, 0, :])):
                                nc.vector.tensor_mul(more[:, ht, :], bank, rc[s][:]).then_inc(m_full, 1)
                            dve.wait_ge(m_used, n + 1)

                    for k in STEPS:
                        kind = k[0]
                        if kind == "more":
                            s = k[1]
                            dve.wait_ge(told.sem, told.at(s))
                            with dve.If(dve.value_load(take_more[0:1, s:s + 1]) > 0):
                                more_labels(s)
                        elif kind == "cnt":
                            s = k[1]
                            dve.wait_ge(g_ready.sem, g_ready.at(k))
                            a = nc.vector.tensor_scalar_add(rc[s][:], gbank(k), CNT_EPS)
                            free(a, k)
                            dve.wait_ge(g_free[GROUPS.index(k) % GBANKS], freed(k))
                            nc.vector.reciprocal(rc[s][:], rc[s][:]).then_inc(rcs.sem, 1)
                            dve.wait_ge(rcs.sem, rcs.at(s))
                            dve.wait_ge(x_lo.sem, x_lo.at((s, "x")))
                        elif kind == "agg":
                            _, s, ht = k
                            dve.wait_ge(g_ready.sem, g_ready.at(k))
                            a = nc.vector.tensor_mul(flt[s][:, ht, :], gbank(k), rc[s][:])
                            a.then_inc(full.sem, 1)
                        elif kind == "in":
                            _, s, et = k
                            dve.wait_ge(act_gru.sem, act_gru.at(("r", s, et, "t")))
                            b = tB[s][:, et, :]
                            nc.vector.scalar_tensor_tensor(out=b, in0=tA[s][:, et, :], scalar=1.0, in1=b,
                                                           op0=ALU.add, op1=ALU.mult).then_inc(dve_gru.sem, 1)
                            dve.wait_ge(dve_gru.sem, dve_gru.at(k + ("v",)))
                            dve.wait_ge(g_ready.sem, g_ready.at(k))
                            nc.vector.tensor_add(b, b, gbank(k)).then_inc(dve_gru.sem, 1)
                        elif kind == "z":
                            _, s, et = k
                            a = tA[s][:, et, :]
                            dve.wait_ge(pool_d.sem, pool_d.at(k))
                            dve.wait_ge(act_gru.sem, act_gru.at(k + ("t",)))
                            nc.vector.scalar_tensor_tensor(out=a, in0=tC[s][:, et, :], scalar=1.0, in1=a,
                                                           op0=ALU.add, op1=ALU.mult).then_inc(dve_gru.sem, 1)
                            dve.wait_ge(dve_gru.sem, dve_gru.at(k + ("e",)))
                            nc.vector.scalar_tensor_tensor(out=a, in0=a, scalar=0.5, in1=tB[s][:, et, :],
                                                           op0=ALU.mult, op1=ALU.add).then_inc(dve_gru.sem, 1)
                        elif kind == "norm" and k[1] == "0":
                            s = k[2]
                            dve.wait_ge(lo_pool.sem, lo_pool.at(("wd", s, DT - 1)))
                            dve.wait_ge(g_ready.sem, g_ready.at(("lt", s, 1)))
                            layer_norm("0", s, lambda it: gbank(("lt", s, it // 2))[:, (it % 2) * D:(it % 2 + 1) * D])
                        elif kind == "norm":
                            _, layer, s = k
                            layer_norm(layer[0] if layer in ("2", "3") else layer, s, lambda it: xi[s][:, it, :])
                        elif kind in ("xt", "q", "k", "v", "hx"):
                            h, l = parts(k)
                            b = column(k)
                            dve.wait_ge(hi.sem, hi.at(k))
                            src = view(k, gbank(k))
                            if b is None:
                                a = nc.vector.tensor_sub(l, src, f32(h))
                            else:
                                a = nc.vector.scalar_tensor_tensor(out=l, in0=src, scalar=b, in1=f32(h),
                                                                   op0=ALU.add, op1=ALU.subtract)
                            a.then_inc(lo.sem, 1)
                        elif kind == "S":
                            _, u, it = k
                            n = tile_at(k)
                            c = shift_col(k)
                            dve.wait_ge(s_ready.sem, s_ready.at(k))
                            if u[0] == "1a" and it == 0:
                                dve.wait_ge(biased.sem, biased.at(u[1]))
                            if n >= RING:
                                dve.wait_ge(t_ready.sem, n - RING + 1)
                            nc.vector.tensor_tensor_reduce(out=probs[:, n % RING, :], in0=psS[:, n % 2, :],
                                                           in1=mbias[u[1]][:, it, :], scale=1.0, scalar=LOWEST,
                                                           op0=ALU.add, op1=ALU.max, accum_out=rmax[:, c:c + 1])\
                                .then_inc(s_taken.sem, 1)
                            dve.wait_ge(s_taken.sem, s_taken.at(k))
                            nc.vector.tensor_scalar_mul(nmax[:, c:c + 1], rmax[:, c:c + 1], -SCALE[u[0]])\
                                .then_inc(shifted.sem, 1)
                        elif kind == "T":
                            _, u, it = k
                            n = tiles_T.index(k)
                            o = slice(it * P, (it + 1) * P)
                            dve.wait_ge(pt_hi.sem, pt_hi.at(k))
                            nc.vector.tensor_sub(ptl[pt_buf(u)][:, :, o], psT[:, n % 2, :].rearrange("p (j i) -> p j i", j=NT),
                                                 f32(pth[pt_buf(u)][:, :, o])).then_inc(pt_lo.sem, 1)
                        elif kind == "pv":
                            _, layer, s, ip = k
                            if ip == 0:
                                c = s * HEADS * NT
                                if layer == "1a":
                                    link(nc.vector.tensor_scalar(flag[:, s, :], rmax[:, c:c + NT], MASKED / 2, None, ALU.is_ge))
                                link(nc.vector.reciprocal(rinv[:, s, 0, :], rsum[:, s, 0, :]))
                                if layer in ("1a", "1b"):
                                    link(nc.vector.tensor_mul(rinv[:, s, 0, :], rinv[:, s, 0, :], flag[:, s, :]))
                                else:
                                    dve.wait_ge(bo_in.sem, bo_in.at(("2", s)))
                            dve.wait_ge(g_ready.sem, g_ready.at(k))
                            for j in range(2):
                                it = 2 * ip + j
                                a = nc.vector.scalar_tensor_tensor(out=xi[s][:, it, :], in0=gbank(k)[:, j * D:(j + 1) * D],
                                                                   scalar=rinv[:, s, 0, it:it + 1], in1=xi[s][:, it, :],
                                                                   op0=ALU.mult, op1=ALU.add)
                            a.then_inc(y_done.sem, 1)
                            dve.wait_ge(y_done.sem, y_done.at(k))
                        elif kind == "ht":
                            _, s, it = k
                            if it == 0:
                                link(nc.vector.reciprocal(rinv[:, s, :, :], rsum[:, s, :, :]))
                                link(nc.vector.reciprocal(nt_[:, s, :], flag[:, s, :]))
                                link(nc.vector.tensor_mul(nt_[:, s, :], nt_[:, s, :], flag[:, s, :]))
                                for h in range(HEADS):
                                    a = nc.vector.tensor_mul(rinv[:, s, h, :], rinv[:, s, h, :], nt_[:, s, :])
                                link(a)
                            dve.wait_ge(h_lo.sem, h_lo.at(k))
                            highp = gbank(k).rearrange("p (h w d) -> p h w d", w=2, d=HD)[:, :, 0, :]
                            o = hn_i[s][:, it, :].rearrange("p (h d) -> p h d", d=HD)
                            link(nc.vector.tensor_add(o, highp, hlo_view(s, it)))
                            r = rinv[:, s, :, it:it + 1].to_broadcast([P, HEADS, HD])
                            nc.vector.tensor_mul(o, o, r).then_inc(h_done.sem, 1)
                        elif kind == "y":
                            _, s, ip = k
                            if ip == 0:
                                dve.wait_ge(bo_in.sem, bo_in.at(("3", s)))
                            dve.wait_ge(g_ready.sem, g_ready.at(k))
                            to = xi[s][:, 2 * ip:2 * ip + 2, :]
                            nc.vector.tensor_add(to, gbank(k).rearrange("p (j d) -> p j d", j=2), to).then_inc(y_done.sem, 1)
                            dve.wait_ge(y_done.sem, y_done.at(k))

                @block.tensor
                def _(pe):
                    def claim(k):
                        n = GROUPS.index(k)
                        if n < GBANKS:
                            return
                        p = GROUPS[n - GBANKS]
                        if p[0] in ("cnt", "wd", "lt", "ov"):
                            pe.wait_ge(g_free[n % GBANKS], freed(p))
                        elif p[0] == "agg":
                            pe.wait_ge(full.sem, full.at(p))
                        elif p[0] in ("hn", "r", "z"):
                            pe.wait_ge(act_gru.sem, act_gru.at(p + ("t",)))
                        elif p[0] == "in":
                            pe.wait_ge(dve_gru.sem, dve_gru.at(p + ("w",)))
                        elif p[0] in ("pv", "y"):
                            pe.wait_ge(y_done.sem, y_done.at(p))
                        elif p[0] == "ht":
                            pe.wait_ge(h_done.sem, h_done.at(p))
                        else:
                            pe.wait_ge(lo.sem, lo.at(p))

                    def run(ps, terms):
                        for n, (a, b) in enumerate(terms):
                            mm = nc.tensor.matmul(ps, a, b, start=(n == 0), stop=(n == len(terms) - 1))
                        return mm

                    def turn(ps, srcs):
                        for n, src in enumerate(srcs):
                            mm = nc.tensor.transpose(ps[:, n * P:(n + 1) * P], src, ident[:])
                        return mm

                    def features(name, s, c, xhT, xlT):
                        t = []
                        for kt in range(DT):
                            w = W(name, kt, c * P, (c + 1) * P)
                            t += terms3(w[0], w[1], xhT[s][:, kt, :], xlT[s][:, kt, :])
                        return t

                    def more_labels(s):
                        for n in range(LABELS - 1):
                            pe.wait_ge(more_mask[s], n + 1)
                            run(psS[:, 0, :], [(ones[:], mask[s][:, nt, :]) for nt in range(NT)]).then_inc(more_sum[s], 1)
                            for ht, bank in enumerate((psS[:, 1, :], psT[:, 0, :])):
                                run(bank, neighbours(s, ht)).then_inc(more_sum[s], 1)
                            pe.wait_ge(more_full[s], 4 * n + 4)
                            for et in range(DT):
                                for kt in range(DT):
                                    c = (n * DT + kt) * D + et * P
                                    mm = nc.tensor.matmul(gbank(("wd", s, et)), wg[:, c:c + P], more[:, kt, :],
                                                          start=False, stop=False, skip_group_check=True)
                            mm.then_inc(more_used[s], 1)

                    def neighbours(s, ht):
                        c = slice(ht * P, (ht + 1) * P)
                        return [(w[s][:, nt, c], mask[s][:, nt, :]) for nt in range(NT) for w in (xl, xh)]

                    for s in range(SLOTS):
                        pe.wait_ge(compared.sem, compared.at(s))
                        run(psS[:, s, :], [(ones_b[:], above[s][:, nt, :]) for nt in range(NT)]).then_inc(counted.sem, 1)
                    for k in STEPS:
                        kind = k[0]
                        if kind not in ("S", "T", "norm", "more"):
                            claim(k)
                            ps = gbank(k)
                        if kind == "cnt":
                            s = k[1]
                            pe.wait_ge(labelled.sem, labelled.at(s))
                            mm = run(ps, [(ones[:], mask[s][:, nt, :]) for nt in range(NT)])
                        elif kind == "agg":
                            _, s, ht = k
                            pe.wait_ge(x_lo.sem, x_lo.at((s, "x")))
                            mm = run(ps, neighbours(s, ht))
                        elif kind == "wd":
                            _, s, et = k
                            if et == 0:
                                pe.wait_ge(lo_pool.sem, lo_pool.at(("agg", s, DT - 1)))
                            t = features("wd1", s, et, qh, ql)
                            for n, (a, b) in enumerate(t[:-1]):
                                nc.tensor.matmul(ps, a, b, start=(n == 0), stop=False)
                            if et == DT - 1:
                                pe.wait_ge(told.sem, told.at(s))
                                with pe.If(pe.value_load(take_more[0:1, s:s + 1]) > 0):
                                    more_labels(s)
                                for e in range(DT):
                                    a, b = features("wd1", s, e, qh, ql)[-1]
                                    nc.tensor.matmul(gbank(("wd", s, e)), a, b, start=False, stop=True)\
                                        .then_inc(g_ready.sem, 1)
                        elif kind in ("hn", "r", "in", "z"):
                            _, s, et = k
                            if kind == "hn" and et == 0:
                                pe.wait_ge(x_lo.sem, x_lo.at((s, "xT")))
                            t = []
                            if kind != "in":
                                t += features({"hn": "nh", "r": "rh", "z": "zh"}[kind], s, et, xTh, xTl)
                            if kind != "hn":
                                pe.wait_ge(lo_pool.sem, lo_pool.at(("wd", s, DT - 1)))
                                t += features({"in": "ni", "r": "ri", "z": "zi"}[kind], s, et, outh, outl)
                            mm = run(ps, t)
                        elif kind == "lt":
                            _, s, ip = k
                            pe.wait_ge(dve_gru.sem, dve_gru.at(("z", s, DT - 1, "o")))
                            mm = turn(ps, [tA[s][:, dt, (2 * ip + j) * P:(2 * ip + j + 1) * P] for j in range(2) for dt in range(DT)])
                        elif kind == "xt":
                            _, layer, s, dt = k
                            pe.wait_ge(normed.sem, normed.at(("norm", layer, s)))
                            mm = turn(ps, [xi[s][:, it, dt * P:(dt + 1) * P] for it in range(NT)])
                        elif kind in ("q", "k"):
                            _, layer, s, c = k
                            pe.wait_ge(lo.sem, lo.at(("xt", {"1a": "0", "1b": "1a", "2": "1b", "3": "2"}[layer], s, DT - 1)))
                            name = "a2" if layer == "2" else kind + layer
                            mm = run(ps, features(name, s, c, xTh, xTl))
                        elif kind == "v":
                            _, layer, s, jp = k
                            name = "v3" if layer == "3" else "c" + layer
                            for j in range(2):
                                jt = slice((2 * jp + j) * P, (2 * jp + j + 1) * P)
                                t = []
                                for kt in range(DT):
                                    w = W(name, kt)
                                    t += terms3(xTh[s][:, kt, jt], xTl[s][:, kt, jt], w[0], w[1])
                                mm = run(ps[:, j * D:(j + 1) * D], t)
                        elif kind == "S":
                            _, u, it = k
                            layer, s, h = u
                            n = tiles_S.index(k)
                            i_ = slice(it * P, (it + 1) * P)
                            if n >= 2:
                                pe.wait_ge(s_taken.sem, n - 1)
                            if layer == "3":
                                if it == 0:
                                    pe.wait_ge(lo.sem, lo.at(("k", "3", s, h // 4)))
                                r = slice(HD * (h % 4), HD * (h % 4) + HD)
                                c = h // 4
                                t = terms3(q3h[s][r, c, i_], q3l[s][r, c, i_], k3h[s][r, c, :], k3l[s][r, c, :])
                            elif layer == "2":
                                if it == 0:
                                    pe.wait_ge(lo.sem, lo.at(("q", "2", s, DT - 1)))
                                t = []
                                for c in range(DT):
                                    t += terms3(qh[s][:, c, i_], ql[s][:, c, i_], xTh[s][:, c, :], xTl[s][:, c, :])
                            else:
                                if it == 0:
                                    pe.wait_ge(lo.sem, lo.at(("k", layer, s, 0)))
                                t = terms3(qh[s][:, 0, i_], ql[s][:, 0, i_], qh[s][:, 1, :], ql[s][:, 1, :])
                            run(psS[:, n % 2, :], t).then_inc(s_ready.sem, 1)
                        elif kind == "T":
                            _, u, it = k
                            n = tiles_T.index(k)
                            pe.wait_ge(p_ready.sem, p_ready.at(("S", u, it)))
                            if n >= 2:
                                pe.wait_ge(pt_lo.sem, n - 1)
                            turn(psT[:, n % 2, :], [probs[:, n % RING, jt * P:(jt + 1) * P] for jt in range(NT)])\
                                .then_inc(t_ready.sem, 1)
                        elif kind == "pv":
                            _, layer, s, ip = k
                            if ip == 0:
                                pe.wait_ge(lo.sem, lo.at(("v", layer, s, 1)))
                                pe.wait_ge(pt_lo.sem, pt_lo.at(("T", (layer, s, 0), NT - 1)))
                            for j in range(2):
                                i_ = slice((2 * ip + j) * P, (2 * ip + j + 1) * P)
                                t = []
                                for jt in range(NT):
                                    t += terms3(pth[s][:, jt, i_], ptl[s][:, jt, i_], vh[s][:, jt, :], vl[s][:, jt, :])
                                mm = run(ps[:, j * D:(j + 1) * D], t)
                        elif kind == "ov":
                            _, s, h = k
                            pe.wait_ge(lo.sem, lo.at(("v", "3", s, 1)))
                            pe.wait_ge(pt_lo.sem, pt_lo.at(("T", ("3", s, h), NT - 1)))
                            t = []
                            for jt in range(NT):
                                v = v3t[s][:, jt, h // 2 * 2:h // 2 * 2 + 2, :, :].rearrange("p h w d -> p (h w d)")
                                t += [(v, ptl[h % 2][:, jt, :]), (v, pth[h % 2][:, jt, :])]
                            mm = run(ps, t)
                        elif kind == "ht":
                            _, s, it = k
                            if it == 0:
                                pe.wait_ge(g_free[GROUPS.index(("ov", s, HEADS - 1)) % GBANKS], freed(("ov", s, HEADS - 1)))
                            mm = turn(ps, [ovs[s][:, p, it * P:(it + 1) * P] for p in range(HEADS // 2)])
                        elif kind == "hx":
                            _, s, dt = k
                            pe.wait_ge(h_done.sem, h_done.at(("ht", s, NT - 1)))
                            mm = turn(ps, [hn_i[s][:, it, dt * P:(dt + 1) * P] for it in range(NT)])
                        elif kind == "y":
                            _, s, ip = k
                            pe.wait_ge(lo.sem, lo.at(("hx", s, DT - 1)))
                            for j in range(2):
                                i_ = slice((2 * ip + j) * P, (2 * ip + j + 1) * P)
                                t = []
                                for kt in range(DT):
                                    w = W("o3", kt)
                                    t += terms3(hTh[s][:, kt, i_], hTl[s][:, kt, i_], w[0], w[1])
                                mm = run(ps[:, j * D:(j + 1) * D], t)
                        if kind not in ("S", "T", "norm", "more", "wd"):
                            mm.then_inc(g_ready.sem, 1)

            nc.gpsimd.sem_clear(range(sem_first, sem_last + 1))
            nc.all_engine_barrier()


def freed(p):
    n = GROUPS.index(p)
    return sum(1 for g in range(n % GBANKS, n + 1, GBANKS) if GROUPS[g][0] in ("cnt", "wd", "lt", "ov"))


def kernel(**inputs):
    import numpy as np
    import concourse.bacc as bacc
    from concourse.bass_utils import run_bass_kernel_spmd as run

    a = {k: np.asarray(v) for k, v in inputs.items()}

    def ktiles(m):
        return m.reshape(-1, P, m.shape[1]).transpose(1, 0, 2).reshape(P, -1)

    wd = a["L0_gnn_Wd"]
    g0, g1, g2, g3 = "L0_gnn_", "L1_gnn_", "L2_gnn_", "L3_gnn_"
    mats = [wd[:, 0:D].T] + [a[g0 + "W" + n].T for n in ("ri", "rh", "zi", "zh", "ni", "nh")]
    for l in range(2):
        mats += [a[g1 + "Wq"][l].T, a[g1 + "Wk"][l].T, a[g1 + "Wc"][l].T]
    mats += [a[g3 + "W" + n] for n in "qkvo"]
    wraw = np.concatenate([ktiles(m) for m in mats], axis=1)
    wfold = np.concatenate([ktiles(m) for m in (a[g2 + "Wq"].T, a[g2 + "Wk"].T, a[g2 + "Wv"].T, a[g2 + "Wo"])], axis=1)
    wgen = np.concatenate([ktiles(wd[:, d * D:(d + 1) * D].T) for d in range(1, LABELS)], axis=1)
    cols = [a[g0 + "b" + n] for n in ("d", "ri", "rh", "zi", "zh", "ni", "nh")]
    for l in range(2):
        cols += [a[g1 + "bq"][l], a[g1 + "bk"][l]]
    cols += [a[g3 + "b" + n] for n in "qkv"]
    bcols = np.concatenate([c.reshape(-1, P).T for c in cols], axis=1)
    rows = [a[g0 + "gamma"], a[g0 + "beta"]]
    for l in range(2):
        rows += [a[g1 + "ln_g"][l], a[g1 + "ln_b"][l]]
    rows += [a[g2 + "bo"], a[g2 + "gamma"], a[g2 + "beta"], a[g3 + "bo"], a[g3 + "gamma"], a[g3 + "beta"]]
    rep = np.broadcast_to(np.concatenate(rows)[None, :], (P, len(REP) * D))

    arrays = {
        "x": a["x"], "xT": a["x"].transpose(0, 2, 1), "adj": a["adj"], "adjT": a["adj"].transpose(0, 2, 1),
        "wraw": wraw, "wfold": wfold, "wgen": wgen, "bcols": bcols, "rep": rep,
    }
    arrays = {f"in_{k}": np.ascontiguousarray(v) for k, v in arrays.items()}
    nc = bacc.Bacc("TRN2", target_bir_lowering=False, num_devices=1)
    args = [nc.dram_tensor(k, v.shape, mybir.dt.from_np(v.dtype), kind="ExternalInput").ap() for k, v in arrays.items()]
    out = nc.dram_tensor("out", (B, N, D), F32, kind="ExternalOutput").ap()
    build(nc, *args, out)
    r = run(nc, [arrays], core_ids=[0])
    return r.results[0]["out"]
```

```python
from contextlib import ExitStack

import concourse.bass as bass
from concourse import mybir

F32 = mybir.dt.float32
F32R = mybir.dt.float32r
BF16 = mybir.dt.bfloat16
I32 = mybir.dt.int32
ALU = mybir.AluOpType
ACT = mybir.ActivationFunctionType
AX_X = mybir.AxisListType.X

P = 128
B, N, D = 16, 512, 256
F1 = 128
HEADS, HD = 8, 32
LABELS = 4
NT = N // P
DT = D // P
SLOTS = 2
CHAIN = 4
GBANKS, RING = 4, 4
MASKED = -1.0e30
LOWEST = -3.0e38
CNT_EPS = 1e-8
LN_EPS = 1e-5
SCALE = {"1a": F1 ** -0.5, "1b": F1 ** -0.5, "2": D ** -0.5, "3": HD ** -0.5}

WIDTH = [("wd1", D), ("ri", D), ("rh", D), ("zi", D), ("zh", D), ("ni", D), ("nh", D),
         ("q1a", F1), ("k1a", F1), ("c1a", D), ("q1b", F1), ("k1b", F1), ("c1b", D),
         ("q3", D), ("k3", D), ("v3", D), ("o3", D)]
COL = {}
RAW = 0
for _name, _width in WIDTH:
    COL[_name] = (RAW, _width)
    RAW += DT * _width
COL["a2"] = (RAW, D)
COL["c2"] = (RAW + DT * D, D)
WCOLS = RAW + 2 * DT * D
FOLD = ["qT2", "kT2", "vT2", "o2"]
GEN = DT * D * (LABELS - 1)

BIAS = ["bd", "bri", "brh", "bzi", "bzh", "bni", "bnh", "bq1a", "bk1a", "bq1b", "bk1b", "bq3", "bk3", "bv3",
        "g0", "b0", "g1a", "b1a", "g1b", "b1b", "g2", "b2", "r", "z", "h"]
BCOL, NB_IN = {}, 0
for _name in BIAS:
    if _name == "r":
        NB_IN_LAST = NB_IN
    BCOL[_name] = NB_IN
    NB_IN += 1 if _name[:3] in ("bq1", "bk1") else DT
NBIAS = NB_IN
NB_IN = NB_IN_LAST
REP = ["g0", "b0", "g1a", "b1a", "g1b", "b1b", "g2", "b2", "g3", "b3"]


LAYERS = ("1a", "1b", "2")
BEFORE = {"1a": "0", "1b": "1a", "2": "1b", "3": "2"}
MM, MM_HALF, TURN = 0.217, 0.119, 0.48

def parts_of(b):
    out = []

    def add(engine, step, us, *needs, lag=0.2):
        out.append((engine, step, us, lag, [n for n in needs if n is not None]))

    def old(engine, step):
        return (engine, step) if b >= SLOTS else None

    o = b - SLOTS
    add("SP", ("x", b), 0.1, old("SP", ("store", o)), lag=3.0)
    add("SP", ("xT", b), 0.1, old("PE", ("ov", o, HEADS - 1, 1)), lag=3.0)
    add("Pool", ("lab", b), 1.2, old("PE", ("S", ("3", o, HEADS - 2), NT - 1)), lag=4.0)
    add("Pool", ("adj", b), 1.2, old("DVE", ("S", ("3", o, HEADS - 1), NT - 1)), lag=4.0)
    add("ACT", ("x", b), 0.9, ("SP", ("x", b)))
    add("ACT", ("xT", b), 0.9, ("SP", ("xT", b)))
    add("DVE", ("x", b), 1.1, ("ACT", ("x", b)))
    add("DVE", ("label", b), 1.8, ("Pool", ("lab", b)))
    add("Pool", ("xT", b), 2.4, ("ACT", ("xT", b)))
    add("PE", ("cnt", b), 4 * MM, ("DVE", ("label", b)))
    add("PE", ("high", b), 4 * MM, ("DVE", ("label", b)))
    for ht in range(DT):
        add("PE", ("agg", b, ht), 8 * MM, ("DVE", ("x", b)))
    add("DVE", ("cnt", b), 4.1, ("PE", ("cnt", b)))
    add("DVE", ("high", b), 0.9, ("PE", ("high", b)))
    for ht in range(DT):
        add("DVE", ("agg", b, ht), 0.6, ("PE", ("agg", b, ht)))
        add("ACT", ("agg", b, ht), 0.5, ("DVE", ("agg", b, ht)))
    add("DVE", ("more", b), 1.4, ("ACT", ("agg", b, 1)))
    add("DVE", ("bias", b), 0.7, ("Pool", ("adj", b)))
    add("PE", ("more", b), 0.0, ("DVE", ("more", b)))
    add("PE", ("wd", b, 0), 5 * MM, ("DVE", ("more", b)))
    add("DVE", ("labels", b), 0.05, ("PE", ("wd", b, 0)), lag=0.0)
    add("PE", ("wd", b, 1), 7 * MM, ("DVE", ("labels", b)))
    for et in range(DT):
        add("ACT", ("wd", b, et), 1.1, ("PE", ("wd", b, 1)))
        add("DVE", ("wd", b, et), 0.6, ("ACT", ("wd", b, et)))
    add("PE", ("hn", b, 0), 6 * MM, ("Pool", ("xT", b)))
    add("PE", ("hn", b, 1), 6 * MM)
    for et in range(DT):
        add("ACT", ("hn", b, et), 0.5, ("PE", ("hn", b, et)))
    for et in range(DT):
        add("PE", ("r", b, et), 12 * MM, ("DVE", ("wd", b, 1)))
        add("PE", ("in", b, et), 6 * MM)
        add("PE", ("z", b, et), 12 * MM)
        add("ACT", ("r", b, et), 0.5, ("PE", ("r", b, et)))
        add("DVE", ("in", b, et), 1.33, ("PE", ("in", b, et)), ("ACT", ("r", b, et)))
        add("ACT", ("in", b, et), 0.5, ("DVE", ("in", b, et)))
        add("Pool", ("z", b, et), 1.3, ("ACT", ("in", b, et)))
        add("ACT", ("z", b, et), 0.5, ("PE", ("z", b, et)))
        add("DVE", ("z", b, et), 1.33, ("Pool", ("z", b, et)), ("ACT", ("z", b, et)))
    for ip in range(2):
        add("PE", ("lt", b, ip), TURN, ("DVE", ("z", b, 1)))
    add("DVE", ("norm", "0", b), 6.1, ("PE", ("lt", b, 1)))

    def transposed(layer):
        for dt in range(DT):
            add("PE", ("xt", layer, b, dt), TURN, ("DVE", ("norm", layer, b)))
        for dt in range(DT):
            add("ACT", ("xt", layer, b, dt), 1.33, ("PE", ("xt", layer, b, dt)))
            add("DVE", ("xt", layer, b, dt), 0.6, ("ACT", ("xt", layer, b, dt)))
        add("Pool", ("affine", layer, b), 4.6, ("PE", ("xt", layer, b, 1)))

    def split(*step):
        add("ACT", step, 0.55, ("PE", step))
        add("DVE", step, 0.63, ("ACT", step))

    def tiles(units, us):
        ts = [(u, it) for u in units for it in range(NT)]
        lag = 3
        for n in range(len(ts) + lag):
            if n < len(ts):
                add("PE", ("S",) + ts[n], us, ("SP", ("stack",) + ts[n][0]) if ts[n][0][0] == "3" else None,
                    ("PE", ("ht", b - 1, 3)) if b and n == NT else None)
                add("DVE", ("S",) + ts[n], 0.8, ("PE", ("S",) + ts[n]))
            if lag <= n < len(ts) + lag:
                u, it = t = ts[n - lag]
                add("PE", ("T",) + t, TURN, ("ACT", ("S",) + t),
                    ("PE", ("ov", b, u[2] - 1, it // 2)) if u[0] == "3" and u[2] else None)
                add("ACT", ("T",) + t, 0.48, ("PE", ("T",) + t),
                    ("PE", ("ov", b, u[2] - 1, it // 2)) if u[0] == "3" and u[2] else None)
                add("DVE", ("T",) + t, 0.6, ("ACT", ("T",) + t))
            if n < len(ts):
                add("ACT", ("S",) + ts[n], 0.71, ("DVE", ("S",) + ts[n]))
            m = n - lag
            if m >= 0 and m % 2 == 1 and units[0][0] == "3":
                u, half = units[m // NT], m % NT // 2
                h = u[2]
                add("PE", ("ov", b, h, half), 8 * MM_HALF, ("DVE", ("T", u, 2 * half + 1)),
                    ("PE", ("ht", b - 1, 3)) if b and h == 0 else None)
                add("ACT", ("ov", b, h, half), 0.35, ("PE", ("ov", b, h, half)),
                    ("PE", ("ht", b, h // 2 - 1)) if h > 1 else ("PE", ("ht", b - 1, 3)) if b else None)
                if half and h % 2:
                    p = h // 2
                    add("PE", ("ht", b, p), TURN, ("ACT", ("ov", b, h, 1)), ("PE", ("hx", b - 1, 1)) if b and p == 0 else None)
                    add("ACT", ("ht", b, p), 0.3, ("PE", ("ht", b, p)), ("DVE", ("ht", b, p - 1)) if p else
                        ("DVE", ("ht", b - 1, 3)) if b else None)
                    add("DVE", ("ht", b, p), 1.5, ("ACT", ("ht", b, p)),
                        ("PE", ("hx", b, 0)) if p == 2 else ("PE", ("hx", b - 1, 1)) if b and not p else None)
                    if p % 2:
                        add("PE", ("hx", b, p // 2), TURN, ("DVE", ("ht", b, p)))
                        split("hx", b, p // 2)

    for layer in LAYERS:
        transposed(BEFORE[layer])
        xt = ("DVE", ("xt", BEFORE[layer], b, 1))
        for c in range(2):
            step = ("k", layer, b, 0) if c and layer != "2" else ("q", layer, b, c)
            add("PE", step, 6 * MM, xt)
            split(*step)
        for jp in range(2):
            step = ("v", layer, b, jp)
            add("PE", step, 12 * MM_HALF, xt)
            split(*step)
        n = len(out)
        tiles([(layer, b, 0)], (6 if layer == "2" else 3) * MM)
        out[n][4].append(("DVE", ("q", "2", b, 1) if layer == "2" else ("k", layer, b, 0)))
        for ip in range(2):
            add("PE", ("pv", layer, b, ip), 24 * MM_HALF, ("DVE", ("T", (layer, b, 0), NT - 1)), ("DVE", ("v", layer, b, 1)))
            add("DVE", ("pv", layer, b, ip), 2.0, ("PE", ("pv", layer, b, ip)), ("Pool", ("affine", BEFORE[layer], b)))
        add("DVE", ("norm", layer, b), 4.1)
    transposed("2")
    xt = ("DVE", ("xt", "2", b, 1))
    order = [("q", "3", b, 0), ("q", "3", b, 1), ("v", "3", b, 0), ("v", "3", b, 1), ("k", "3", b, 0), ("k", "3", b, 1)]
    for n, step in enumerate(order):
        add("PE", step, (12 * MM_HALF if step[0] == "v" else 6 * MM), xt)
    for n, step in enumerate(order):
        add("ACT", step, 0.5, ("PE", step), ("PE", order[-1]) if step[0] == "k" else None)
        add("DVE", step, 0.63, ("ACT", step))
    for h in range(HEADS):
        user = ("S", ("3", b, h - 2), NT - 1) if h > 1 else ("S", ("3", b - 1, 7), NT - 1) if b and h else None
        add("SP", ("stack", "3", b, h), 0.5, ("DVE", ("k", "3", b, h // 4)), user and ("PE", user), lag=2.5)
    tiles([("3", b, h) for h in range(HEADS)], MM)
    for ip in range(2):
        add("PE", ("y", b, ip), 12 * MM_HALF, ("DVE", ("hx", b, 1)))
        add("DVE", ("y", b, ip), 1.5, ("PE", ("y", b, ip)), ("Pool", ("affine", "2", b)))
    add("DVE", ("norm", "3", b), 4.1)
    add("Pool", ("affine", "3", b), 4.6, ("DVE", ("norm", "3", b)))
    add("SP", ("store", b), 0.1, ("Pool", ("affine", "3", b)), lag=3.0)
    return out

def reader(step):
    kind = step[0]
    if kind == "more":
        return []
    if kind == "lt":
        return [("DVE", ("norm", "0", step[1]))]
    return [("ACT" if kind in ("wd", "xt", "hn", "r", "z", "ov") else "DVE", step)]


def opens(step):
    if step[0] == "more" or step[0] in ("wd", "lt") and step[2] == 0:
        return step[1]
    if step[0] == "k" and step[1] == "3" and step[3] == 0:
        return step[2]
    return None


def schedule():
    engines = ("PE", "ACT", "DVE", "Pool", "SP")
    parts, todo, after = {}, {}, {}
    for b in range(CHAIN):
        for part in parts_of(b):
            kind = part[1][0]
            lane = todo.setdefault((part[0], b, kind if kind in ("S", "T") else "main"), [])
            if lane:
                after.setdefault(lane[-1][:2], []).append((part[:2], 0.0))
            lane.append(part)
            parts[part[:2]] = part
    for part in parts.values():
        for need in part[4]:
            after.setdefault(need, []).append((part[:2], parts[need][3]))
    rest = {}

    def way(p):
        todo_ = [p]
        while todo_:
            q = todo_[-1]
            open_ = [n for n, _ in after.get(q, []) if n not in rest]
            if q in rest or not open_:
                rest[q] = parts[q][2] + max([lag + rest[n] for n, lag in after.get(q, [])] + [0.0])
                todo_.pop()
            else:
                todo_ += open_
        return rest[p]

    free, order, end = dict.fromkeys(engines, 0.0), {e: [] for e in engines}, {}
    at = dict.fromkeys(todo, 0)
    groups, scores, turned, taken, meeting = [], [], [], 0, None
    for _ in range(len(parts)):
        best = None
        for k, lane in todo.items():
            if at[k] == len(lane):
                continue
            e, b, _ = k
            _, step, us, lag, needs = lane[at[k]]
            needs = list(needs)
            if step[0] == "labels" and groups:
                needs += reader(groups[-GBANKS])
            if e == "PE":
                if meeting is not None and step != ("wd", meeting, 1):
                    continue
                if order[e] and groups and order[e][-1] == groups[-1] and opens(groups[-1]) not in (None, b):
                    continue
                if step[0] == "S":
                    needs += [("DVE", p) for p in scores[-2:-1]]
                elif step[0] == "T":
                    needs += [("DVE", p) for p in turned[-2:-1]]
                elif len(groups) >= GBANKS:
                    needs += reader(groups[-GBANKS])
            if e == "DVE" and step[0] == "S":
                if taken == len(scores) or scores[taken] != step:
                    continue
                if taken >= RING:
                    needs.append(("PE", ("T",) + scores[taken - RING][1:]))
            if any(p not in end for p in needs):
                continue
            start = max([free[e]] + [end[p] for p in needs])
            key = (start, -way((e, step)))
            if best is None or key < best[0]:
                best = (key, k, step, us, lag)
        (start, _), k, step, us, lag = best
        e = k[0]
        free[e] = start + us
        end[e, step] = start + us + lag
        at[k] += 1
        order[e].append(step)
        if e == "PE":
            (scores if step[0] == "S" else turned if step[0] == "T" else groups).append(step)
        taken += e == "DVE" and step[0] == "S"
        if step[0] == "labels":
            meeting = step[1]
        elif step[0] == "wd" and e == "PE" and step[2] == 1:
            meeting = None
    return order, groups


ORDER, GROUPS = schedule()
SPLIT = ("agg", "wd", "xt", "q", "k", "v", "hx")
NUMBER = {k: n for n, k in enumerate(GROUPS)}


def steps(engine, *kinds):
    return [k for k in ORDER[engine] if k[0] in kinds]


class Signal:

    def __init__(self, sem, keys):
        self.sem = sem
        self.where = {k: n + 1 for n, k in enumerate(keys)}
        assert len(self.where) == len(keys)

    def at(self, key):
        return self.where[key]


def terms3(lh, ll, rh, rl):
    return [(lh, rl), (ll, rh), (lh, rh)]


def build(nc, x, xT, adj, adjT, wraw, wfold, wgen, bcols, rep, rep_bo, out):
    ctx = ExitStack()
    with ctx:
        at = [nc.sbuf_base + 63 & ~63]

        def sb(name, shape, dt, where=None):
            size = mybir.dt.size(dt)
            for n in shape[1:]:
                size *= n
            if where is None:
                where = at[0]
                at[0] += (size + 63) & ~63
            return nc.alloc_sbuf_tensor_at(name, shape, dt, offset=where), where

        def new(name, shape, dt):
            return sb(name, shape, dt)[0]

        wh = new("weights_high", [P, WCOLS], F32R)
        wl = new("weights_low", [P, WCOLS], F32R)
        wg = new("weights_labels", [P, GEN], F32)
        rp = new("rows_replicated", [P, len(REP) * D], F32)
        bc = new("bias_columns", [P, NBIAS], F32)
        ident = new("identity", [P, P], F32)
        ones = new("ones", [P, P], F32R)
        ones_b = new("ones_bf16", [P, P], BF16)

        probs = new("probs", [P, RING, N], F32)

        mbias, labT, xi, vh, vl, xTh, xTl, qh, ql, pth, ptl = ([] for _ in range(11))
        xf, lab_ats, above, more = [], [], [], []
        xh, xl, outh, outl, xTf, tA, tB, tC, mask, rc, flt = ([] for _ in range(11))
        v3t, q_at = [], []
        for s in range(SLOTS):
            t, bias_at = sb(f"mask_bias{s}", [P, NT, N], BF16)
            mbias.append(t)
            t, lab_at = sb(f"labels_T{s}", [P, NT, N], BF16)
            labT.append(t)
            t, xi_at = sb(f"x_nodes{s}", [P, NT, D], F32)
            xi.append(t)
            t, v_at = sb(f"v_high{s}", [P, NT, D], F32R)
            vh.append(t)
            t, vl_at = sb(f"v_low{s}", [P, NT, D], F32R)
            vl.append(t)
            t, xt_at = sb(f"xT_high{s}", [P, DT, N], F32R)
            xTh.append(t)
            xTl.append(sb(f"xT_low{s}", [P, DT, N], F32R)[0])
            t, qa = sb(f"q_high{s}", [P, DT, N], F32R)
            qh.append(t)
            ql.append(sb(f"q_low{s}", [P, DT, N], F32R)[0])
            q_at.append(qa)
            t, pt_at = sb(f"probsT_high{s}", [P, NT, N], F32R)
            pth.append(t)
            ptl.append(sb(f"probsT_low{s}", [P, NT, N], F32R)[0])
            kb = 1024
            xh.append(sb(f"x_high{s}", [P, NT, D], F32R, v_at)[0])
            xl.append(sb(f"x_low{s}", [P, NT, D], F32R, vl_at)[0])
            outh.append(sb(f"msg_high{s}", [P, DT, N], F32R, qa)[0])
            outl.append(sb(f"msg_low{s}", [P, DT, N], F32R, qa + 4 * kb)[0])
            above.append(sb(f"label_above_1_{s}", [P, NT, N], BF16, qa)[0])
            more.append(sb(f"more_messages{s}", [P, DT, N], F32, xi_at)[0])
            flt.append(sb(f"unsplit{s}", [P, DT, N], F32, xi_at)[0])
            xTf.append(sb(f"x_features{s}", [P, DT, N], F32, pt_at)[0])
            tA.append(sb(f"gate_r{s}", [P, DT, N], F32, pt_at + 4 * kb)[0])
            tB.append(sb(f"cand{s}", [P, DT, N], F32, pt_at + 8 * kb)[0])
            tC.append(sb(f"gate_z{s}", [P, DT, N], F32, pt_at + 12 * kb)[0])
            mask.append(sb(f"label_mask{s}", [P, NT, N], F32R, pt_at + 4 * kb)[0])
            rc.append(sb(f"one_over_count{s}", [P, N], F32, pt_at + 12 * kb)[0])
            v3t.append(sb(f"v3_{s}", [P, NT, HEADS, 2, HD], F32R, v_at)[0])
            lab_ats.append(lab_at)
            xf.append(sb(f"xT_unsplit{s}", [P, DT, N], F32, pt_at)[0])
        spare = at[0]
        at[0] += 4 * kb
        stq = [sb(f"stack_q{n}", [P, N], F32R, w)[0] for n, w in enumerate(lab_ats + [spare])]
        stk = [sb(f"stack_k{n}", [P, N], F32R, w + 2 * kb)[0] for n, w in enumerate(lab_ats + [spare])]
        ovs = new("pair_T", [P, N], F32)
        hn_i = new("heads_nodes", [P, NT, P], F32)
        hlo = new("pair_low", [P, NT, 2, HD], F32)

        rmax = new("row_max", [P, SLOTS * NT], F32)
        nmax = new("row_shift", [P, SLOTS * NT], F32)
        rsum = new("row_sum", [P, SLOTS, HEADS, NT], F32)
        rinv = new("row_inverse", [P, SLOTS, HEADS, NT], F32)
        nan_ = new("nan_without_edge", [P, SLOTS, NT], F32)
        flag = new("row_has_edge", [P, SLOTS, NT], F32)
        stats = new("ln_stats", [P, SLOTS, NT, 6], F32)
        mv = new("ln_mean_var", [P, SLOTS, NT, 2], F32)
        var = new("ln_var", [P, SLOTS, NT], F32)
        rstd = new("ln_rstd", [P, SLOTS, NT], F32)
        nt_ = new("ln_newton", [P, SLOTS, NT], F32)
        n_above = new("n_above", [1, SLOTS], F32)
        take_more = new("take_more", [1, SLOTS], I32)
        assert at[0] <= nc.sbuf_usable_end, (at[0], nc.sbuf_usable_end)
        raw = sb("weights_raw", [P, RAW], F32, (q_at[0] - 28 * kb))[0]
        fold_at = q_at[0] - 28 * kb + RAW * 4
        foldr = sb("fold_raw", [P, 4, DT, D], F32, fold_at)[0]
        foldh = sb("fold_high", [P, 4, DT, D], F32R, fold_at + 8 * kb)[0]
        foldl = sb("fold_low", [P, 4, DT, D], F32R, fold_at + 16 * kb)[0]
        bo_rows = sb("bo_rows", [P, 2, D], F32, fold_at + 24 * kb)[0]

        psS = ctx.enter_context(nc.psum_tensor("scores_bank", [P, 2, 512], F32))
        psT = ctx.enter_context(nc.psum_tensor("transposed_bank", [P, 2, 512], F32))
        psG = ctx.enter_context(nc.psum_tensor("group_bank", [P, GBANKS, 512], F32))

        def W(name, kt, lo=0, hi=None):
            off, width = COL[name]
            hi = width if hi is None else hi
            a, b = off + kt * width + lo, off + kt * width + hi
            return wh[:, a:b], wl[:, a:b]

        def bias(name, c=0):
            return bc[:, BCOL[name] + c:BCOL[name] + c + 1]

        def row(name):
            n = REP.index(name)
            return rp[:, n * D:(n + 1) * D]

        def f32(ap):
            return ap.bitcast(F32)

        def sem(name):
            return ctx.enter_context(nc.semaphore(name))

        w_in, f_in, c_in, id0, id1 = sem("w_in"), sem("f_in"), sem("c_in"), sem("id0"), sem("id1")
        w_hi, w_lo, f_hi, f_lo, fold_mm, fold_hi, fold_lo, b_done = (sem(n) for n in (
            "w_hi", "w_lo", "f_hi", "f_lo", "fold_mm", "fold_hi", "fold_lo", "b_done"))
        r_done = sem("r_done")
        CH = 1024
        chunks = [(a, min(a + CH, RAW)) for a in range(0, RAW, CH)]
        with nc.Block() as block:
            @block.sync
            def _(sp):
                sp.dma_start(foldr[:].rearrange("p a b c -> p (a b c)"), wfold).then_inc(f_in, 16)
                sp.dma_start(raw[:], wraw).then_inc(w_in, 16)
                sp.dma_start(wg[:], wgen).then_inc(c_in, 16)
                sp.dma_start(rp[:], rep).then_inc(c_in, 16)
                sp.dma_start(bc[:, 0:NB_IN], bcols).then_inc(c_in, 16)
                sp.dma_start(bo_rows[:].rearrange("p a d -> p (a d)"), rep_bo).then_inc(c_in, 16)
                sp.wait_ge(c_in, 64)

            @block.gpsimd
            def _(pool):
                nc.gpsimd.memset(ident[:], 0.0).then_inc(id0, 1)
                pool.wait_ge(id0, 1)
                nc.gpsimd.affine_select(out=ident[:], in_=ident[:], compare_op=ALU.not_equal, fill=1.0, base=0,
                                        pattern=[[-1, P]], channel_multiplier=1).then_inc(id0, 1)
                nc.gpsimd.memset(f32(ones[:]), 1.0).then_inc(id1, 1)
                nc.gpsimd.memset(ones_b[:], 1.0).then_inc(id1, 1)

            @block.scalar
            def _(act):
                act.wait_ge(f_in, 16)
                nc.scalar.copy(foldh[:], foldr[:]).then_inc(f_hi, 1)
                act.wait_ge(w_in, 16)
                for a, b in chunks:
                    nc.scalar.copy(wh[:, a:b], raw[:, a:b]).then_inc(w_hi, 1)
                for g in range(4):
                    act.wait_ge(fold_mm, g + 1)
                    a = RAW + g * D
                    nc.scalar.copy(wh[:, a:a + D], psG[:, g, 0:D]).then_inc(fold_hi, 1)

            @block.vector
            def _(dve):
                dve.wait_ge(f_hi, 1)
                nc.vector.tensor_sub(foldl[:], foldr[:], f32(foldh[:])).then_inc(f_lo, 1)
                for n, (a, b) in enumerate(chunks):
                    dve.wait_ge(w_hi, n + 1)
                    nc.vector.tensor_sub(wl[:, a:b], raw[:, a:b], f32(wh[:, a:b])).then_inc(w_lo, 1)
                for g in range(4):
                    dve.wait_ge(fold_hi, g + 1)
                    a = RAW + g * D
                    nc.vector.tensor_sub(wl[:, a:a + D], psG[:, g, 0:D], f32(wh[:, a:a + D])).then_inc(fold_lo, 1)
                dve.wait_ge(c_in, 64)
                for n, beta in enumerate(("b1b", "b2")):
                    nc.vector.tensor_add(row(beta), row(beta), bo_rows[:, n, :]).then_inc(r_done, 1)
                n = 0
                for to, parts in (("r", ("bri", "brh")), ("z", ("bzi", "bzh"))):
                    c, a, b = BCOL[to], BCOL[parts[0]], BCOL[parts[1]]
                    nc.vector.tensor_add(bc[:, c:c + DT], bc[:, a:a + DT], bc[:, b:b + DT]).then_inc(b_done, 1)
                    n += 1
                    dve.wait_ge(b_done, n)
                    nc.vector.tensor_scalar_mul(bc[:, c:c + DT], bc[:, c:c + DT], 0.5).then_inc(b_done, 1)
                    n += 1
                c, a = BCOL["h"], BCOL["bnh"]
                nc.vector.tensor_scalar_mul(bc[:, c:c + DT], bc[:, a:a + DT], 0.5).then_inc(b_done, 1)

            @block.tensor
            def _(pe):
                pe.wait_ge(f_lo, 1)
                for g in range(4):
                    left, right = (0, 1) if g < 2 else (2, 3)
                    c = slice((g % 2) * P, (g % 2) * P + P)
                    terms = []
                    for kt in range(DT):
                        terms += terms3(foldh[:, left, kt, c], foldl[:, left, kt, c],
                                        foldh[:, right, kt, :], foldl[:, right, kt, :])
                    for n, (a, b) in enumerate(terms):
                        mm = nc.tensor.matmul(psG[:, g, 0:D], a, b, start=(n == 0), stop=(n == len(terms) - 1))
                    mm.then_inc(fold_mm, 1)

        def signal(name, keys):
            return Signal(sem(name), list(keys))

        adj_in = [sem(f"adj_in{s}") for s in range(SLOTS)]
        lab_in = [sem(f"lab_in{s}") for s in range(SLOTS)]
        x_in = [sem(f"x_in{s}") for s in range(SLOTS)]
        xT_in = [sem(f"xT_in{s}") for s in range(SLOTS)]
        stack_in = [sem(f"stack_in{r}") for r in range(SLOTS + 1)]
        g_ready = signal("g_ready", [k for k in GROUPS if k[0] != "more"])
        s_ready = signal("s_ready", steps("PE", "S"))
        t_ready = signal("t_ready", steps("PE", "T"))
        x_hi = signal("x_hi", steps("ACT", "x", "xT"))
        hi = signal("hi", steps("ACT", *SPLIT))
        whole = signal("whole", steps("ACT", "wd", "xt"))
        act_gru = signal("act_gru", steps("ACT", "hn", "r", "in", "z"))
        p_ready = signal("p_ready", steps("ACT", "S"))
        pt_hi = signal("pt_hi", steps("ACT", "T"))
        ov_out = signal("ov_out", steps("ACT", "ov"))
        h_lo = signal("h_lo", steps("ACT", "ht"))
        x_lo = signal("x_lo", steps("DVE", "x"))
        labelled = signal("labelled", steps("DVE", "label"))
        compared = signal("compared", steps("DVE", "label"))
        told = signal("told", steps("DVE", "high"))
        cnt_read = signal("cnt_read", steps("DVE", "cnt"))
        rcs = signal("rcs", steps("DVE", "cnt"))
        full = signal("full", steps("DVE", "agg"))
        lo = signal("lo", [j for k in steps("DVE", "more", *SPLIT) if k[0] != "agg" for j in
                           ([("agg", k[1], ht) for ht in range(DT)] if k[0] == "more" else [k])])
        biased = signal("biased", steps("DVE", "bias"))
        dve_gru = signal("dve_gru", [k + (w,) for k in steps("DVE", "in", "z") for w in
                                     (("v", "w") if k[0] == "in" else ("e", "o"))])
        s_taken = signal("s_taken", steps("DVE", "S"))
        shifted = signal("shifted", steps("DVE", "S"))
        pt_lo = signal("pt_lo", steps("DVE", "T"))
        y_done = signal("y_done", steps("DVE", "pv", "y"))
        normed = signal("normed", steps("DVE", "norm"))
        h_done = signal("h_done", steps("DVE", "ht"))
        xT_lo = signal("xT_lo", steps("Pool", "xT"))
        pool_d = signal("pool_d", steps("Pool", "z"))
        affine = signal("affine", [k + (w,) for k in steps("Pool", "affine") for w in ("scaled", "shifted")])
        more_mask = [sem(f"more_mask{b}") for b in range(CHAIN)]
        more_sum = [sem(f"more_sum{b}") for b in range(CHAIN)]
        more_full = [sem(f"more_full{b}") for b in range(CHAIN)]
        more_used = [sem(f"more_used{b}") for b in range(CHAIN)]
        chain = sem("dve_chain")
        stored = [sem(f"stored{s}") for s in range(SLOTS)]
        sem_first, sem_last = x_in[0].num, stored[-1].num
        TURNS = CHAIN // SLOTS
        LAST = HEADS - 1

        def slot(b):
            return b % SLOTS

        def uses(b):
            return b // SLOTS + 1

        def stack_of(b, h):
            return slot(b) if h % 2 == 0 else SLOTS

        def stacked(b, h):
            users = [k for k in steps("SP", "stack") if stack_of(k[2], k[3]) == stack_of(b, h)]
            return (users.index(("stack", "3", b, h)) + 1) * 8 * 16

        def gbank(k):
            return psG[:, NUMBER[k] % GBANKS, :]

        def parts(k):
            kind = k[0]
            if kind in ("agg", "hx"):
                s = slot(k[1])
                return qh[s][:, k[2], :], ql[s][:, k[2], :]
            if kind == "wd":
                s = slot(k[1])
                return outh[s][:, k[2], :], outl[s][:, k[2], :]
            _, layer, b, c = k
            s = slot(b)
            if kind == "xt" or kind == "k" and layer == "3":
                return xTh[s][:, c, :], xTl[s][:, c, :]
            if kind == "q":
                return qh[s][:, c, :], ql[s][:, c, :]
            if kind == "k":
                return qh[s][:, 1, :], ql[s][:, 1, :]
            if layer == "3":
                return v3t[s][:, 2 * c:2 * c + 2, :, 0, :], v3t[s][:, 2 * c:2 * c + 2, :, 1, :]
            return vh[s][:, 2 * c:2 * c + 2, :], vl[s][:, 2 * c:2 * c + 2, :]

        def view(k, ap):
            if k[0] == "v":
                if k[1] == "3":
                    return ap.rearrange("p (j h d) -> p j h d", j=2, h=HEADS)
                return ap.rearrange("p (j d) -> p j d", j=2)
            return ap

        split_bias = {("q", "1a"): "bq1a", ("q", "1b"): "bq1b", ("k", "1a"): "bk1a", ("k", "1b"): "bk1b",
                      ("q", "3"): "bq3", ("k", "3"): "bk3"}

        def column(k):
            if k[0] == "hx":
                return bias("bv3", k[2])
            if k[0] in ("q", "k") and (k[0], k[1]) in split_bias:
                return bias(split_bias[k[0], k[1]], k[3])
            return None

        def pair(ap, w):
            return ap.rearrange("p (t h w d) -> p t h w d", h=2, w=2, d=HD)[:, :, :, w, :]

        tiles = {k[1:]: n for n, k in enumerate(steps("PE", "S"))}

        def ring(k):
            return probs[:, tiles[k[1:]] % RING, :]

        def turned(k):
            return psT[:, t_ready.at(k) % 2, :]

        def shift_col(k):
            c = slot(k[1][1]) * NT + k[2]
            return slice(c, c + 1)

        with nc.Fori(0, B // CHAIN) as i:
            with nc.Block() as block:
                @block.sync
                def _(sp):
                    for k in ORDER["SP"]:
                        kind = k[0]
                        if kind in ("x", "xT", "store"):
                            b = k[1]
                            s = slot(b)
                            g = i * CHAIN + b
                        if kind == "x":
                            if b >= SLOTS:
                                sp.wait_ge(stored[s], 16 * uses(b - SLOTS))
                            sp.dma_start(xi[s][:], x[g].rearrange("(t p) d -> p t d", p=P)).then_inc(x_in[s], 16)
                        elif kind == "xT":
                            if b >= SLOTS:
                                sp.wait_ge(g_ready.sem, g_ready.at(("ov", b - SLOTS, LAST, 1)))
                            sp.dma_start(xTf[s][:], xT[g].rearrange("(t p) n -> p t n", p=P)).then_inc(xT_in[s], 16)
                        elif kind == "stack":
                            _, _, b, h = k
                            s, n = slot(b), stack_of(b, h)
                            c, r = h // 4, slice(HD * (h % 4), HD * (h % 4) + HD)
                            sp.wait_ge(lo.sem, lo.at(("k", "3", b, c)))
                            if h > 1:
                                sp.wait_ge(s_ready.sem, s_ready.at(("S", ("3", b, h - 2), NT - 1)))
                            elif h and b:
                                sp.wait_ge(s_ready.sem, s_ready.at(("S", ("3", b - 1, LAST), NT - 1)))
                            for to, blocks in ((stq, (qh, qh, ql, ql)), (stk, (xTh, xTl, xTh, xTl))):
                                for j, src in enumerate(blocks):
                                    sp.dma_start(f32(to[n][HD * j:HD * j + HD, :]), f32(src[s][r, c, :])).then_inc(stack_in[n], 16)
                        elif kind == "store":
                            sp.wait_ge(affine.sem, affine.at(("affine", "3", b, "shifted")))
                            sp.dma_start(out[g].rearrange("(t p) d -> p t d", p=P), xi[s][:]).then_inc(stored[s], 16)
                    for s in range(SLOTS):
                        sp.wait_ge(stored[s], 16 * TURNS)

                @block.gpsimd
                def _(pool):
                    for k in ORDER["Pool"]:
                        kind = k[0]
                        if kind == "lab":
                            b = k[1]
                            if b >= SLOTS:
                                pool.wait_ge(s_ready.sem, s_ready.at(("S", ("3", b - SLOTS, LAST - 1), NT - 1)))
                            nc.gpsimd.dma_start(labT[slot(b)][:], adjT[i * CHAIN + b].rearrange("(t p) n -> p t n", p=P))\
                                .then_inc(lab_in[slot(b)], 16)
                        elif kind == "adj":
                            b = k[1]
                            if b >= SLOTS:
                                pool.wait_ge(s_taken.sem, s_taken.at(("S", ("3", b - SLOTS, LAST), NT - 1)))
                            nc.gpsimd.dma_start(mbias[slot(b)][:], adj[i * CHAIN + b].rearrange("(t p) n -> p t n", p=P))\
                                .then_inc(adj_in[slot(b)], 16)
                        elif kind == "xT":
                            s = slot(k[1])
                            pool.wait_ge(x_hi.sem, x_hi.at(k))
                            nc.gpsimd.tensor_sub(xTl[s][:], xTf[s][:], f32(xTh[s][:])).then_inc(xT_lo.sem, 1)
                        elif kind == "z":
                            _, b, et = k
                            s = slot(b)
                            pool.wait_ge(act_gru.sem, act_gru.at(("in", b, et)))
                            nc.gpsimd.tensor_sub(tA[s][:, et, :], xTf[s][:, et, :], tB[s][:, et, :]).then_inc(pool_d.sem, 1)
                        elif kind == "affine":
                            _, layer, b = k
                            s = slot(b)
                            if layer == "3":
                                pool.wait_ge(normed.sem, normed.at(("norm", "3", b)))
                            else:
                                pool.wait_ge(g_ready.sem, g_ready.at(("xt", layer, b, DT - 1)))
                            g, beta = (row(w + layer).unsqueeze(1).to_broadcast([P, NT, D]) for w in "gb")
                            nc.gpsimd.tensor_mul(xi[s][:], xi[s][:], g).then_inc(affine.sem, 1)
                            pool.wait_ge(affine.sem, affine.at(k + ("scaled",)))
                            nc.gpsimd.tensor_add(xi[s][:], xi[s][:], beta).then_inc(affine.sem, 1)

                @block.scalar
                def _(act):
                    for k in ORDER["ACT"]:
                        kind = k[0]
                        if kind == "x":
                            b = k[1]
                            act.wait_ge(x_in[slot(b)], 16 * uses(b))
                            nc.scalar.copy(xh[slot(b)][:], xi[slot(b)][:]).then_inc(x_hi.sem, 1)
                        elif kind == "xT":
                            b = k[1]
                            act.wait_ge(xT_in[slot(b)], 16 * uses(b))
                            nc.scalar.copy(xTh[slot(b)][:], xTf[slot(b)][:]).then_inc(x_hi.sem, 1)
                        elif kind == "agg":
                            act.wait_ge(full.sem, full.at(k))
                            nc.scalar.copy(parts(k)[0], flt[slot(k[1])][:, k[2], :]).then_inc(hi.sem, 1)
                        elif kind == "wd":
                            _, b, et = k
                            act.wait_ge(g_ready.sem, g_ready.at(("wd", b, DT - 1)))
                            nc.scalar.activation(parts(k)[0], gbank(k), ACT.Relu, bias=bias("bd", et)).then_inc(hi.sem, 1)
                            nc.scalar.activation(flt[slot(b)][:, et, :], gbank(k), ACT.Relu, bias=bias("bd", et))\
                                .then_inc(whole.sem, 1)
                        elif kind == "xt":
                            _, layer, b, dt = k
                            act.wait_ge(g_ready.sem, g_ready.at(k))
                            g, beta = bias("g" + layer, dt), bias("b" + layer, dt)
                            nc.scalar.activation(parts(k)[0], gbank(k), ACT.Identity, bias=beta, scale=g).then_inc(hi.sem, 1)
                            nc.scalar.activation(xf[slot(b)][:, dt, :], gbank(k), ACT.Identity, bias=beta, scale=g)\
                                .then_inc(whole.sem, 1)
                        elif kind in ("hn", "r", "z"):
                            _, b, et = k
                            act.wait_ge(g_ready.sem, g_ready.at(k))
                            to, fn, col = {"hn": (tB, ACT.Identity, "h"), "r": (tA, ACT.Tanh, "r"), "z": (tC, ACT.Tanh, "z")}[kind]
                            nc.scalar.activation(to[slot(b)][:, et, :], gbank(k), fn, bias=bias(col, et), scale=0.5)\
                                .then_inc(act_gru.sem, 1)
                        elif kind == "in":
                            _, b, et = k
                            act.wait_ge(dve_gru.sem, dve_gru.at(k + ("w",)))
                            c = tB[slot(b)][:, et, :]
                            nc.scalar.activation(c, c, ACT.Tanh, bias=bias("bni", et)).then_inc(act_gru.sem, 1)
                        elif kind in ("q", "k", "v", "hx"):
                            act.wait_ge(g_ready.sem, g_ready.at(k))
                            if k[:2] == ("k", "3"):
                                act.wait_ge(g_ready.sem, g_ready.at(k[:3] + (DT - 1,)))
                            high, col = parts(k)[0], column(k)
                            if col is None:
                                a = nc.scalar.copy(high, view(k, gbank(k)))
                            else:
                                a = nc.scalar.activation(high, gbank(k), ACT.Identity, bias=col)
                            a.then_inc(hi.sem, 1)
                        elif kind == "S":
                            _, u, it = k
                            act.wait_ge(shifted.sem, shifted.at(k))
                            nc.scalar.activation(ring(k), ring(k), ACT.Exp, bias=nmax[:, shift_col(k)], scale=SCALE[u[0]],
                                                 accum_out=rsum[:, slot(u[1]), u[2], it:it + 1]).then_inc(p_ready.sem, 1)
                        elif kind == "T":
                            _, u, it = k
                            act.wait_ge(t_ready.sem, t_ready.at(k))
                            if u[2]:
                                act.wait_ge(g_ready.sem, g_ready.at(("ov", u[1], u[2] - 1, it // 2)))
                            nc.scalar.copy(pth[slot(u[1])][:, :, it * P:(it + 1) * P],
                                           turned(k).rearrange("p (j i) -> p j i", j=NT)).then_inc(pt_hi.sem, 1)
                        elif kind == "ov":
                            _, b, h, half = k
                            rows = slice((h % 2) * 64, (h % 2) * 64 + 64)
                            act.wait_ge(g_ready.sem, g_ready.at(k))
                            if h > 1:
                                act.wait_ge(g_ready.sem, g_ready.at(("ht", b, h // 2 - 1)))
                            elif b:
                                act.wait_ge(g_ready.sem, g_ready.at(("ht", b - 1, HEADS // 2 - 1)))
                            nc.scalar.copy(ovs[rows, half * D:(half + 1) * D], gbank(k)[rows, 0:D]).then_inc(ov_out.sem, 1)
                        elif kind == "ht":
                            _, b, p = k
                            act.wait_ge(g_ready.sem, g_ready.at(k))
                            if p:
                                act.wait_ge(h_done.sem, h_done.at(("ht", b, p - 1)))
                            elif b:
                                act.wait_ge(h_done.sem, h_done.at(("ht", b - 1, HEADS // 2 - 1)))
                            nc.scalar.copy(hlo[:], pair(gbank(k), 1)).then_inc(h_lo.sem, 1)

                @block.vector
                def _(dve):
                    links = [0]

                    def link(ins):
                        links[0] += 1
                        ins.then_inc(chain, 1)
                        dve.wait_ge(chain, links[0])

                    def moments(s, it, src):
                        return nc.vector.bn_stats(stats[:, s, it, :], src)

                    def layer_norm(s, src):
                        for it in range(NT):
                            st = nc.vector.bn_aggr(mv[:, s, it, :], stats[:, s, it, :])
                        link(st)
                        v, y, t = var[:, s, :], rstd[:, s, :], nt_[:, s, :]
                        link(nc.vector.tensor_scalar_add(v, mv[:, s, :, 1], LN_EPS))
                        link(nc.vector.tensor_single_scalar(t.bitcast(I32), v.bitcast(I32), 1, ALU.logical_shift_right))
                        link(nc.vector.tensor_scalar(y.bitcast(I32), t.bitcast(I32), -1.0, float(0x5F3759DF), ALU.mult, ALU.add))
                        for _ in range(3):
                            link(nc.vector.tensor_mul(t, y, y))
                            link(nc.vector.scalar_tensor_tensor(out=t, in0=t, scalar=-0.5, in1=v, op0=ALU.mult, op1=ALU.mult))
                            link(nc.vector.scalar_tensor_tensor(out=y, in0=t, scalar=1.5, in1=y, op0=ALU.add, op1=ALU.mult))
                        for it in range(NT):
                            a = nc.vector.tensor_scalar(xi[s][:, it, :], src(it), mv[:, s, it, 0:1], y[:, it:it + 1],
                                                        ALU.subtract, ALU.mult)
                        return a

                    def more_labels(b):
                        s, bank = slot(b), gbank(("more", b))
                        for n in range(LABELS - 1):
                            nc.vector.tensor_scalar(mask[s][:], labT[s][:], float(n + 2), None, ALU.is_equal)\
                                .then_inc(more_mask[b], 1)
                            dve.wait_ge(more_sum[b], 3 * n + 1)
                            nc.vector.tensor_scalar_add(rc[s][:], bank, CNT_EPS).then_inc(more_full[b], 1)
                            dve.wait_ge(more_full[b], 4 * n + 1)
                            nc.vector.reciprocal(rc[s][:], rc[s][:]).then_inc(more_full[b], 1)
                            dve.wait_ge(more_full[b], 4 * n + 2)
                            for ht in range(DT):
                                dve.wait_ge(more_sum[b], 3 * n + 2 + ht)
                                nc.vector.tensor_mul(more[s][:, ht, :], bank, rc[s][:]).then_inc(more_full[b], 1)
                            dve.wait_ge(more_used[b], n + 1)

                    for k in ORDER["DVE"]:
                        kind = k[0]
                        if kind == "x":
                            s = slot(k[1])
                            dve.wait_ge(x_hi.sem, x_hi.at(k))
                            nc.vector.tensor_sub(xl[s][:], xi[s][:], f32(xh[s][:])).then_inc(x_lo.sem, 1)
                        elif kind == "label":
                            b = k[1]
                            s = slot(b)
                            dve.wait_ge(lab_in[s], i * (16 * TURNS) + 16 * uses(b))
                            nc.vector.tensor_scalar(mask[s][:], labT[s][:], 1.0, None, ALU.is_equal).then_inc(labelled.sem, 1)
                            nc.vector.tensor_scalar(above[s][:], labT[s][:], 2.0, None, ALU.is_ge).then_inc(compared.sem, 1)
                        elif kind == "cnt":
                            s = slot(k[1])
                            dve.wait_ge(g_ready.sem, g_ready.at(k))
                            nc.vector.tensor_scalar_add(rc[s][:], gbank(k), CNT_EPS).then_inc(cnt_read.sem, 1)
                            dve.wait_ge(cnt_read.sem, cnt_read.at(k))
                            nc.vector.reciprocal(rc[s][:], rc[s][:]).then_inc(rcs.sem, 1)
                        elif kind == "high":
                            s = slot(k[1])
                            dve.wait_ge(g_ready.sem, g_ready.at(k))
                            link(nc.vector.tensor_reduce(n_above[:, s:s + 1], gbank(k)[0:1, :], AX_X, ALU.max))
                            nc.vector.tensor_copy(take_more[:, s:s + 1], n_above[:, s:s + 1]).then_inc(told.sem, 1)
                        elif kind == "agg":
                            _, b, ht = k
                            dve.wait_ge(rcs.sem, rcs.at(("cnt", b)))
                            dve.wait_ge(x_lo.sem, x_lo.at(("x", b)))
                            dve.wait_ge(g_ready.sem, g_ready.at(k))
                            nc.vector.tensor_mul(flt[slot(b)][:, ht, :], gbank(k), rc[slot(b)][:]).then_inc(full.sem, 1)
                        elif kind == "more":
                            s, b = slot(k[1]), k[1]
                            for ht in range(DT):
                                k2 = ("agg", b, ht)
                                dve.wait_ge(hi.sem, hi.at(k2))
                                nc.vector.tensor_sub(parts(k2)[1], flt[s][:, ht, :], f32(parts(k2)[0])).then_inc(lo.sem, 1)
                        elif kind == "labels":
                            b = k[1]
                            s = slot(b)
                            dve.wait_ge(told.sem, told.at(("high", b)))
                            with dve.If(dve.value_load(take_more[0:1, s:s + 1]) > 0):
                                more_labels(b)
                        elif kind == "bias":
                            b = k[1]
                            s = slot(b)
                            dve.wait_ge(adj_in[s], i * (16 * TURNS) + 16 * uses(b))
                            nc.vector.tensor_scalar(mbias[s][:], mbias[s][:], 0.0, MASKED, ALU.is_equal, ALU.mult)\
                                .then_inc(biased.sem, 1)
                        elif kind == "in":
                            _, b, et = k
                            c = tB[slot(b)][:, et, :]
                            dve.wait_ge(act_gru.sem, act_gru.at(("r", b, et)))
                            nc.vector.scalar_tensor_tensor(out=c, in0=tA[slot(b)][:, et, :], scalar=1.0, in1=c,
                                                           op0=ALU.add, op1=ALU.mult).then_inc(dve_gru.sem, 1)
                            dve.wait_ge(dve_gru.sem, dve_gru.at(k + ("v",)))
                            dve.wait_ge(g_ready.sem, g_ready.at(k))
                            nc.vector.tensor_add(c, c, gbank(k)).then_inc(dve_gru.sem, 1)
                        elif kind == "z":
                            _, b, et = k
                            s = slot(b)
                            a = tA[s][:, et, :]
                            dve.wait_ge(pool_d.sem, pool_d.at(k))
                            dve.wait_ge(act_gru.sem, act_gru.at(k))
                            nc.vector.scalar_tensor_tensor(out=a, in0=tC[s][:, et, :], scalar=1.0, in1=a,
                                                           op0=ALU.add, op1=ALU.mult).then_inc(dve_gru.sem, 1)
                            dve.wait_ge(dve_gru.sem, dve_gru.at(k + ("e",)))
                            nc.vector.scalar_tensor_tensor(out=a, in0=a, scalar=0.5, in1=tB[s][:, et, :],
                                                           op0=ALU.mult, op1=ALU.add).then_inc(dve_gru.sem, 1)
                        elif kind == "norm":
                            _, layer, b = k
                            s = slot(b)
                            if layer == "0":
                                def src(it):
                                    return gbank(("lt", b, it // 2))[:, (it % 2) * D:(it % 2 + 1) * D]
                                dve.wait_ge(lo.sem, lo.at(("wd", b, DT - 1)))
                                for it in range(NT):
                                    if it % 2 == 0:
                                        dve.wait_ge(g_ready.sem, g_ready.at(("lt", b, it // 2)))
                                    st = moments(s, it, src(it))
                                link(st)
                                layer_norm(s, src).then_inc(normed.sem, 1)
                            else:
                                layer_norm(s, lambda it: xi[s][:, it, :]).then_inc(normed.sem, 1)
                        elif kind in ("wd", "xt"):
                            s = slot(k[1] if kind == "wd" else k[2])
                            high, low = parts(k)
                            dve.wait_ge(whole.sem, whole.at(k))
                            nc.vector.tensor_sub(low, (flt if kind == "wd" else xf)[s][:, k[-1], :], f32(high)).then_inc(lo.sem, 1)
                        elif kind in ("q", "k", "v", "hx"):
                            high, low = parts(k)
                            col = column(k)
                            dve.wait_ge(hi.sem, hi.at(k))
                            src = view(k, gbank(k))
                            if col is None:
                                a = nc.vector.tensor_sub(low, src, f32(high))
                            else:
                                a = nc.vector.scalar_tensor_tensor(out=low, in0=src, scalar=col, in1=f32(high),
                                                                   op0=ALU.add, op1=ALU.subtract)
                            a.then_inc(lo.sem, 1)
                        elif kind == "S":
                            _, u, it = k
                            b, n = u[1], tiles[k[1:]]
                            dve.wait_ge(s_ready.sem, s_ready.at(k))
                            if u[0] == "1a" and it == 0:
                                dve.wait_ge(biased.sem, biased.at(("bias", b)))
                            if n >= RING:
                                dve.wait_ge(t_ready.sem, t_ready.at(("T",) + steps("PE", "S")[n - RING][1:]))
                            nc.vector.tensor_tensor_reduce(out=ring(k), in0=psS[:, n % 2, :], in1=mbias[slot(b)][:, it, :],
                                                           scale=1.0, scalar=LOWEST, op0=ALU.add, op1=ALU.max,
                                                           accum_out=rmax[:, shift_col(k)]).then_inc(s_taken.sem, 1)
                            dve.wait_ge(s_taken.sem, s_taken.at(k))
                            nc.vector.tensor_scalar_mul(nmax[:, shift_col(k)], rmax[:, shift_col(k)], -SCALE[u[0]])\
                                .then_inc(shifted.sem, 1)
                        elif kind == "T":
                            _, u, it = k
                            o = slice(it * P, (it + 1) * P)
                            dve.wait_ge(pt_hi.sem, pt_hi.at(k))
                            nc.vector.tensor_sub(ptl[slot(u[1])][:, :, o], turned(k).rearrange("p (j i) -> p j i", j=NT),
                                                 f32(pth[slot(u[1])][:, :, o])).then_inc(pt_lo.sem, 1)
                        elif kind == "pv":
                            _, layer, b, ip = k
                            s = slot(b)
                            if ip == 0:
                                if layer == "1a":
                                    link(nc.vector.tensor_scalar(flag[:, s, :], rmax[:, s * NT:(s + 1) * NT], MASKED / 2, None,
                                                                 ALU.is_ge))
                                link(nc.vector.reciprocal(rinv[:, s, 0, :], rsum[:, s, 0, :]))
                                if layer in ("1a", "1b"):
                                    link(nc.vector.tensor_mul(rinv[:, s, 0, :], rinv[:, s, 0, :], flag[:, s, :]))
                                dve.wait_ge(affine.sem, affine.at(("affine", BEFORE[layer], b, "shifted")))
                            dve.wait_ge(g_ready.sem, g_ready.at(k))
                            for j in range(2):
                                it = 2 * ip + j
                                a = nc.vector.scalar_tensor_tensor(out=xi[s][:, it, :], in0=gbank(k)[:, j * D:(j + 1) * D],
                                                                   scalar=rinv[:, s, 0, it:it + 1], in1=xi[s][:, it, :],
                                                                   op0=ALU.mult, op1=ALU.add)
                            a.then_inc(y_done.sem, 1)
                            dve.wait_ge(y_done.sem, y_done.at(k))
                            for it in (2 * ip, 2 * ip + 1):
                                st = moments(s, it, xi[s][:, it, :])
                            link(st)
                        elif kind == "ht":
                            _, b, p = k
                            s = slot(b)
                            r = rinv[:, s, 2 * p:2 * p + 2, :]
                            if p == 0:
                                link(nc.vector.reciprocal(nan_[:, s, :], flag[:, s, :]))
                                link(nc.vector.tensor_mul(nan_[:, s, :], nan_[:, s, :], flag[:, s, :]))
                            link(nc.vector.reciprocal(r, rsum[:, s, 2 * p:2 * p + 2, :]))
                            link(nc.vector.tensor_mul(r, r, nan_[:, s, :].unsqueeze(1).to_broadcast([P, 2, NT])))
                            if p == 2:
                                dve.wait_ge(g_ready.sem, g_ready.at(("hx", b, 0)))
                            elif p == 0 and b:
                                dve.wait_ge(g_ready.sem, g_ready.at(("hx", b - 1, DT - 1)))
                            dve.wait_ge(h_lo.sem, h_lo.at(k))
                            o = hn_i[:].rearrange("p t (h d) -> p t h d", d=HD)[:, :, 2 * (p % 2):2 * (p % 2) + 2, :]
                            link(nc.vector.tensor_add(o, pair(gbank(k), 0), hlo[:]))
                            r = r.rearrange("p h t -> p t h").unsqueeze(3).to_broadcast([P, NT, 2, HD])
                            nc.vector.tensor_mul(o, o, r).then_inc(h_done.sem, 1)
                        elif kind == "y":
                            _, b, ip = k
                            s = slot(b)
                            if ip == 0:
                                dve.wait_ge(affine.sem, affine.at(("affine", "2", b, "shifted")))
                            dve.wait_ge(g_ready.sem, g_ready.at(k))
                            to = xi[s][:, 2 * ip:2 * ip + 2, :]
                            nc.vector.tensor_add(to, gbank(k).rearrange("p (j d) -> p j d", j=2), to).then_inc(y_done.sem, 1)
                            dve.wait_ge(y_done.sem, y_done.at(k))
                            for it in (2 * ip, 2 * ip + 1):
                                st = moments(s, it, xi[s][:, it, :])
                            link(st)

                @block.tensor
                def _(pe):
                    def claim(k):
                        if NUMBER[k] < GBANKS:
                            return
                        p = GROUPS[NUMBER[k] - GBANKS]
                        kind = p[0]
                        if kind == "cnt":
                            pe.wait_ge(cnt_read.sem, cnt_read.at(p))
                        elif kind == "high":
                            pe.wait_ge(told.sem, told.at(p))
                        elif kind == "agg":
                            pe.wait_ge(full.sem, full.at(p))
                        elif kind in ("wd", "xt"):
                            pe.wait_ge(whole.sem, whole.at(p))
                        elif kind in ("hn", "r", "z"):
                            pe.wait_ge(act_gru.sem, act_gru.at(p))
                        elif kind == "in":
                            pe.wait_ge(dve_gru.sem, dve_gru.at(p + ("w",)))
                        elif kind == "lt":
                            pe.wait_ge(normed.sem, normed.at(("norm", "0", p[1])))
                        elif kind in ("pv", "y"):
                            pe.wait_ge(y_done.sem, y_done.at(p))
                        elif kind == "ov":
                            pe.wait_ge(ov_out.sem, ov_out.at(p))
                        elif kind == "ht":
                            pe.wait_ge(h_done.sem, h_done.at(p))
                        elif kind != "more":
                            pe.wait_ge(lo.sem, lo.at(p))

                    def run(ps, terms):
                        for n, (a, b) in enumerate(terms):
                            mm = nc.tensor.matmul(ps, a, b, start=(n == 0), stop=(n == len(terms) - 1))
                        return mm

                    def turn(ps, srcs):
                        for n, src in enumerate(srcs):
                            mm = nc.tensor.transpose(ps[:, n * P:(n + 1) * P], src, ident[:])
                        return mm

                    def features(name, s, c, high, low):
                        t = []
                        for kt in range(DT):
                            w = W(name, kt, c * P, (c + 1) * P)
                            t += terms3(w[0], w[1], high[s][:, kt, :], low[s][:, kt, :])
                        return t

                    def neighbours(s, ht):
                        c = slice(ht * P, (ht + 1) * P)
                        return [(w[s][:, nt, c], mask[s][:, nt, :]) for nt in range(NT) for w in (xl, xh)]

                    def more_labels(b):
                        s, bank = slot(b), gbank(("more", b))
                        for n in range(LABELS - 1):
                            pe.wait_ge(more_mask[b], n + 1)
                            run(bank, [(ones[:], mask[s][:, nt, :]) for nt in range(NT)]).then_inc(more_sum[b], 1)
                            for ht in range(DT):
                                pe.wait_ge(more_full[b], 4 * n + 1 if ht == 0 else 4 * n + 3)
                                run(bank, neighbours(s, ht)).then_inc(more_sum[b], 1)
                            pe.wait_ge(more_full[b], 4 * n + 4)
                            for et in range(DT):
                                for kt in range(DT):
                                    c = (n * DT + kt) * D + et * P
                                    mm = nc.tensor.matmul(gbank(("wd", b, et)), wg[:, c:c + P], more[s][:, kt, :],
                                                          start=False, stop=False, skip_group_check=True)
                            mm.then_inc(more_used[b], 1)

                    for k in ORDER["PE"]:
                        kind = k[0]
                        if kind not in ("S", "T"):
                            claim(k)
                            ps = gbank(k)
                        if kind in ("cnt", "agg", "more", "wd", "hn", "r", "in", "z", "lt", "ov", "ht", "hx", "y"):
                            b = k[1]
                            s = slot(b)
                        if kind == "cnt":
                            pe.wait_ge(labelled.sem, labelled.at(("label", b)))
                            mm = run(ps, [(ones[:], mask[s][:, nt, :]) for nt in range(NT)])
                        elif kind == "high":
                            s = slot(k[1])
                            pe.wait_ge(compared.sem, compared.at(("label", k[1])))
                            mm = run(ps, [(ones_b[:], above[s][:, nt, :]) for nt in range(NT)])
                        elif kind == "agg":
                            pe.wait_ge(x_lo.sem, x_lo.at(("x", b)))
                            mm = run(ps, neighbours(s, k[2]))
                        elif kind == "more":
                            mm = None
                        elif kind == "wd":
                            et = k[2]
                            if et == 0:
                                pe.wait_ge(lo.sem, lo.at(("agg", b, DT - 1)))
                            t = features("wd1", s, et, qh, ql)
                            for n, (a, c) in enumerate(t[:-1]):
                                nc.tensor.matmul(ps, a, c, start=(n == 0), stop=False)
                            mm = None
                            if et == DT - 1:
                                pe.wait_ge(told.sem, told.at(("high", b)))
                                with pe.If(pe.value_load(take_more[0:1, s:s + 1]) > 0):
                                    more_labels(b)
                                for e in range(DT):
                                    a, c = features("wd1", s, e, qh, ql)[-1]
                                    nc.tensor.matmul(gbank(("wd", b, e)), a, c, start=False, stop=True).then_inc(g_ready.sem, 1)
                        elif kind in ("hn", "r", "in", "z"):
                            et = k[2]
                            if kind == "hn" and et == 0:
                                pe.wait_ge(xT_lo.sem, xT_lo.at(("xT", b)))
                            t = []
                            if kind != "in":
                                t += features({"hn": "nh", "r": "rh", "z": "zh"}[kind], s, et, xTh, xTl)
                            if kind != "hn":
                                pe.wait_ge(lo.sem, lo.at(("wd", b, DT - 1)))
                                t += features({"in": "ni", "r": "ri", "z": "zi"}[kind], s, et, outh, outl)
                            mm = run(ps, t)
                        elif kind == "lt":
                            pe.wait_ge(dve_gru.sem, dve_gru.at(("z", b, DT - 1, "o")))
                            mm = turn(ps, [tA[s][:, dt, (2 * k[2] + j) * P:(2 * k[2] + j + 1) * P]
                                           for j in range(2) for dt in range(DT)])
                        elif kind == "xt":
                            _, layer, b, dt = k
                            pe.wait_ge(normed.sem, normed.at(("norm", layer, b)))
                            mm = turn(ps, [xi[slot(b)][:, it, dt * P:(dt + 1) * P] for it in range(NT)])
                        elif kind in ("q", "k"):
                            _, layer, b, c = k
                            pe.wait_ge(lo.sem, lo.at(("xt", BEFORE[layer], b, DT - 1)))
                            mm = run(ps, features("a2" if layer == "2" else kind + layer, slot(b), c if layer in "23" else 0,
                                                  xTh, xTl))
                        elif kind == "v":
                            _, layer, b, jp = k
                            s = slot(b)
                            pe.wait_ge(lo.sem, lo.at(("xt", BEFORE[layer], b, DT - 1)))
                            for j in range(2):
                                jt = slice((2 * jp + j) * P, (2 * jp + j + 1) * P)
                                t = []
                                for kt in range(DT):
                                    w = W("v3" if layer == "3" else "c" + layer, kt)
                                    t += terms3(xTh[s][:, kt, jt], xTl[s][:, kt, jt], w[0], w[1])
                                mm = run(ps[:, j * D:(j + 1) * D], t)
                        elif kind == "S":
                            _, u, it = k
                            layer, b, h = u
                            s, n = slot(b), tiles[k[1:]]
                            i_ = slice(it * P, (it + 1) * P)
                            if n >= 2:
                                pe.wait_ge(s_taken.sem, s_taken.at(steps("PE", "S")[n - 2]))
                            if layer == "3":
                                r = stack_of(b, h)
                                if it == 0:
                                    pe.wait_ge(stack_in[r], stacked(b, h))
                                t = [(stq[r][:, i_], stk[r][:, :])]
                            elif layer == "2":
                                if it == 0:
                                    pe.wait_ge(lo.sem, lo.at(("q", "2", b, DT - 1)))
                                t = []
                                for c in range(DT):
                                    t += terms3(qh[s][:, c, i_], ql[s][:, c, i_], xTh[s][:, c, :], xTl[s][:, c, :])
                            else:
                                if it == 0:
                                    pe.wait_ge(lo.sem, lo.at(("k", layer, b, 0)))
                                t = terms3(qh[s][:, 0, i_], ql[s][:, 0, i_], qh[s][:, 1, :], ql[s][:, 1, :])
                            run(psS[:, n % 2, :], t).then_inc(s_ready.sem, 1)
                        elif kind == "T":
                            n = t_ready.at(k)
                            pe.wait_ge(p_ready.sem, p_ready.at(("S",) + k[1:]))
                            if n > 2:
                                pe.wait_ge(pt_lo.sem, pt_lo.at(steps("PE", "T")[n - 3]))
                            turn(turned(k), [ring(k)[:, jt * P:(jt + 1) * P] for jt in range(NT)]).then_inc(t_ready.sem, 1)
                        elif kind == "pv":
                            _, layer, b, ip = k
                            s = slot(b)
                            if ip == 0:
                                pe.wait_ge(lo.sem, lo.at(("v", layer, b, 1)))
                                pe.wait_ge(pt_lo.sem, pt_lo.at(("T", (layer, b, 0), NT - 1)))
                            for j in range(2):
                                i_ = slice((2 * ip + j) * P, (2 * ip + j + 1) * P)
                                t = []
                                for jt in range(NT):
                                    t += terms3(pth[s][:, jt, i_], ptl[s][:, jt, i_], vh[s][:, jt, :], vl[s][:, jt, :])
                                mm = run(ps[:, j * D:(j + 1) * D], t)
                        elif kind == "ov":
                            _, b, h, half = k
                            i_ = slice(half * D, (half + 1) * D)
                            pe.wait_ge(lo.sem, lo.at(("v", "3", b, 1)))
                            pe.wait_ge(pt_lo.sem, pt_lo.at(("T", ("3", b, h), 2 * half + 1)))
                            t = []
                            for jt in range(NT):
                                v = v3t[s][:, jt, h // 2 * 2:h // 2 * 2 + 2, :, :].rearrange("p h w d -> p (h w d)")
                                t += [(v, ptl[s][:, jt, i_]), (v, pth[s][:, jt, i_])]
                            mm = run(ps[:, 0:D], t)
                        elif kind == "ht":
                            pe.wait_ge(ov_out.sem, ov_out.at(("ov", b, 2 * k[2] + 1, 1)))
                            mm = turn(ps, [ovs[:, it * P:(it + 1) * P] for it in range(NT)])
                        elif kind == "hx":
                            pe.wait_ge(h_done.sem, h_done.at(("ht", b, 2 * k[2] + 1)))
                            mm = turn(ps, [hn_i[:, it, :] for it in range(NT)])
                        elif kind == "y":
                            pe.wait_ge(lo.sem, lo.at(("hx", b, DT - 1)))
                            for j in range(2):
                                i_ = slice((2 * k[2] + j) * P, (2 * k[2] + j + 1) * P)
                                t = []
                                for kt in range(DT):
                                    w = W("o3", kt)
                                    t += terms3(qh[s][:, kt, i_], ql[s][:, kt, i_], w[0], w[1])
                                mm = run(ps[:, j * D:(j + 1) * D], t)
                        if kind not in ("S", "T") and mm is not None:
                            mm.then_inc(g_ready.sem, 1)

            nc.gpsimd.sem_clear(range(sem_first, sem_last + 1))
            nc.all_engine_barrier()


def kernel(**inputs):
    import numpy as np
    import concourse.bacc as bacc
    from concourse.bass_utils import run_bass_kernel_spmd as run

    a = {k: np.asarray(v) for k, v in inputs.items()}

    def ktiles(m):
        return m.reshape(-1, P, m.shape[1]).transpose(1, 0, 2).reshape(P, -1)

    wd = a["L0_gnn_Wd"]
    g0, g1, g2, g3 = "L0_gnn_", "L1_gnn_", "L2_gnn_", "L3_gnn_"
    mats = [wd[:, 0:D].T] + [a[g0 + "W" + n].T for n in ("ri", "rh", "zi", "zh", "ni", "nh")]
    for l in range(2):
        mats += [a[g1 + "Wq"][l].T, a[g1 + "Wk"][l].T, a[g1 + "Wc"][l].T]
    mats += [a[g3 + "W" + n] for n in "qkvo"]
    wraw = np.concatenate([ktiles(m) for m in mats], axis=1)
    wfold = np.concatenate([ktiles(m) for m in (a[g2 + "Wq"].T, a[g2 + "Wk"].T, a[g2 + "Wv"].T, a[g2 + "Wo"])], axis=1)
    wgen = np.concatenate([ktiles(wd[:, d * D:(d + 1) * D].T) for d in range(1, LABELS)], axis=1)
    cols = [a[g0 + "b" + n] for n in ("d", "ri", "rh", "zi", "zh", "ni", "nh")]
    for l in range(2):
        cols += [a[g1 + "bq"][l], a[g1 + "bk"][l]]
    cols += [a[g3 + "b" + n] for n in "qkv"] + [a[g0 + "gamma"], a[g0 + "beta"]]
    for l in range(2):
        cols += [a[g1 + "ln_g"][l], a[g1 + "ln_b"][l]]
    cols += [a[g2 + "gamma"], a[g2 + "beta"]]
    bcols = np.concatenate([c.reshape(-1, P).T for c in cols], axis=1)
    rows = [a[g0 + "gamma"], a[g0 + "beta"]]
    for l in range(2):
        rows += [a[g1 + "ln_g"][l], a[g1 + "ln_b"][l]]
    rows += [a[g2 + "gamma"], a[g2 + "beta"], a[g3 + "gamma"], a[g3 + "beta"]]
    rep = np.broadcast_to(np.concatenate(rows)[None, :], (P, len(REP) * D))
    rep_bo = np.broadcast_to(np.concatenate([a[g2 + "bo"], a[g3 + "bo"]])[None, :], (P, 2 * D))

    arrays = {
        "x": a["x"], "xT": a["x"].transpose(0, 2, 1), "adj": a["adj"], "adjT": a["adj"].transpose(0, 2, 1),
        "wraw": wraw, "wfold": wfold, "wgen": wgen, "bcols": bcols, "rep": rep, "rep_bo": rep_bo,
    }
    arrays = {f"in_{k}": np.ascontiguousarray(v) for k, v in arrays.items()}
    nc = bacc.Bacc("TRN2", target_bir_lowering=False, num_devices=1)
    args = [nc.dram_tensor(k, v.shape, mybir.dt.from_np(v.dtype), kind="ExternalInput").ap() for k, v in arrays.items()]
    out = nc.dram_tensor("out", (B, N, D), F32, kind="ExternalOutput").ap()
    build(nc, *args, out)
    r = run(nc, [arrays], core_ids=[0])
    return r.results[0]["out"]
```

```python
from contextlib import ExitStack

import concourse.bass as bass
from concourse import mybir

F32 = mybir.dt.float32
F32R = mybir.dt.float32r
BF16 = mybir.dt.bfloat16
I32 = mybir.dt.int32
ALU = mybir.AluOpType
ACT = mybir.ActivationFunctionType
AX_X = mybir.AxisListType.X

P = 128
B, N, D = 16, 512, 256
F1 = 128
HEADS, HD = 8, 32
LABELS = 4
NT = N // P
DT = D // P
SLOTS = 2
CHAIN = 4
GBANKS, RING = 4, 4
MASKED = 1.0e30
HIGHEST = 3.0e38
CNT_EPS = 1e-8
LN_EPS = 1e-5
SCALE = {"1a": -F1 ** -0.5, "1b": -F1 ** -0.5, "2": -D ** -0.5, "3": -HD ** -0.5}

WIDTH = [("wd1", D), ("ri", D), ("rh", D), ("zi", D), ("zh", D), ("ni", D), ("nh", D),
         ("q1a", F1), ("k1a", F1), ("c1a", D), ("q1b", F1), ("k1b", F1), ("c1b", D),
         ("q3", D), ("k3", D), ("v3", D), ("o3", D)]
COL = {}
RAW = 0
for _name, _width in WIDTH:
    COL[_name] = (RAW, _width)
    RAW += DT * _width
COL["a2"] = (RAW, D)
COL["c2"] = (RAW + DT * D, D)
WCOLS = RAW + 2 * DT * D
GEN = DT * D * (LABELS - 1)

BIAS = ["bd", "bri", "brh", "bzi", "bzh", "bni", "bnh", "bq1a", "bk1a", "bq1b", "bk1b", "bq3", "bk3", "bv3",
        "g0", "b0", "g1a", "b1a", "g1b", "b1b", "g2", "b2", "r", "z", "h"]
BCOL, NB_IN = {}, 0
for _name in BIAS:
    if _name == "r":
        NB_IN_LAST = NB_IN
    BCOL[_name] = NB_IN
    NB_IN += 1 if _name[:3] in ("bq1", "bk1") else DT
NBIAS = NB_IN
NB_IN = NB_IN_LAST
REP = ["g0", "b0", "g1a", "b1a", "g1b", "b1b", "g2", "b2", "g3", "b3"]


LAYERS = ("1a", "1b", "2")
BEFORE = {"1a": "0", "1b": "1a", "2": "1b", "3": "2"}
MM, MM_HALF, TURN = 0.217, 0.119, 0.48

def parts_of(b):
    out = []

    def add(engine, step, us, *needs, lag=0.2):
        out.append((engine, step, us, lag, [n for n in needs if n is not None]))

    def old(engine, step):
        return (engine, step) if b >= SLOTS else None

    def norm(layer):
        add("ACT", ("norm", layer, b), 0.95, ("DVE", ("norm", layer, b)))

    o = b - SLOTS
    used = old("PE", ("ov", o, HEADS - 1, 1))
    add("SP", ("x", b), 2.4, used, lag=2.5)
    add("SP", ("xT", b), 2.4, used, lag=2.5)
    add("Pool", ("lab", b), 1.2, old("PE", ("S", ("3", o, HEADS - 2), NT - 1)), lag=4.0)
    add("Pool", ("adj", b), 1.2, old("DVE", ("S", ("3", o, HEADS - 1), NT - 1)), lag=4.0)
    add("DVE", ("label", b), 1.8, ("Pool", ("lab", b)), used)
    add("PE", ("cnt", b), 4 * MM, ("DVE", ("label", b)))
    add("PE", ("high", b), 4 * MM, ("DVE", ("label", b)))
    add("ACT", ("cnt", b), 0.5, ("PE", ("cnt", b)))
    for n in range(NT):
        add("DVE", ("rc", b, n), 0.85, ("ACT", ("cnt", b)))
    add("DVE", ("high", b), 0.9, ("PE", ("high", b)))
    add("ACT", ("x", b), 0.9, ("SP", ("x", b)))
    add("DVE", ("x", b), 1.1, ("ACT", ("x", b)))
    add("ACT", ("xT", b), 0.9, ("SP", ("xT", b)), ("PE", ("high", b)))
    add("Pool", ("xT", b), 2.4, ("ACT", ("xT", b)))
    for ht in range(DT):
        add("PE", ("agg", b, ht), 8 * MM, ("DVE", ("x", b)), old("PE", ("y", o, 1)))
    for ht in range(DT):
        add("DVE", ("agg", b, ht), 0.6, ("PE", ("agg", b, ht)), old("SP", ("store", o)))
        add("ACT", ("agg", b, ht), 0.5, ("DVE", ("agg", b, ht)))
    add("DVE", ("more", b), 1.4, ("ACT", ("agg", b, 1)))
    add("DVE", ("bias", b), 0.7, ("Pool", ("adj", b)))
    add("PE", ("more", b), 0.0, ("DVE", ("more", b)))
    add("PE", ("wd", b, 0), 5 * MM, ("DVE", ("more", b)))
    add("DVE", ("labels", b), 0.05, ("PE", ("wd", b, 0)), lag=0.0)
    add("PE", ("wd", b, 1), 7 * MM, ("DVE", ("labels", b)))
    for et in range(DT):
        add("ACT", ("wd", b, et), 1.1, ("PE", ("wd", b, 1)))
        add("DVE", ("wd", b, et), 0.6, ("ACT", ("wd", b, et)))
    add("PE", ("hn", b, 0), 6 * MM, ("Pool", ("xT", b)))
    add("PE", ("hn", b, 1), 6 * MM)
    for et in range(DT):
        add("ACT", ("hn", b, et), 0.5, ("PE", ("hn", b, et)))
    for et in range(DT):
        add("PE", ("r", b, et), 12 * MM, ("DVE", ("wd", b, 1)))
        add("PE", ("in", b, et), 6 * MM)
        add("PE", ("z", b, et), 12 * MM)
        add("ACT", ("r", b, et), 0.5, ("PE", ("r", b, et)))
        add("DVE", ("in", b, et), 1.33, ("PE", ("in", b, et)), ("ACT", ("r", b, et)))
        add("ACT", ("in", b, et), 0.5, ("DVE", ("in", b, et)))
        add("Pool", ("z", b, et), 1.3, ("ACT", ("in", b, et)))
        add("ACT", ("z", b, et), 0.5, ("PE", ("z", b, et)))
        add("DVE", ("z", b, et), 1.33, ("Pool", ("z", b, et)), ("ACT", ("z", b, et)))
    for ip in range(2):
        add("PE", ("lt", b, ip), TURN, ("DVE", ("z", b, 1)))
    add("DVE", ("norm", "0", b), 5.1, ("PE", ("lt", b, 1)), lag=0.0)
    norm("0")

    def transposed(layer):
        for dt in range(DT):
            add("PE", ("xt", layer, b, dt), TURN, ("ACT", ("norm", layer, b)))
        for dt in range(DT):
            add("ACT", ("xt", layer, b, dt), 1.33, ("PE", ("xt", layer, b, dt)))
            add("DVE", ("xt", layer, b, dt), 0.6, ("ACT", ("xt", layer, b, dt)))
        add("Pool", ("affine", layer, b), 4.6, ("PE", ("xt", layer, b, 1)))

    def split(*step):
        add("ACT", step, 0.55, ("PE", step))
        add("DVE", step, 0.63, ("ACT", step))

    def tiles(units, us):
        ts = [(u, it) for u in units for it in range(NT)]
        lag = 3
        for n in range(len(ts) + lag):
            if n < len(ts):
                add("PE", ("S",) + ts[n], us, ("SP", ("stack",) + ts[n][0]) if ts[n][0][0] == "3" else None,
                    ("PE", ("ht", b - 1, 3)) if b and n == NT else None)
                add("DVE", ("S",) + ts[n], 0.6, ("PE", ("S",) + ts[n]))
            if lag <= n < len(ts) + lag:
                u, it = t = ts[n - lag]
                add("PE", ("T",) + t, TURN, ("ACT", ("S",) + t),
                    ("PE", ("ov", b, u[2] - 1, it // 2)) if u[0] == "3" and u[2] else None)
                add("ACT", ("T",) + t, 0.48, ("PE", ("T",) + t),
                    ("PE", ("ov", b, u[2] - 1, it // 2)) if u[0] == "3" and u[2] else None)
                add("DVE", ("T",) + t, 0.6, ("ACT", ("T",) + t))
            if n < len(ts):
                add("ACT", ("S",) + ts[n], 0.71, ("DVE", ("S",) + ts[n]))
            m = n - lag
            if m >= 0 and m % 2 == 1 and units[0][0] == "3":
                u, half = units[m // NT], m % NT // 2
                h = u[2]
                add("PE", ("ov", b, h, half), 8 * MM_HALF, ("DVE", ("T", u, 2 * half + 1)),
                    ("PE", ("ht", b - 1, 3)) if b and h == 0 else None)
                add("ACT", ("ov", b, h, half), 0.35, ("PE", ("ov", b, h, half)),
                    ("PE", ("ht", b, h // 2 - 1)) if h > 1 else ("PE", ("ht", b - 1, 3)) if b else None)
                if half and h % 2:
                    p = h // 2
                    add("PE", ("ht", b, p), TURN, ("ACT", ("ov", b, h, 1)), ("PE", ("hx", b - 1, 1)) if b and p == 0 else None)
                    add("ACT", ("ht", b, p), 0.3, ("PE", ("ht", b, p)), ("DVE", ("ht", b, p - 1)) if p else
                        ("DVE", ("ht", b - 1, 3)) if b else None)
                    add("DVE", ("ht", b, p), 1.2, ("ACT", ("ht", b, p)),
                        ("PE", ("hx", b, 0)) if p == 2 else ("PE", ("hx", b - 1, 1)) if b and not p else None)
                    if p % 2:
                        add("PE", ("hx", b, p // 2), TURN, ("DVE", ("ht", b, p)))
                        split("hx", b, p // 2)

    for layer in LAYERS:
        transposed(BEFORE[layer])
        xt = ("DVE", ("xt", BEFORE[layer], b, 1))
        for c in range(2):
            step = ("k", layer, b, 0) if c and layer != "2" else ("q", layer, b, c)
            add("PE", step, 6 * MM, xt)
            split(*step)
        for jp in range(2):
            step = ("v", layer, b, jp)
            add("PE", step, 12 * MM_HALF, xt)
            split(*step)
        n = len(out)
        tiles([(layer, b, 0)], (6 if layer == "2" else 3) * MM)
        out[n][4].append(("DVE", ("q", "2", b, 1) if layer == "2" else ("k", layer, b, 0)))
        for ip in range(2):
            add("PE", ("pv", layer, b, ip), 24 * MM_HALF, ("DVE", ("T", (layer, b, 0), NT - 1)), ("DVE", ("v", layer, b, 1)))
            add("DVE", ("pv", layer, b, ip), 1.8, ("PE", ("pv", layer, b, ip)), ("Pool", ("affine", BEFORE[layer], b)))
        add("DVE", ("norm", layer, b), 3.3, lag=0.0)
        norm(layer)
    transposed("2")
    xt = ("DVE", ("xt", "2", b, 1))
    order = [("q", "3", b, 0), ("k", "3", b, 0), ("v", "3", b, 0), ("v", "3", b, 1), ("q", "3", b, 1), ("k", "3", b, 1)]
    for n, step in enumerate(order):
        add("PE", step, (12 * MM_HALF if step[0] == "v" else 6 * MM), xt)
    for n, step in enumerate(order):
        add("ACT", step, 0.5, ("PE", step), ("PE", order[-1]) if n >= 4 else None)
        add("DVE", step, 0.63, ("ACT", step))
    for h in range(HEADS):
        user = ("S", ("3", b, h - 2), NT - 1) if h > 1 else ("S", ("3", b - 1, 7), NT - 1) if b and h else None
        add("SP", ("stack", "3", b, h), 3.7, ("DVE", ("k", "3", b, h // 4)), user and ("PE", user), lag=2.3)
    tiles([("3", b, h) for h in range(HEADS)], MM)
    for ip in range(2):
        add("PE", ("y", b, ip), 12 * MM_HALF, ("DVE", ("hx", b, 1)))
        add("DVE", ("y", b, ip), 1.7, ("PE", ("y", b, ip)), ("Pool", ("affine", "2", b)))
    add("DVE", ("norm", "3", b), 3.4, lag=0.0)
    norm("3")
    add("Pool", ("affine", "3", b), 4.6, ("ACT", ("norm", "3", b)))
    add("SP", ("store", b), 0.1, ("Pool", ("affine", "3", b)), lag=3.0)
    return out

def reader(step):
    kind = step[0]
    if kind == "more":
        return []
    if kind == "lt":
        return [("ACT" if step[2] else "DVE", ("norm", "0", step[1]))]
    return [("ACT" if kind in ("cnt", "wd", "xt", "hn", "r", "z", "ov") else "DVE", step)]


def opens(step):
    if step[0] == "more" or step[0] in ("wd", "lt") and step[2] == 0:
        return step[1]
    if step[:2] == ("q", "3") and step[3] == 1:
        return step[2]
    return None


def schedule():
    engines = ("PE", "ACT", "DVE", "Pool", "SP")
    parts, todo, after = {}, {}, {}
    for b in range(CHAIN):
        for part in parts_of(b):
            kind = part[1][0]
            lane = todo.setdefault((part[0], b, kind if kind in ("S", "T") else "main"), [])
            if lane:
                after.setdefault(lane[-1][:2], []).append((part[:2], 0.0))
            lane.append(part)
            parts[part[:2]] = part
    for part in parts.values():
        for need in part[4]:
            after.setdefault(need, []).append((part[:2], parts[need][3]))
    rest = {}

    def way(p):
        todo_ = [p]
        while todo_:
            q = todo_[-1]
            open_ = [n for n, _ in after.get(q, []) if n not in rest]
            if q in rest or not open_:
                rest[q] = parts[q][2] + max([lag + rest[n] for n, lag in after.get(q, [])] + [0.0])
                todo_.pop()
            else:
                todo_ += open_
        return rest[p]

    free, order, end = dict.fromkeys(engines, 0.0), {e: [] for e in engines}, {}
    at = dict.fromkeys(todo, 0)
    groups, scores, turned, taken, meeting = [], [], [], 0, None
    for _ in range(len(parts)):
        best = None
        for k, lane in todo.items():
            if at[k] == len(lane):
                continue
            e, b, _ = k
            _, step, us, lag, needs = lane[at[k]]
            needs = list(needs)
            if step[0] == "labels" and groups:
                needs += reader(groups[-GBANKS])
            if e == "PE":
                if meeting is not None and step != ("wd", meeting, 1):
                    continue
                if order[e] and groups and order[e][-1] == groups[-1] and opens(groups[-1]) not in (None, b):
                    continue
                if step[0] == "S":
                    needs += [("DVE", p) for p in scores[-2:-1]]
                elif step[0] == "T":
                    needs += [("DVE", p) for p in turned[-2:-1]]
                elif len(groups) >= GBANKS:
                    needs += reader(groups[-GBANKS])
            if e == "DVE" and step[0] == "S":
                if taken == len(scores) or scores[taken] != step:
                    continue
                if taken >= RING:
                    needs.append(("PE", ("T",) + scores[taken - RING][1:]))
            if any(p not in end for p in needs):
                continue
            start = max([free[e]] + [end[p] for p in needs])
            key = (start, -way((e, step)) - urgency(e, step))
            if best is None or key < best[0]:
                best = (key, k, step, us, lag)
        (start, _), k, step, us, lag = best
        e = k[0]
        free[e] = start + us
        end[e, step] = start + us + lag
        at[k] += 1
        order[e].append(step)
        if e == "PE":
            (scores if step[0] == "S" else turned if step[0] == "T" else groups).append(step)
        taken += e == "DVE" and step[0] == "S"
        if step[0] == "labels":
            meeting = step[1]
        elif step[0] == "wd" and e == "PE" and step[2] == 1:
            meeting = None
    return order, groups


FRONT_FIRST = {
    "PE": {"T": 80, "hn": 40, "in": 20, "r": -20, "v": -20, "xt": 40},
    "ACT": {"S": -20, "v": -10},
    "DVE": {"T": 80, "high": 10, "more": 20, "norm": -10, "q": 80, "rc": -40, "x": -20, "xt": 10},
    "Pool": {"lab": 80},
}
HEADS_FIRST = {
    "PE": {"S": 10, "T": 80, "ht": 80, "ov": 40},
    "ACT": {"S": -20, "ht": -20, "k": 40},
    "DVE": {"ht": 10, "y": -10},
}


def urgency(e, step):
    kind = step[0]
    heads = kind in ("ov", "ht", "hx", "y") or (step[1][0] if kind in ("S", "T") else step[1]) == "3"
    return (HEADS_FIRST if heads else FRONT_FIRST).get(e, {}).get(kind, 0)


ORDER, GROUPS = schedule()
SPLIT = ("agg", "wd", "xt", "q", "k", "v", "hx")
NUMBER = {k: n for n, k in enumerate(GROUPS)}


def steps(engine, *kinds):
    return [k for k in ORDER[engine] if k[0] in kinds]


class Signal:

    def __init__(self, sem, keys):
        self.sem = sem
        self.where = {k: n + 1 for n, k in enumerate(keys)}
        assert len(self.where) == len(keys)

    def at(self, key):
        return self.where[key]


def terms3(lh, ll, rh, rl):
    return [(lh, rl), (ll, rh), (lh, rh)]


def build(nc, x, xT, adj, adjT, wraw, wfold, wgen, bcols, rep, rep_bo, out):
    ctx = ExitStack()
    with ctx:
        at = [nc.sbuf_base + 63 & ~63]

        def sb(name, shape, dt, where=None):
            size = mybir.dt.size(dt)
            for n in shape[1:]:
                size *= n
            if where is None:
                where = at[0]
                at[0] += (size + 63) & ~63
            return nc.alloc_sbuf_tensor_at(name, shape, dt, offset=where), where

        def new(name, shape, dt):
            return sb(name, shape, dt)[0]

        wh = new("weights_high", [P, WCOLS], F32R)
        wl = new("weights_low", [P, WCOLS], F32R)
        wg = new("weights_labels", [P, GEN], F32)
        rp = new("rows_replicated", [P, len(REP) * D], F32)
        bc = new("bias_columns", [P, NBIAS], F32)
        ident = new("identity", [P, P], F32)
        ones = new("ones", [P, P], F32R)
        ones_b = new("ones_bf16", [P, P], BF16)

        probs = new("probs", [P, RING, N], F32)

        mbias, labT, xi, vh, vl, xTh, xTl, qh, ql, pth, ptl = ([] for _ in range(11))
        xf, lab_ats, above, more, xraw = ([] for _ in range(5))
        xh, xl, outh, outl, xTf, tA, tB, tC, mask, rc, flt = ([] for _ in range(11))
        v3t, q_at = [], []
        for s in range(SLOTS):
            t, _ = sb(f"mask_bias{s}", [P, NT, N], BF16)
            mbias.append(t)
            t, lab_at = sb(f"labels_T{s}", [P, NT, N], BF16)
            labT.append(t)
            t, xi_at = sb(f"x_nodes{s}", [P, NT, D], F32)
            xi.append(t)
            t, v_at = sb(f"v_high{s}", [P, NT, D], F32R)
            vh.append(t)
            t, vl_at = sb(f"v_low{s}", [P, NT, D], F32R)
            vl.append(t)
            t, xt_at = sb(f"xT_high{s}", [P, DT, N], F32R)
            xTh.append(t)
            xTl.append(sb(f"xT_low{s}", [P, DT, N], F32R)[0])
            t, qa = sb(f"q_high{s}", [P, DT, N], F32R)
            qh.append(t)
            ql.append(sb(f"q_low{s}", [P, DT, N], F32R)[0])
            q_at.append(qa)
            t, pt_at = sb(f"probsT_high{s}", [P, NT, N], F32R)
            pth.append(t)
            ptl.append(sb(f"probsT_low{s}", [P, NT, N], F32R)[0])
            kb = 1024
            xh.append(sb(f"x_high{s}", [P, NT, D], F32R, v_at)[0])
            xl.append(sb(f"x_low{s}", [P, NT, D], F32R, vl_at)[0])
            outh.append(sb(f"msg_high{s}", [P, DT, N], F32R, qa)[0])
            outl.append(sb(f"msg_low{s}", [P, DT, N], F32R, qa + 4 * kb)[0])
            above.append(sb(f"label_above_1_{s}", [P, NT, N], BF16, xt_at)[0])
            xraw.append(sb(f"x_unsplit{s}", [P, NT, D], F32, vl_at)[0])
            more.append(sb(f"more_messages{s}", [P, DT, N], F32, xi_at)[0])
            flt.append(sb(f"unsplit{s}", [P, DT, N], F32, xi_at)[0])
            xTf.append(sb(f"x_features{s}", [P, DT, N], F32, pt_at)[0])
            tA.append(sb(f"gate_r{s}", [P, DT, N], F32, pt_at + 4 * kb)[0])
            tB.append(sb(f"cand{s}", [P, DT, N], F32, pt_at + 8 * kb)[0])
            tC.append(sb(f"gate_z{s}", [P, DT, N], F32, pt_at + 12 * kb)[0])
            mask.append(sb(f"label_mask{s}", [P, NT, N], F32R, pt_at + 4 * kb)[0])
            rc.append(sb(f"one_over_count{s}", [P, N], F32, pt_at + 12 * kb)[0])
            v3t.append(sb(f"v3_{s}", [P, NT, HEADS, 2, HD], F32R, v_at)[0])
            lab_ats.append(lab_at)
            xf.append(sb(f"xT_unsplit{s}", [P, DT, N], F32, pt_at)[0])
        spare = at[0]
        at[0] += 4 * kb
        stq = [sb(f"stack_q{n}", [P, N], F32R, w)[0] for n, w in enumerate(lab_ats + [spare])]
        stk = [sb(f"stack_k{n}", [P, N], F32R, w + 2 * kb)[0] for n, w in enumerate(lab_ats + [spare])]
        ovs = new("pair_T", [P, N], F32)
        hn_i = new("heads_nodes", [P, NT, P], F32)
        hlo = new("pair_low", [P, NT, 2, HD], F32)

        nmax = new("negated_row_max", [P, SLOTS * NT], F32)
        rsum = new("row_sum", [P, SLOTS, HEADS, NT], F32)
        rinv = new("row_inverse", [P, SLOTS, HEADS, NT], F32)
        nan_ = new("nan_without_edge", [P, SLOTS, NT], F32)
        flag = new("row_has_edge", [P, SLOTS, NT], F32)
        stats = new("ln_stats", [P, SLOTS, NT, 6], F32)
        mv = new("ln_mean_var", [P, SLOTS, NT, 2], F32)
        var = new("ln_var", [P, SLOTS, NT], F32)
        rstd = new("ln_rstd", [P, SLOTS, NT], F32)
        nt_ = new("ln_newton", [P, SLOTS, NT], F32)
        shift = new("ln_shift", [P, SLOTS, NT], F32)
        std = new("ln_std", [P, SLOTS, NT], F32)
        n_above = new("n_above", [1, SLOTS], F32)
        take_more = new("take_more", [1, SLOTS], I32)
        assert at[0] <= nc.sbuf_usable_end, (at[0], nc.sbuf_usable_end)
        raw = sb("weights_raw", [P, RAW], F32, (q_at[0] - 28 * kb))[0]
        fold_at = q_at[0] - 28 * kb + RAW * 4
        foldr = sb("fold_raw", [P, 4, DT, D], F32, fold_at)[0]
        foldh = sb("fold_high", [P, 4, DT, D], F32R, fold_at + 8 * kb)[0]
        foldl = sb("fold_low", [P, 4, DT, D], F32R, fold_at + 16 * kb)[0]
        bo_rows = sb("bo_rows", [P, 2, D], F32, fold_at + 24 * kb)[0]

        psS = ctx.enter_context(nc.psum_tensor("scores_bank", [P, 2, 512], F32))
        psT = ctx.enter_context(nc.psum_tensor("transposed_bank", [P, 2, 512], F32))
        psG = ctx.enter_context(nc.psum_tensor("group_bank", [P, GBANKS, 512], F32))

        def W(name, kt, lo=0, hi=None):
            off, width = COL[name]
            hi = width if hi is None else hi
            a, b = off + kt * width + lo, off + kt * width + hi
            return wh[:, a:b], wl[:, a:b]

        def bias(name, c=0):
            return bc[:, BCOL[name] + c:BCOL[name] + c + 1]

        def row(name):
            n = REP.index(name)
            return rp[:, n * D:(n + 1) * D]

        def f32(ap):
            return ap.bitcast(F32)

        def sem(name):
            return ctx.enter_context(nc.semaphore(name))

        w_in, f_in, c_in, id0, id1 = sem("w_in"), sem("f_in"), sem("c_in"), sem("id0"), sem("id1")
        w_hi, w_lo, f_hi, f_lo, fold_mm, fold_hi, fold_lo, b_done = (sem(n) for n in (
            "w_hi", "w_lo", "f_hi", "f_lo", "fold_mm", "fold_hi", "fold_lo", "b_done"))
        r_done, q_scaled = sem("r_done"), sem("q_scaled")
        SCALED = [("q1a", "1a"), ("q1b", "1b"), ("q3", "3")]

        def fold_scale(g):
            return SCALE["2"] if g < DT else 1.0

        CH = 1024
        chunks = [(a, min(a + CH, RAW)) for a in range(0, RAW, CH)]
        with nc.Block() as block:
            @block.sync
            def _(sp):
                sp.dma_start(foldr[:].rearrange("p a b c -> p (a b c)"), wfold).then_inc(f_in, 16)
                sp.dma_start(raw[:], wraw).then_inc(w_in, 16)
                sp.dma_start(wg[:], wgen).then_inc(c_in, 16)
                sp.dma_start(rp[:], rep).then_inc(c_in, 16)
                sp.dma_start(bc[:, 0:NB_IN], bcols).then_inc(c_in, 16)
                sp.dma_start(bo_rows[:].rearrange("p a d -> p (a d)"), rep_bo).then_inc(c_in, 16)
                sp.wait_ge(c_in, 64)

            @block.gpsimd
            def _(pool):
                nc.gpsimd.memset(ident[:], 0.0).then_inc(id0, 1)
                pool.wait_ge(id0, 1)
                nc.gpsimd.affine_select(out=ident[:], in_=ident[:], compare_op=ALU.not_equal, fill=1.0, base=0,
                                        pattern=[[-1, P]], channel_multiplier=1).then_inc(id0, 1)
                nc.gpsimd.memset(f32(ones[:]), 1.0).then_inc(id1, 1)
                nc.gpsimd.memset(ones_b[:], 1.0).then_inc(id1, 1)

            @block.scalar
            def _(act):
                act.wait_ge(f_in, 16)
                nc.scalar.copy(foldh[:], foldr[:]).then_inc(f_hi, 1)
                act.wait_ge(q_scaled, len(SCALED))
                for a, b in chunks:
                    nc.scalar.copy(wh[:, a:b], raw[:, a:b]).then_inc(w_hi, 1)
                for g in range(4):
                    act.wait_ge(fold_mm, g + 1)
                    a = RAW + g * D
                    nc.scalar.activation(wh[:, a:a + D], psG[:, g, 0:D], ACT.Copy, scale=fold_scale(g)).then_inc(fold_hi, 1)

            @block.vector
            def _(dve):
                dve.wait_ge(w_in, 16)
                for name, layer in SCALED:
                    a = COL[name][0]
                    cols = raw[:, a:a + DT * COL[name][1]]
                    nc.vector.tensor_scalar_mul(cols, cols, SCALE[layer]).then_inc(q_scaled, 1)
                dve.wait_ge(f_hi, 1)
                nc.vector.tensor_sub(foldl[:], foldr[:], f32(foldh[:])).then_inc(f_lo, 1)
                for n, (a, b) in enumerate(chunks):
                    dve.wait_ge(w_hi, n + 1)
                    nc.vector.tensor_sub(wl[:, a:b], raw[:, a:b], f32(wh[:, a:b])).then_inc(w_lo, 1)
                for g in range(4):
                    dve.wait_ge(fold_hi, g + 1)
                    a = RAW + g * D
                    nc.vector.scalar_tensor_tensor(out=wl[:, a:a + D], in0=psG[:, g, 0:D], scalar=fold_scale(g),
                                                   in1=f32(wh[:, a:a + D]), op0=ALU.mult, op1=ALU.subtract).then_inc(fold_lo, 1)
                dve.wait_ge(c_in, 64)
                for n, beta in enumerate(("b1b", "b2")):
                    nc.vector.tensor_add(row(beta), row(beta), bo_rows[:, n, :]).then_inc(r_done, 1)
                for name, layer in SCALED:
                    cols = bc[:, BCOL["b" + name]:BCOL["b" + name] + (DT if layer == "3" else 1)]
                    nc.vector.tensor_scalar_mul(cols, cols, SCALE[layer]).then_inc(r_done, 1)
                n = 0
                for to, parts in (("r", ("bri", "brh")), ("z", ("bzi", "bzh"))):
                    c, a, b = BCOL[to], BCOL[parts[0]], BCOL[parts[1]]
                    nc.vector.tensor_add(bc[:, c:c + DT], bc[:, a:a + DT], bc[:, b:b + DT]).then_inc(b_done, 1)
                    n += 1
                    dve.wait_ge(b_done, n)
                    nc.vector.tensor_scalar_mul(bc[:, c:c + DT], bc[:, c:c + DT], 0.5).then_inc(b_done, 1)
                    n += 1
                c, a = BCOL["h"], BCOL["bnh"]
                nc.vector.tensor_scalar_mul(bc[:, c:c + DT], bc[:, a:a + DT], 0.5).then_inc(b_done, 1)

            @block.tensor
            def _(pe):
                pe.wait_ge(f_lo, 1)
                for g in range(4):
                    left, right = (0, 1) if g < 2 else (2, 3)
                    c = slice((g % 2) * P, (g % 2) * P + P)
                    terms = []
                    for kt in range(DT):
                        terms += terms3(foldh[:, left, kt, c], foldl[:, left, kt, c],
                                        foldh[:, right, kt, :], foldl[:, right, kt, :])
                    for n, (a, b) in enumerate(terms):
                        mm = nc.tensor.matmul(psG[:, g, 0:D], a, b, start=(n == 0), stop=(n == len(terms) - 1))
                    mm.then_inc(fold_mm, 1)

        def signal(name, keys):
            return Signal(sem(name), list(keys))

        adj_in = [sem(f"adj_in{s}") for s in range(SLOTS)]
        lab_in = [sem(f"lab_in{s}") for s in range(SLOTS)]
        x_in = [sem(f"x_in{s}") for s in range(SLOTS)]
        xT_in = [sem(f"xT_in{s}") for s in range(SLOTS)]
        stack_in = [sem(f"stack_in{r}") for r in range(SLOTS + 1)]
        g_ready = signal("g_ready", [k for k in GROUPS if k[0] != "more"])
        s_ready = signal("s_ready", steps("PE", "S"))
        t_ready = signal("t_ready", steps("PE", "T"))
        x_hi = signal("x_hi", steps("ACT", "x", "xT"))
        hi = signal("hi", steps("ACT", *SPLIT))
        whole = signal("whole", steps("ACT", "wd", "xt"))
        act_gru = signal("act_gru", steps("ACT", "hn", "r", "in", "z"))
        normed2 = signal("normed2", [k + (it,) for k in steps("ACT", "norm") for it in range(NT // 2, NT)])
        p_ready = signal("p_ready", steps("ACT", "S"))
        pt_hi = signal("pt_hi", steps("ACT", "T"))
        ov_out = signal("ov_out", steps("ACT", "ov"))
        h_lo = signal("h_lo", steps("ACT", "ht"))
        x_lo = signal("x_lo", steps("DVE", "x"))
        labelled = signal("labelled", steps("DVE", "label"))
        compared = signal("compared", steps("DVE", "label"))
        told = signal("told", steps("DVE", "high"))
        cnt_read = signal("cnt_read", steps("ACT", "cnt"))
        rcs = signal("rcs", steps("DVE", "rc"))
        full = signal("full", steps("DVE", "agg"))
        lo = signal("lo", [j for k in steps("DVE", "more", *SPLIT) if k[0] != "agg" for j in
                           ([("agg", k[1], ht) for ht in range(DT)] if k[0] == "more" else [k])])
        biased = signal("biased", steps("DVE", "bias"))
        dve_gru = signal("dve_gru", [k + (w,) for k in steps("DVE", "in", "z") for w in
                                     (("v", "w") if k[0] == "in" else ("e", "o"))])
        s_taken = signal("s_taken", steps("DVE", "S"))
        pt_lo = signal("pt_lo", steps("DVE", "T"))
        y_done = signal("y_done", steps("DVE", "pv", "y"))
        scaled = signal("scaled", steps("DVE", "norm"))
        normed = signal("normed", [k + (it,) for k in steps("DVE", "norm") for it in range(NT // 2)])
        h_done = signal("h_done", steps("DVE", "ht"))
        xT_lo = signal("xT_lo", steps("Pool", "xT"))
        pool_d = signal("pool_d", steps("Pool", "z"))
        affine = signal("affine", [k + (w,) for k in steps("Pool", "affine") for w in ("scaled", "shifted")])
        more_mask = [sem(f"more_mask{b}") for b in range(CHAIN)]
        more_sum = [sem(f"more_sum{b}") for b in range(CHAIN)]
        more_full = [sem(f"more_full{b}") for b in range(CHAIN)]
        more_used = [sem(f"more_used{b}") for b in range(CHAIN)]
        chain = sem("dve_chain")
        stored = [sem(f"stored{s}") for s in range(SLOTS)]
        sem_first, sem_last = x_in[0].num, stored[-1].num
        TURNS = CHAIN // SLOTS
        LAST = HEADS - 1

        def slot(b):
            return b % SLOTS

        def uses(b):
            return b // SLOTS + 1

        def stack_of(b, h):
            return slot(b) if h % 2 == 0 else SLOTS

        def stacked(b, h):
            users = [k for k in steps("SP", "stack") if stack_of(k[2], k[3]) == stack_of(b, h)]
            return (users.index(("stack", "3", b, h)) + 1) * 6 * 16

        def gbank(k):
            return psG[:, NUMBER[k] % GBANKS, :]

        def parts(k):
            kind = k[0]
            if kind in ("agg", "hx"):
                s = slot(k[1])
                return qh[s][:, k[2], :], ql[s][:, k[2], :]
            if kind == "wd":
                s = slot(k[1])
                return outh[s][:, k[2], :], outl[s][:, k[2], :]
            _, layer, b, c = k
            s = slot(b)
            if kind == "xt":
                return xTh[s][:, c, :], xTl[s][:, c, :]
            if kind in ("q", "k") and layer == "3":
                n = 0 if kind == "q" else 1
                return (xTh[s][:, n, :], xTl[s][:, n, :]) if c else (qh[s][:, n, :], ql[s][:, n, :])
            if kind == "q":
                return qh[s][:, c, :], ql[s][:, c, :]
            if kind == "k":
                return qh[s][:, 1, :], ql[s][:, 1, :]
            if layer == "3":
                return v3t[s][:, 2 * c:2 * c + 2, :, 0, :], v3t[s][:, 2 * c:2 * c + 2, :, 1, :]
            return vh[s][:, 2 * c:2 * c + 2, :], vl[s][:, 2 * c:2 * c + 2, :]

        def view(k, ap):
            if k[0] == "v":
                if k[1] == "3":
                    return ap.rearrange("p (j h d) -> p j h d", j=2, h=HEADS)
                return ap.rearrange("p (j d) -> p j d", j=2)
            return ap

        split_bias = {("q", "1a"): "bq1a", ("q", "1b"): "bq1b", ("k", "1a"): "bk1a", ("k", "1b"): "bk1b",
                      ("q", "3"): "bq3", ("k", "3"): "bk3"}

        def column(k):
            if k[0] == "hx":
                return bias("bv3", k[2])
            if k[0] in ("q", "k") and (k[0], k[1]) in split_bias:
                return bias(split_bias[k[0], k[1]], k[3])
            return None

        def combined(b, it):
            return gbank(("lt", b, it // 2))[:, (it % 2) * D:(it % 2 + 1) * D]

        def pair(ap, w):
            return ap.rearrange("p (t h w d) -> p t h w d", h=2, w=2, d=HD)[:, :, :, w, :]

        tiles = {k[1:]: n for n, k in enumerate(steps("PE", "S"))}

        def ring(k):
            return probs[:, tiles[k[1:]] % RING, :]

        def turned(k):
            return psT[:, t_ready.at(k) % 2, :]

        def shift_col(k):
            c = slot(k[1][1]) * NT + k[2]
            return slice(c, c + 1)

        with nc.Fori(0, B // CHAIN) as i:
            with nc.Block() as block:
                @block.sync
                def _(sp):
                    for k in ORDER["SP"]:
                        kind = k[0]
                        if kind in ("x", "xT", "store"):
                            b = k[1]
                            s = slot(b)
                            g = i * CHAIN + b
                        if kind == "x":
                            if b >= SLOTS:
                                sp.wait_ge(g_ready.sem, g_ready.at(("ov", b - SLOTS, LAST, 1)))
                            sp.dma_start(xraw[s][:], x[g].rearrange("(t p) d -> p t d", p=P)).then_inc(x_in[s], 16)
                        elif kind == "xT":
                            if b >= SLOTS:
                                sp.wait_ge(g_ready.sem, g_ready.at(("ov", b - SLOTS, LAST, 1)))
                            sp.dma_start(xTf[s][:], xT[g].rearrange("(t p) n -> p t n", p=P)).then_inc(xT_in[s], 16)
                        elif kind == "stack":
                            _, _, b, h = k
                            s, n = slot(b), stack_of(b, h)
                            c, r = h // 4, slice(HD * (h % 4), HD * (h % 4) + HD)
                            sp.wait_ge(lo.sem, lo.at(("k", "3", b, c)))
                            if h > 1:
                                sp.wait_ge(s_ready.sem, s_ready.at(("S", ("3", b, h - 2), NT - 1)))
                            elif h and b:
                                sp.wait_ge(s_ready.sem, s_ready.at(("S", ("3", b - 1, LAST), NT - 1)))
                            q, key = parts(("q", "3", b, c)), parts(("k", "3", b, c))
                            for to, blocks in ((stq, (q[1], q[0], q[0])), (stk, (key[0], key[1], key[0]))):
                                for j, src in enumerate(blocks):
                                    sp.dma_start(f32(to[n][HD * j:HD * j + HD, :]), f32(src[r, :])).then_inc(stack_in[n], 16)
                        elif kind == "store":
                            sp.wait_ge(affine.sem, affine.at(("affine", "3", b, "shifted")))
                            sp.dma_start(out[g].rearrange("(t p) d -> p t d", p=P), xi[s][:]).then_inc(stored[s], 16)
                    for s in range(SLOTS):
                        sp.wait_ge(stored[s], 16 * TURNS)

                @block.gpsimd
                def _(pool):
                    for k in ORDER["Pool"]:
                        kind = k[0]
                        if kind == "lab":
                            b = k[1]
                            if b >= SLOTS:
                                pool.wait_ge(s_ready.sem, s_ready.at(("S", ("3", b - SLOTS, LAST - 1), NT - 1)))
                            nc.gpsimd.dma_start(labT[slot(b)][:], adjT[i * CHAIN + b].rearrange("(t p) n -> p t n", p=P))\
                                .then_inc(lab_in[slot(b)], 16)
                        elif kind == "adj":
                            b = k[1]
                            if b >= SLOTS:
                                pool.wait_ge(s_taken.sem, s_taken.at(("S", ("3", b - SLOTS, LAST), NT - 1)))
                            nc.gpsimd.dma_start(mbias[slot(b)][:], adj[i * CHAIN + b].rearrange("(t p) n -> p t n", p=P))\
                                .then_inc(adj_in[slot(b)], 16)
                        elif kind == "xT":
                            s = slot(k[1])
                            pool.wait_ge(x_hi.sem, x_hi.at(k))
                            nc.gpsimd.tensor_sub(xTl[s][:], xTf[s][:], f32(xTh[s][:])).then_inc(xT_lo.sem, 1)
                        elif kind == "z":
                            _, b, et = k
                            s = slot(b)
                            pool.wait_ge(act_gru.sem, act_gru.at(("in", b, et)))
                            nc.gpsimd.tensor_sub(tA[s][:, et, :], xTf[s][:, et, :], tB[s][:, et, :]).then_inc(pool_d.sem, 1)
                        elif kind == "affine":
                            _, layer, b = k
                            s = slot(b)
                            if layer == "3":
                                pool.wait_ge(normed.sem, normed.at(("norm", "3", b, NT // 2 - 1)))
                                pool.wait_ge(normed2.sem, normed2.at(("norm", "3", b, NT - 1)))
                            else:
                                pool.wait_ge(g_ready.sem, g_ready.at(("xt", layer, b, DT - 1)))
                            g, beta = (row(w + layer).unsqueeze(1).to_broadcast([P, NT, D]) for w in "gb")
                            nc.gpsimd.tensor_mul(xi[s][:], xi[s][:], g).then_inc(affine.sem, 1)
                            pool.wait_ge(affine.sem, affine.at(k + ("scaled",)))
                            nc.gpsimd.tensor_add(xi[s][:], xi[s][:], beta).then_inc(affine.sem, 1)

                @block.scalar
                def _(act):
                    for k in ORDER["ACT"]:
                        kind = k[0]
                        if kind == "x":
                            b = k[1]
                            act.wait_ge(x_in[slot(b)], 16 * uses(b))
                            nc.scalar.copy(xh[slot(b)][:], xraw[slot(b)][:]).then_inc(x_hi.sem, 1)
                        elif kind == "xT":
                            b = k[1]
                            act.wait_ge(xT_in[slot(b)], 16 * uses(b))
                            act.wait_ge(g_ready.sem, g_ready.at(("high", b)))
                            nc.scalar.copy(xTh[slot(b)][:], xTf[slot(b)][:]).then_inc(x_hi.sem, 1)
                        elif kind == "cnt":
                            act.wait_ge(g_ready.sem, g_ready.at(k))
                            nc.scalar.activation(rc[slot(k[1])][:], gbank(k), ACT.Copy, bias=CNT_EPS).then_inc(cnt_read.sem, 1)
                        elif kind == "agg":
                            act.wait_ge(full.sem, full.at(k))
                            nc.scalar.copy(parts(k)[0], flt[slot(k[1])][:, k[2], :]).then_inc(hi.sem, 1)
                        elif kind == "wd":
                            _, b, et = k
                            act.wait_ge(g_ready.sem, g_ready.at(("wd", b, DT - 1)))
                            nc.scalar.activation(parts(k)[0], gbank(k), ACT.Relu, bias=bias("bd", et)).then_inc(hi.sem, 1)
                            nc.scalar.activation(flt[slot(b)][:, et, :], gbank(k), ACT.Relu, bias=bias("bd", et))\
                                .then_inc(whole.sem, 1)
                        elif kind == "xt":
                            _, layer, b, dt = k
                            act.wait_ge(g_ready.sem, g_ready.at(k))
                            g, beta = bias("g" + layer, dt), bias("b" + layer, dt)
                            nc.scalar.activation(parts(k)[0], gbank(k), ACT.Identity, bias=beta, scale=g).then_inc(hi.sem, 1)
                            nc.scalar.activation(xf[slot(b)][:, dt, :], gbank(k), ACT.Identity, bias=beta, scale=g)\
                                .then_inc(whole.sem, 1)
                        elif kind in ("hn", "r", "z"):
                            _, b, et = k
                            act.wait_ge(g_ready.sem, g_ready.at(k))
                            to, fn, col = {"hn": (tB, ACT.Identity, "h"), "r": (tA, ACT.Tanh, "r"), "z": (tC, ACT.Tanh, "z")}[kind]
                            nc.scalar.activation(to[slot(b)][:, et, :], gbank(k), fn, bias=bias(col, et), scale=0.5)\
                                .then_inc(act_gru.sem, 1)
                        elif kind == "in":
                            _, b, et = k
                            act.wait_ge(dve_gru.sem, dve_gru.at(k + ("w",)))
                            c = tB[slot(b)][:, et, :]
                            nc.scalar.activation(c, c, ACT.Tanh, bias=bias("bni", et)).then_inc(act_gru.sem, 1)
                        elif kind == "norm":
                            _, layer, b = k
                            s = slot(b)
                            act.wait_ge(scaled.sem, scaled.at(k))
                            for it in range(NT // 2, NT):
                                src = combined(b, it) if layer == "0" else xi[s][:, it, :]
                                nc.scalar.activation(xi[s][:, it, :], src, ACT.Identity, bias=shift[:, s, it:it + 1],
                                                     scale=rstd[:, s, it:it + 1]).then_inc(normed2.sem, 1)
                        elif kind in ("q", "k", "v", "hx"):
                            act.wait_ge(g_ready.sem, g_ready.at(k))
                            if k[1] == "3" and k[0] != "v" and k[3]:
                                act.wait_ge(g_ready.sem, g_ready.at(("k", "3", k[2], 1)))
                            high, col = parts(k)[0], column(k)
                            if col is None:
                                a = nc.scalar.copy(high, view(k, gbank(k)))
                            else:
                                a = nc.scalar.activation(high, gbank(k), ACT.Identity, bias=col)
                            a.then_inc(hi.sem, 1)
                        elif kind == "S":
                            _, u, it = k
                            act.wait_ge(s_taken.sem, s_taken.at(k))
                            nc.scalar.activation(ring(k), ring(k), ACT.Exp, bias=nmax[:, shift_col(k)], scale=-1.0,
                                                 accum_out=rsum[:, slot(u[1]), u[2], it:it + 1]).then_inc(p_ready.sem, 1)
                        elif kind == "T":
                            _, u, it = k
                            act.wait_ge(t_ready.sem, t_ready.at(k))
                            if u[2]:
                                act.wait_ge(g_ready.sem, g_ready.at(("ov", u[1], u[2] - 1, it // 2)))
                            nc.scalar.copy(pth[slot(u[1])][:, :, it * P:(it + 1) * P],
                                           turned(k).rearrange("p (j i) -> p j i", j=NT)).then_inc(pt_hi.sem, 1)
                        elif kind == "ov":
                            _, b, h, half = k
                            rows = slice((h % 2) * 64, (h % 2) * 64 + 64)
                            act.wait_ge(g_ready.sem, g_ready.at(k))
                            if h > 1:
                                act.wait_ge(g_ready.sem, g_ready.at(("ht", b, h // 2 - 1)))
                            elif b:
                                act.wait_ge(g_ready.sem, g_ready.at(("ht", b - 1, HEADS // 2 - 1)))
                            nc.scalar.copy(ovs[rows, half * D:(half + 1) * D], gbank(k)[rows, 0:D]).then_inc(ov_out.sem, 1)
                        elif kind == "ht":
                            _, b, p = k
                            act.wait_ge(g_ready.sem, g_ready.at(k))
                            if p:
                                act.wait_ge(h_done.sem, h_done.at(("ht", b, p - 1)))
                            elif b:
                                act.wait_ge(h_done.sem, h_done.at(("ht", b - 1, HEADS // 2 - 1)))
                            nc.scalar.copy(hlo[:], pair(gbank(k), 1)).then_inc(h_lo.sem, 1)

                @block.vector
                def _(dve):
                    links = [0]

                    def link(ins):
                        links[0] += 1
                        ins.then_inc(chain, 1)
                        dve.wait_ge(chain, links[0])

                    def mark(ins):
                        links[0] += 1
                        ins.then_inc(chain, 1)
                        return links[0]

                    def moments(s, it, src):
                        mark(nc.vector.bn_stats(stats[:, s, it, :], src))

                    def summed(k, b, ip, scale):
                        s = slot(b)
                        for j, it in enumerate((2 * ip, 2 * ip + 1)):
                            a = nc.vector.scalar_tensor_tensor(out=xi[s][:, it, :], in0=gbank(k)[:, j * D:(j + 1) * D],
                                                               scalar=scale[:, it:it + 1], in1=xi[s][:, it, :],
                                                               op0=ALU.mult, op1=ALU.add)
                            if j == 0:
                                first = mark(a)
                        a.then_inc(y_done.sem, 1)
                        dve.wait_ge(chain, first)
                        moments(s, 2 * ip, xi[s][:, 2 * ip, :])
                        dve.wait_ge(y_done.sem, y_done.at(k))
                        moments(s, 2 * ip + 1, xi[s][:, 2 * ip + 1, :])

                    def layer_norm(s, src):
                        dve.wait_ge(chain, links[0])
                        for it in range(NT):
                            st = nc.vector.bn_aggr(mv[:, s, it, :], stats[:, s, it, :])
                        link(st)
                        v, y, t, g = var[:, s, :], rstd[:, s, :], nt_[:, s, :], std[:, s, :]
                        link(nc.vector.tensor_scalar_add(v, mv[:, s, :, 1], LN_EPS))
                        link(nc.vector.tensor_single_scalar(t.bitcast(I32), v.bitcast(I32), 1, ALU.logical_shift_right))
                        link(nc.vector.tensor_scalar(y.bitcast(I32), t.bitcast(I32), -1.0, float(0x5F3759DF), ALU.mult, ALU.add))
                        link(nc.vector.tensor_mul(g, v, y))
                        for step in range(3):
                            link(nc.vector.scalar_tensor_tensor(out=t, in0=g, scalar=-0.5, in1=y, op0=ALU.mult, op1=ALU.mult))
                            if step < 2:
                                nc.vector.scalar_tensor_tensor(out=g, in0=t, scalar=1.5, in1=g, op0=ALU.add, op1=ALU.mult)
                            link(nc.vector.scalar_tensor_tensor(out=y, in0=t, scalar=1.5, in1=y, op0=ALU.add, op1=ALU.mult))
                        nc.vector.scalar_tensor_tensor(out=shift[:, s, :], in0=mv[:, s, :, 0], scalar=-1.0, in1=y,
                                                       op0=ALU.mult, op1=ALU.mult).then_inc(scaled.sem, 1)
                        for it in range(NT // 2):
                            nc.vector.tensor_scalar(xi[s][:, it, :], src(it), mv[:, s, it, 0:1], y[:, it:it + 1],
                                                    ALU.subtract, ALU.mult).then_inc(normed.sem, 1)

                    def more_labels(b):
                        s, bank = slot(b), gbank(("more", b))
                        for n in range(LABELS - 1):
                            nc.vector.tensor_scalar(mask[s][:], labT[s][:], float(n + 2), None, ALU.is_equal)\
                                .then_inc(more_mask[b], 1)
                            dve.wait_ge(more_sum[b], 3 * n + 1)
                            nc.vector.tensor_scalar_add(rc[s][:], bank, CNT_EPS).then_inc(more_full[b], 1)
                            dve.wait_ge(more_full[b], 4 * n + 1)
                            nc.vector.reciprocal(rc[s][:], rc[s][:]).then_inc(more_full[b], 1)
                            dve.wait_ge(more_full[b], 4 * n + 2)
                            for ht in range(DT):
                                dve.wait_ge(more_sum[b], 3 * n + 2 + ht)
                                nc.vector.tensor_mul(more[s][:, ht, :], bank, rc[s][:]).then_inc(more_full[b], 1)
                            dve.wait_ge(more_used[b], n + 1)

                    for k in ORDER["DVE"]:
                        kind = k[0]
                        if kind == "x":
                            s = slot(k[1])
                            dve.wait_ge(x_hi.sem, x_hi.at(k))
                            nc.vector.tensor_sub(xl[s][:], xraw[s][:], f32(xh[s][:])).then_inc(x_lo.sem, 1)
                        elif kind == "label":
                            b = k[1]
                            s = slot(b)
                            if b >= SLOTS:
                                dve.wait_ge(g_ready.sem, g_ready.at(("ov", b - SLOTS, LAST, 1)))
                            dve.wait_ge(lab_in[s], i * (16 * TURNS) + 16 * uses(b))
                            nc.vector.tensor_scalar(mask[s][:], labT[s][:], 1.0, None, ALU.is_equal).then_inc(labelled.sem, 1)
                            nc.vector.tensor_scalar(above[s][:], labT[s][:], 2.0, None, ALU.is_ge).then_inc(compared.sem, 1)
                        elif kind == "rc":
                            c = rc[slot(k[1])][:, k[2] * P:(k[2] + 1) * P]
                            dve.wait_ge(cnt_read.sem, cnt_read.at(("cnt", k[1])))
                            nc.vector.reciprocal(c, c).then_inc(rcs.sem, 1)
                        elif kind == "high":
                            s = slot(k[1])
                            dve.wait_ge(g_ready.sem, g_ready.at(k))
                            link(nc.vector.tensor_reduce(n_above[:, s:s + 1], gbank(k)[0:1, :], AX_X, ALU.max))
                            nc.vector.tensor_copy(take_more[:, s:s + 1], n_above[:, s:s + 1]).then_inc(told.sem, 1)
                        elif kind == "agg":
                            _, b, ht = k
                            dve.wait_ge(rcs.sem, rcs.at(("rc", b, NT - 1)))
                            if b >= SLOTS:
                                dve.wait_ge(stored[slot(b)], 16 * uses(b - SLOTS))
                            dve.wait_ge(g_ready.sem, g_ready.at(k))
                            nc.vector.tensor_mul(flt[slot(b)][:, ht, :], gbank(k), rc[slot(b)][:]).then_inc(full.sem, 1)
                        elif kind == "more":
                            s, b = slot(k[1]), k[1]
                            for ht in range(DT):
                                k2 = ("agg", b, ht)
                                dve.wait_ge(hi.sem, hi.at(k2))
                                nc.vector.tensor_sub(parts(k2)[1], flt[s][:, ht, :], f32(parts(k2)[0])).then_inc(lo.sem, 1)
                        elif kind == "labels":
                            b = k[1]
                            s = slot(b)
                            dve.wait_ge(told.sem, told.at(("high", b)))
                            with dve.If(dve.value_load(take_more[0:1, s:s + 1]) > 0):
                                more_labels(b)
                        elif kind == "bias":
                            b = k[1]
                            s = slot(b)
                            dve.wait_ge(adj_in[s], i * (16 * TURNS) + 16 * uses(b))
                            nc.vector.tensor_scalar(mbias[s][:], mbias[s][:], 0.0, MASKED, ALU.is_equal, ALU.mult)\
                                .then_inc(biased.sem, 1)
                        elif kind == "in":
                            _, b, et = k
                            c = tB[slot(b)][:, et, :]
                            dve.wait_ge(act_gru.sem, act_gru.at(("r", b, et)))
                            nc.vector.scalar_tensor_tensor(out=c, in0=tA[slot(b)][:, et, :], scalar=1.0, in1=c,
                                                           op0=ALU.add, op1=ALU.mult).then_inc(dve_gru.sem, 1)
                            dve.wait_ge(dve_gru.sem, dve_gru.at(k + ("v",)))
                            dve.wait_ge(g_ready.sem, g_ready.at(k))
                            nc.vector.tensor_add(c, c, gbank(k)).then_inc(dve_gru.sem, 1)
                        elif kind == "z":
                            _, b, et = k
                            s = slot(b)
                            a = tA[s][:, et, :]
                            dve.wait_ge(pool_d.sem, pool_d.at(k))
                            dve.wait_ge(act_gru.sem, act_gru.at(k))
                            nc.vector.scalar_tensor_tensor(out=a, in0=tC[s][:, et, :], scalar=1.0, in1=a,
                                                           op0=ALU.add, op1=ALU.mult).then_inc(dve_gru.sem, 1)
                            dve.wait_ge(dve_gru.sem, dve_gru.at(k + ("e",)))
                            nc.vector.scalar_tensor_tensor(out=a, in0=a, scalar=0.5, in1=tB[s][:, et, :],
                                                           op0=ALU.mult, op1=ALU.add).then_inc(dve_gru.sem, 1)
                        elif kind == "norm":
                            _, layer, b = k
                            s = slot(b)
                            if layer == "0":
                                dve.wait_ge(lo.sem, lo.at(("wd", b, DT - 1)))
                                for it in range(NT):
                                    if it % 2 == 0:
                                        dve.wait_ge(g_ready.sem, g_ready.at(("lt", b, it // 2)))
                                    moments(s, it, combined(b, it))
                                layer_norm(s, lambda it: combined(b, it))
                            else:
                                layer_norm(s, lambda it: xi[s][:, it, :])
                        elif kind in ("wd", "xt"):
                            s = slot(k[1] if kind == "wd" else k[2])
                            high, low = parts(k)
                            dve.wait_ge(whole.sem, whole.at(k))
                            nc.vector.tensor_sub(low, (flt if kind == "wd" else xf)[s][:, k[-1], :], f32(high)).then_inc(lo.sem, 1)
                        elif kind in ("q", "k", "v", "hx"):
                            high, low = parts(k)
                            col = column(k)
                            dve.wait_ge(hi.sem, hi.at(k))
                            src = view(k, gbank(k))
                            if col is None:
                                a = nc.vector.tensor_sub(low, src, f32(high))
                            else:
                                a = nc.vector.scalar_tensor_tensor(out=low, in0=src, scalar=col, in1=f32(high),
                                                                   op0=ALU.add, op1=ALU.subtract)
                            a.then_inc(lo.sem, 1)
                        elif kind == "S":
                            _, u, it = k
                            b, n = u[1], tiles[k[1:]]
                            dve.wait_ge(s_ready.sem, s_ready.at(k))
                            if u[0] == "1a" and it == 0:
                                dve.wait_ge(biased.sem, biased.at(("bias", b)))
                            if n >= RING:
                                dve.wait_ge(t_ready.sem, t_ready.at(("T",) + steps("PE", "S")[n - RING][1:]))
                            nc.vector.tensor_tensor_reduce(out=ring(k), in0=psS[:, n % 2, :], in1=mbias[slot(b)][:, it, :],
                                                           scale=1.0, scalar=HIGHEST, op0=ALU.add, op1=ALU.min,
                                                           accum_out=nmax[:, shift_col(k)]).then_inc(s_taken.sem, 1)
                        elif kind == "T":
                            _, u, it = k
                            o = slice(it * P, (it + 1) * P)
                            dve.wait_ge(pt_hi.sem, pt_hi.at(k))
                            nc.vector.tensor_sub(ptl[slot(u[1])][:, :, o], turned(k).rearrange("p (j i) -> p j i", j=NT),
                                                 f32(pth[slot(u[1])][:, :, o])).then_inc(pt_lo.sem, 1)
                        elif kind == "pv":
                            _, layer, b, ip = k
                            s = slot(b)
                            if ip == 0:
                                if layer == "1a":
                                    link(nc.vector.tensor_scalar(flag[:, s, :], nmax[:, s * NT:(s + 1) * NT], MASKED / 2, None,
                                                                 ALU.is_le))
                                link(nc.vector.reciprocal(rinv[:, s, 0, :], rsum[:, s, 0, :]))
                                if layer in ("1a", "1b"):
                                    link(nc.vector.tensor_mul(rinv[:, s, 0, :], rinv[:, s, 0, :], flag[:, s, :]))
                                dve.wait_ge(affine.sem, affine.at(("affine", BEFORE[layer], b, "shifted")))
                            dve.wait_ge(g_ready.sem, g_ready.at(k))
                            summed(k, b, ip, rinv[:, s, 0, :])
                        elif kind == "ht":
                            _, b, p = k
                            s = slot(b)
                            r = rinv[:, s, 2 * p:2 * p + 2, :]
                            link(nc.vector.reciprocal(r, rsum[:, s, 2 * p:2 * p + 2, :]))
                            if p == 2:
                                dve.wait_ge(g_ready.sem, g_ready.at(("hx", b, 0)))
                            elif p == 0 and b:
                                dve.wait_ge(g_ready.sem, g_ready.at(("hx", b - 1, DT - 1)))
                            dve.wait_ge(h_lo.sem, h_lo.at(k))
                            o = hn_i[:].rearrange("p t (h d) -> p t h d", d=HD)[:, :, 2 * (p % 2):2 * (p % 2) + 2, :]
                            link(nc.vector.tensor_add(o, pair(gbank(k), 0), hlo[:]))
                            r = r.rearrange("p h t -> p t h").unsqueeze(3).to_broadcast([P, NT, 2, HD])
                            nc.vector.tensor_mul(o, o, r).then_inc(h_done.sem, 1)
                        elif kind == "y":
                            _, b, ip = k
                            s = slot(b)
                            if ip == 0:
                                link(nc.vector.reciprocal(nan_[:, s, :], flag[:, s, :]))
                                link(nc.vector.tensor_mul(nan_[:, s, :], nan_[:, s, :], flag[:, s, :]))
                                dve.wait_ge(affine.sem, affine.at(("affine", "2", b, "shifted")))
                            dve.wait_ge(g_ready.sem, g_ready.at(k))
                            summed(k, b, ip, nan_[:, s, :])

                @block.tensor
                def _(pe):
                    def claim(k):
                        if NUMBER[k] < GBANKS:
                            return
                        p = GROUPS[NUMBER[k] - GBANKS]
                        kind = p[0]
                        if kind == "cnt":
                            pe.wait_ge(cnt_read.sem, cnt_read.at(p))
                        elif kind == "high":
                            pe.wait_ge(told.sem, told.at(p))
                        elif kind == "agg":
                            pe.wait_ge(full.sem, full.at(p))
                        elif kind in ("wd", "xt"):
                            pe.wait_ge(whole.sem, whole.at(p))
                        elif kind in ("hn", "r", "z"):
                            pe.wait_ge(act_gru.sem, act_gru.at(p))
                        elif kind == "in":
                            pe.wait_ge(dve_gru.sem, dve_gru.at(p + ("w",)))
                        elif kind == "lt":
                            half = normed2 if p[2] else normed
                            pe.wait_ge(half.sem, half.at(("norm", "0", p[1], 2 * p[2] + 1)))
                        elif kind in ("pv", "y"):
                            pe.wait_ge(y_done.sem, y_done.at(p))
                        elif kind == "ov":
                            pe.wait_ge(ov_out.sem, ov_out.at(p))
                        elif kind == "ht":
                            pe.wait_ge(h_done.sem, h_done.at(p))
                        elif kind != "more":
                            pe.wait_ge(lo.sem, lo.at(p))

                    def run(ps, terms):
                        for n, (a, b) in enumerate(terms):
                            mm = nc.tensor.matmul(ps, a, b, start=(n == 0), stop=(n == len(terms) - 1))
                        return mm

                    def turn(ps, srcs):
                        for n, src in enumerate(srcs):
                            mm = nc.tensor.transpose(ps[:, n * P:(n + 1) * P], src, ident[:])
                        return mm

                    def features(name, s, c, high, low):
                        t = []
                        for kt in range(DT):
                            w = W(name, kt, c * P, (c + 1) * P)
                            t += terms3(w[0], w[1], high[s][:, kt, :], low[s][:, kt, :])
                        return t

                    def neighbours(s, ht):
                        c = slice(ht * P, (ht + 1) * P)
                        return [(w[s][:, nt, c], mask[s][:, nt, :]) for nt in range(NT) for w in (xl, xh)]

                    def more_labels(b):
                        s, bank = slot(b), gbank(("more", b))
                        for n in range(LABELS - 1):
                            pe.wait_ge(more_mask[b], n + 1)
                            run(bank, [(ones[:], mask[s][:, nt, :]) for nt in range(NT)]).then_inc(more_sum[b], 1)
                            for ht in range(DT):
                                pe.wait_ge(more_full[b], 4 * n + 1 if ht == 0 else 4 * n + 3)
                                run(bank, neighbours(s, ht)).then_inc(more_sum[b], 1)
                            pe.wait_ge(more_full[b], 4 * n + 4)
                            for et in range(DT):
                                for kt in range(DT):
                                    c = (n * DT + kt) * D + et * P
                                    mm = nc.tensor.matmul(gbank(("wd", b, et)), wg[:, c:c + P], more[s][:, kt, :],
                                                          start=False, stop=False, skip_group_check=True)
                            mm.then_inc(more_used[b], 1)

                    for k in ORDER["PE"]:
                        kind = k[0]
                        if kind not in ("S", "T"):
                            claim(k)
                            ps = gbank(k)
                        if kind in ("cnt", "agg", "more", "wd", "hn", "r", "in", "z", "lt", "ov", "ht", "hx", "y"):
                            b = k[1]
                            s = slot(b)
                        if kind == "cnt":
                            pe.wait_ge(labelled.sem, labelled.at(("label", b)))
                            mm = run(ps, [(ones[:], mask[s][:, nt, :]) for nt in range(NT)])
                        elif kind == "high":
                            s = slot(k[1])
                            pe.wait_ge(compared.sem, compared.at(("label", k[1])))
                            mm = run(ps, [(ones_b[:], above[s][:, nt, :]) for nt in range(NT)])
                        elif kind == "agg":
                            pe.wait_ge(x_lo.sem, x_lo.at(("x", b)))
                            mm = run(ps, neighbours(s, k[2]))
                        elif kind == "more":
                            mm = None
                        elif kind == "wd":
                            et = k[2]
                            if et == 0:
                                pe.wait_ge(lo.sem, lo.at(("agg", b, DT - 1)))
                            t = features("wd1", s, et, qh, ql)
                            for n, (a, c) in enumerate(t[:-1]):
                                nc.tensor.matmul(ps, a, c, start=(n == 0), stop=False)
                            mm = None
                            if et == DT - 1:
                                pe.wait_ge(told.sem, told.at(("high", b)))
                                with pe.If(pe.value_load(take_more[0:1, s:s + 1]) > 0):
                                    more_labels(b)
                                for e in range(DT):
                                    a, c = features("wd1", s, e, qh, ql)[-1]
                                    nc.tensor.matmul(gbank(("wd", b, e)), a, c, start=False, stop=True).then_inc(g_ready.sem, 1)
                        elif kind in ("hn", "r", "in", "z"):
                            et = k[2]
                            if kind == "hn" and et == 0:
                                pe.wait_ge(xT_lo.sem, xT_lo.at(("xT", b)))
                            t = []
                            if kind != "in":
                                t += features({"hn": "nh", "r": "rh", "z": "zh"}[kind], s, et, xTh, xTl)
                            if kind != "hn":
                                pe.wait_ge(lo.sem, lo.at(("wd", b, DT - 1)))
                                t += features({"in": "ni", "r": "ri", "z": "zi"}[kind], s, et, outh, outl)
                            mm = run(ps, t)
                        elif kind == "lt":
                            pe.wait_ge(dve_gru.sem, dve_gru.at(("z", b, DT - 1, "o")))
                            mm = turn(ps, [tA[s][:, dt, (2 * k[2] + j) * P:(2 * k[2] + j + 1) * P]
                                           for j in range(2) for dt in range(DT)])
                        elif kind == "xt":
                            _, layer, b, dt = k
                            for it in range(NT):
                                half = normed if it < NT // 2 else normed2
                                pe.wait_ge(half.sem, half.at(("norm", layer, b, it)))
                                mm = nc.tensor.transpose(ps[:, it * P:(it + 1) * P], xi[slot(b)][:, it, dt * P:(dt + 1) * P], ident[:])
                        elif kind in ("q", "k"):
                            _, layer, b, c = k
                            pe.wait_ge(lo.sem, lo.at(("xt", BEFORE[layer], b, DT - 1)))
                            mm = run(ps, features("a2" if layer == "2" else kind + layer, slot(b), c if layer in "23" else 0,
                                                  xTh, xTl))
                        elif kind == "v":
                            _, layer, b, jp = k
                            s = slot(b)
                            pe.wait_ge(lo.sem, lo.at(("xt", BEFORE[layer], b, DT - 1)))
                            for j in range(2):
                                jt = slice((2 * jp + j) * P, (2 * jp + j + 1) * P)
                                t = []
                                for kt in range(DT):
                                    w = W("v3" if layer == "3" else "c" + layer, kt)
                                    t += terms3(xTh[s][:, kt, jt], xTl[s][:, kt, jt], w[0], w[1])
                                mm = run(ps[:, j * D:(j + 1) * D], t)
                        elif kind == "S":
                            _, u, it = k
                            layer, b, h = u
                            s, n = slot(b), tiles[k[1:]]
                            i_ = slice(it * P, (it + 1) * P)
                            if n >= 2:
                                pe.wait_ge(s_taken.sem, s_taken.at(steps("PE", "S")[n - 2]))
                            if layer == "3":
                                r = stack_of(b, h)
                                if it == 0:
                                    pe.wait_ge(stack_in[r], stacked(b, h))
                                t = [(stq[r][0:3 * HD, i_], stk[r][0:3 * HD, :])]
                            elif layer == "2":
                                if it == 0:
                                    pe.wait_ge(lo.sem, lo.at(("q", "2", b, DT - 1)))
                                t = []
                                for c in range(DT):
                                    t += terms3(qh[s][:, c, i_], ql[s][:, c, i_], xTh[s][:, c, :], xTl[s][:, c, :])
                            else:
                                if it == 0:
                                    pe.wait_ge(lo.sem, lo.at(("k", layer, b, 0)))
                                t = terms3(qh[s][:, 0, i_], ql[s][:, 0, i_], qh[s][:, 1, :], ql[s][:, 1, :])
                            run(psS[:, n % 2, :], t).then_inc(s_ready.sem, 1)
                        elif kind == "T":
                            n = t_ready.at(k)
                            pe.wait_ge(p_ready.sem, p_ready.at(("S",) + k[1:]))
                            if n > 2:
                                pe.wait_ge(pt_lo.sem, pt_lo.at(steps("PE", "T")[n - 3]))
                            turn(turned(k), [ring(k)[:, jt * P:(jt + 1) * P] for jt in range(NT)]).then_inc(t_ready.sem, 1)
                        elif kind == "pv":
                            _, layer, b, ip = k
                            s = slot(b)
                            if ip == 0:
                                pe.wait_ge(lo.sem, lo.at(("v", layer, b, 1)))
                                pe.wait_ge(pt_lo.sem, pt_lo.at(("T", (layer, b, 0), NT - 1)))
                            for j in range(2):
                                i_ = slice((2 * ip + j) * P, (2 * ip + j + 1) * P)
                                t = []
                                for jt in range(NT):
                                    t += terms3(pth[s][:, jt, i_], ptl[s][:, jt, i_], vh[s][:, jt, :], vl[s][:, jt, :])
                                mm = run(ps[:, j * D:(j + 1) * D], t)
                        elif kind == "ov":
                            _, b, h, half = k
                            i_ = slice(half * D, (half + 1) * D)
                            pe.wait_ge(lo.sem, lo.at(("v", "3", b, 1)))
                            pe.wait_ge(pt_lo.sem, pt_lo.at(("T", ("3", b, h), 2 * half + 1)))
                            t = []
                            for jt in range(NT):
                                v = v3t[s][:, jt, h // 2 * 2:h // 2 * 2 + 2, :, :].rearrange("p h w d -> p (h w d)")
                                t += [(v, ptl[s][:, jt, i_]), (v, pth[s][:, jt, i_])]
                            mm = run(ps[:, 0:D], t)
                        elif kind == "ht":
                            pe.wait_ge(ov_out.sem, ov_out.at(("ov", b, 2 * k[2] + 1, 1)))
                            mm = turn(ps, [ovs[:, it * P:(it + 1) * P] for it in range(NT)])
                        elif kind == "hx":
                            pe.wait_ge(h_done.sem, h_done.at(("ht", b, 2 * k[2] + 1)))
                            mm = turn(ps, [hn_i[:, it, :] for it in range(NT)])
                        elif kind == "y":
                            pe.wait_ge(lo.sem, lo.at(("hx", b, DT - 1)))
                            for j in range(2):
                                i_ = slice((2 * k[2] + j) * P, (2 * k[2] + j + 1) * P)
                                t = []
                                for kt in range(DT):
                                    w = W("o3", kt)
                                    t += terms3(qh[s][:, kt, i_], ql[s][:, kt, i_], w[0], w[1])
                                mm = run(ps[:, j * D:(j + 1) * D], t)
                        if kind not in ("S", "T") and mm is not None:
                            mm.then_inc(g_ready.sem, 1)

            nc.gpsimd.sem_clear(range(sem_first, sem_last + 1))
            nc.all_engine_barrier()


def kernel(**inputs):
    import numpy as np
    import concourse.bacc as bacc
    from concourse.bass_utils import run_bass_kernel_spmd as run

    a = {k: np.asarray(v) for k, v in inputs.items()}

    def ktiles(m):
        return m.reshape(-1, P, m.shape[1]).transpose(1, 0, 2).reshape(P, -1)

    wd = a["L0_gnn_Wd"]
    g0, g1, g2, g3 = "L0_gnn_", "L1_gnn_", "L2_gnn_", "L3_gnn_"
    mats = [wd[:, 0:D].T] + [a[g0 + "W" + n].T for n in ("ri", "rh", "zi", "zh", "ni", "nh")]
    for l in range(2):
        mats += [a[g1 + "Wq"][l].T, a[g1 + "Wk"][l].T, a[g1 + "Wc"][l].T]
    mats += [a[g3 + "W" + n] for n in "qkvo"]
    wraw = np.concatenate([ktiles(m) for m in mats], axis=1)
    wfold = np.concatenate([ktiles(m) for m in (a[g2 + "Wq"].T, a[g2 + "Wk"].T, a[g2 + "Wv"].T, a[g2 + "Wo"])], axis=1)
    wgen = np.concatenate([ktiles(wd[:, d * D:(d + 1) * D].T) for d in range(1, LABELS)], axis=1)
    cols = [a[g0 + "b" + n] for n in ("d", "ri", "rh", "zi", "zh", "ni", "nh")]
    for l in range(2):
        cols += [a[g1 + "bq"][l], a[g1 + "bk"][l]]
    cols += [a[g3 + "b" + n] for n in "qkv"] + [a[g0 + "gamma"], a[g0 + "beta"]]
    for l in range(2):
        cols += [a[g1 + "ln_g"][l], a[g1 + "ln_b"][l]]
    cols += [a[g2 + "gamma"], a[g2 + "beta"]]
    bcols = np.concatenate([c.reshape(-1, P).T for c in cols], axis=1)
    rows = [a[g0 + "gamma"], a[g0 + "beta"]]
    for l in range(2):
        rows += [a[g1 + "ln_g"][l], a[g1 + "ln_b"][l]]
    rows += [a[g2 + "gamma"], a[g2 + "beta"], a[g3 + "gamma"], a[g3 + "beta"]]
    rep = np.broadcast_to(np.concatenate(rows)[None, :], (P, len(REP) * D))
    rep_bo = np.broadcast_to(np.concatenate([a[g2 + "bo"], a[g3 + "bo"]])[None, :], (P, 2 * D))

    arrays = {
        "x": a["x"], "xT": a["x"].transpose(0, 2, 1), "adj": a["adj"], "adjT": a["adj"].transpose(0, 2, 1),
        "wraw": wraw, "wfold": wfold, "wgen": wgen, "bcols": bcols, "rep": rep, "rep_bo": rep_bo,
    }
    arrays = {f"in_{k}": np.ascontiguousarray(v) for k, v in arrays.items()}
    nc = bacc.Bacc("TRN2", target_bir_lowering=False, num_devices=1)
    args = [nc.dram_tensor(k, v.shape, mybir.dt.from_np(v.dtype), kind="ExternalInput").ap() for k, v in arrays.items()]
    out = nc.dram_tensor("out", (B, N, D), F32, kind="ExternalOutput").ap()
    build(nc, *args, out)
    r = run(nc, [arrays], core_ids=[0])
    return r.results[0]["out"]
```
